# Optimizing a Trainium2 kernel written in Bass

```python
import numpy as np
import jax
import jax.numpy as jnp

def _softmax(x, axis=-1):
    return jax.nn.softmax(x, axis=axis)

def _gelu(x):
    return jax.nn.gelu(x, approximate=True)

def _silu(x):
    return jax.nn.silu(x)

def _sigmoid(x):
    return jax.nn.sigmoid(x)

def _layernorm(x, axis=-1, eps=1e-05):
    m = jnp.mean(x, axis=axis, keepdims=True)
    v = jnp.var(x, axis=axis, keepdims=True)
    return (x - m) / jnp.sqrt(v + eps)

def _scatter_add(tgt, idx, src, axis=0):
    return tgt.at[idx].add(src)

def _segment_sum(src, seg, n):
    return jax.ops.segment_sum(src, seg, n)
kernel_name = 'mk_decoder_preln_d1_seqx_r4_80c261'

def setup_inputs(seed: int=0):
    np.random.seed(seed)
    _w = jnp.asarray

    def _rec_inputs():
        import jax
        import jax.numpy as jnp
        _rk = jax.random.key(seed)
        x = 7.22e-05 + 1 * jax.random.normal(jax.random.fold_in(_rk, 1), (16, 256, 512), jnp.float32)
        _lenS = 256 - jax.random.randint(jax.random.fold_in(_rk, 7), (16,), 0, max(1, 256 // 4) + 1, jnp.int32)
        _lenS2 = 256 - jax.random.randint(jax.random.fold_in(_rk, 8), (16,), 0, max(1, 256 // 4) + 1, jnp.int32)
        _ctx_2048P = jax.random.normal(jax.random.fold_in(_rk, 11), (16, 16, 512), jnp.float32)
        _ctx_2048c = jax.random.dirichlet(jax.random.fold_in(_rk, 511), 0.3 * jnp.ones((16,), jnp.float32), (16, 256))
        _ctx_2048t = jnp.einsum('bsk,bkd->bsd', _ctx_2048c, _ctx_2048P)
        _ctx_2048t = _ctx_2048t * jax.lax.rsqrt(jnp.mean(jnp.square(_ctx_2048t)) + 1e-12) * 0.953939
        ctx_2048 = 4.13588e-05 + 0.999923 * (_ctx_2048t + 0.3 * jax.random.normal(jax.random.fold_in(_rk, 611), (16, 256, 512), jnp.float32))
        return (x, ctx_2048)
    x, ctx_2048 = _rec_inputs()

    def _L0_attn_setup():
        import jax, jax.numpy as jnp
        import numpy as np
        H = 16
        EPS_DEN = 1e-06

        def _decay_scan(x, decay, init):
            xT = jnp.moveaxis(x, 2, 0)

            def step(s, xt):
                s = decay * s + xt
                return (s, s)
            _, ys = jax.lax.scan(step, init, xT)
            return jnp.moveaxis(ys, 0, 2)

        def _phi(z):
            return jax.nn.elu(z) + 1.0

        def _reference_tuple_inner(x, w_qkv, w_out, decay_param):
            B, T, Hid = x.shape
            D = Hid // H
            qkv = x @ w_qkv
            q, k, v = jnp.split(qkv, 3, axis=-1)

            def to_bhtd(t):
                return t.reshape(B, T, H, D).transpose(0, 2, 1, 3)
            q = _phi(to_bhtd(q))
            k = _phi(to_bhtd(k))
            v = to_bhtd(v)
            decay = jax.nn.sigmoid(decay_param).reshape(1, H, 1)
            init = jnp.zeros((B, H, D), dtype=x.dtype)
            running_kv = _decay_scan(k * v, decay, init)
            running_ksum = _decay_scan(k, decay, init)
            den = jnp.clip(jnp.sum(q * running_ksum, axis=-1, keepdims=True), EPS_DEN, None)
            out = q * running_kv / den
            out = out.transpose(0, 2, 1, 3).reshape(B, T, Hid) @ w_out
            new_kv = running_kv[:, :, -1, :]
            new_ksum = running_ksum[:, :, -1, :]
            return (out, new_kv, new_ksum)
        key = jax.random.key(seed)
        k1, k2, k3 = jax.random.split(key, 3)
        x = jax.random.normal(k1, (2, 1024, 512), dtype=jnp.float32)
        w_qkv = jax.random.normal(k2, (512, 1536), dtype=jnp.float32) * 0.02
        w_out = jax.random.normal(k3, (512, 512), dtype=jnp.float32) * 0.02
        decay_param = jnp.full((H,), 0.95, dtype=jnp.float32)
        return {'x': x, 'w_qkv': w_qkv, 'w_out': w_out, 'decay_param': decay_param}
    _L0_attn_all = _L0_attn_setup()
    _L0_attn_in = {k: v for k, v in _L0_attn_all.items() if k in ('w_qkv', 'w_out', 'decay_param')}
    del _L0_attn_all

    def _L0_xattn_setup():
        import jax, jax.numpy as jnp
        import numpy as np
        B, D, N, H = (4, 256, 512, 16)
        HD = D // H

        def rotate_half(x):
            x1 = x[..., 0::2]
            x2 = x[..., 1::2]
            return jnp.stack((-x2, x1), axis=-1).reshape(x.shape)

        def apply_cached_rotary_emb(freqs, t):
            return t * freqs[0] + rotate_half(t) * freqs[1]
        key = jax.random.key(seed)
        ks = jax.random.split(key, 13)
        s = 1.0 / np.sqrt(D)
        inp = {'query': jax.random.normal(ks[0], (B, D, N), jnp.float32), 'key': jax.random.normal(ks[1], (B, D, N), jnp.float32), 'value': jax.random.normal(ks[2], (B, D, N), jnp.float32), 'encoding': jax.random.normal(ks[3], (2, 1, 1, N, HD), jnp.float32), 'Wq': jax.random.normal(ks[4], (D, D), jnp.float32) * s, 'bq': jax.random.normal(ks[5], (D,), jnp.float32) * s, 'Wk': jax.random.normal(ks[6], (D, D), jnp.float32) * s, 'bk': jax.random.normal(ks[7], (D,), jnp.float32) * s, 'Wv': jax.random.normal(ks[8], (D, D), jnp.float32) * s, 'bv': jax.random.normal(ks[9], (D,), jnp.float32) * s, 'Wm': jax.random.normal(ks[10], (D, D), jnp.float32) * s, 'bm': jax.random.normal(ks[11], (D,), jnp.float32) * s}
        return inp
    _L0_xattn_all = _L0_xattn_setup()
    _L0_xattn_in = {k: v for k, v in _L0_xattn_all.items() if k in ('encoding', 'Wq', 'bq', 'Wk', 'bk', 'Wv', 'bv', 'Wm', 'bm')}
    del _L0_xattn_all

    def _L0_ffn_setup():
        import jax, jax.numpy as jnp
        import numpy as np
        H = 512
        I = 352
        E = 8
        K = 2
        B, S = (4, 512)

        def _moe(x, router_w, w1, w2):
            b, s, h = x.shape
            xf = x.reshape(-1, h)
            T = xf.shape[0]
            logits = xf @ router_w.T
            topk_vals, topk_idx = jax.lax.top_k(logits, K)
            topk_w = jax.nn.softmax(topk_vals, axis=-1)
            exp_id = topk_idx.reshape(-1)
            exp_w = topk_w.reshape(-1)
            order = jnp.argsort(exp_id)
            x_sorted = xf[order // K]
            counts = jnp.bincount(exp_id, length=E).astype(jnp.int32)
            y1 = jax.lax.ragged_dot(x_sorted, jnp.swapaxes(w1, 1, 2), counts)
            gate, up = jnp.split(y1, 2, axis=-1)
            y_act = jax.nn.silu(gate) * up
            y2 = jax.lax.ragged_dot(y_act, jnp.swapaxes(w2, 1, 2), counts)
            inv = jnp.argsort(order)
            y_pairs = y2[inv] * exp_w[:, None]
            y = y_pairs.reshape(T, K, h).sum(axis=1)
            return y.reshape(b, s, h)
        key = jax.random.key(seed)
        k1, k2, k3, k4 = jax.random.split(key, 4)
        x = jax.random.normal(k1, (B, S, H), dtype=jnp.float32)
        router_w = jax.random.normal(k2, (E, H), dtype=jnp.float32) * 0.02
        w1 = jax.random.normal(k3, (E, 2 * I, H), dtype=jnp.float32) * 0.02
        w2 = jax.random.normal(k4, (E, H, I), dtype=jnp.float32) * 0.02
        return {'x': x, 'router_w': router_w, 'w1': w1, 'w2': w2}
    _L0_ffn_all = _L0_ffn_setup()
    _L0_ffn_in = {k: v for k, v in _L0_ffn_all.items() if k in ('router_w', 'w1', 'w2')}
    del _L0_ffn_all
    return {'x': x, 'ctx_2048': ctx_2048, 'L0_attn_w_qkv': _L0_attn_in['w_qkv'], 'L0_attn_w_out': _L0_attn_in['w_out'], 'L0_attn_decay_param': _L0_attn_in['decay_param'], 'L0_xattn_encoding': _L0_xattn_in['encoding'], 'L0_xattn_Wq': _L0_xattn_in['Wq'], 'L0_xattn_bq': _L0_xattn_in['bq'], 'L0_xattn_Wk': _L0_xattn_in['Wk'], 'L0_xattn_bk': _L0_xattn_in['bk'], 'L0_xattn_Wv': _L0_xattn_in['Wv'], 'L0_xattn_bv': _L0_xattn_in['bv'], 'L0_xattn_Wm': _L0_xattn_in['Wm'], 'L0_xattn_bm': _L0_xattn_in['bm'], 'L0_ffn_router_w': _L0_ffn_in['router_w'], 'L0_ffn_w1': _L0_ffn_in['w1'], 'L0_ffn_w2': _L0_ffn_in['w2']}

def reference(x, ctx_2048, L0_attn_w_qkv, L0_attn_w_out, L0_attn_decay_param, L0_xattn_encoding, L0_xattn_Wq, L0_xattn_bq, L0_xattn_Wk, L0_xattn_bk, L0_xattn_Wv, L0_xattn_bv, L0_xattn_Wm, L0_xattn_bm, L0_ffn_router_w, L0_ffn_w1, L0_ffn_w2):
    import jax
    import jax.numpy as jnp

    def _L0_attn_ref(x, w_qkv, w_out, decay_param):
        import jax, jax.numpy as jnp
        import numpy as np
        H = 16
        EPS_DEN = 1e-06

        def _decay_scan(x, decay, init):
            xT = jnp.moveaxis(x, 2, 0)

            def step(s, xt):
                s = decay * s + xt
                return (s, s)
            _, ys = jax.lax.scan(step, init, xT)
            return jnp.moveaxis(ys, 0, 2)

        def _phi(z):
            return jax.nn.elu(z) + 1.0

        def _reference_tuple_inner(x, w_qkv, w_out, decay_param):
            B, T, Hid = x.shape
            D = Hid // H
            qkv = x @ w_qkv
            q, k, v = jnp.split(qkv, 3, axis=-1)

            def to_bhtd(t):
                return t.reshape(B, T, H, D).transpose(0, 2, 1, 3)
            q = _phi(to_bhtd(q))
            k = _phi(to_bhtd(k))
            v = to_bhtd(v)
            decay = jax.nn.sigmoid(decay_param).reshape(1, H, 1)
            init = jnp.zeros((B, H, D), dtype=x.dtype)
            running_kv = _decay_scan(k * v, decay, init)
            running_ksum = _decay_scan(k, decay, init)
            den = jnp.clip(jnp.sum(q * running_ksum, axis=-1, keepdims=True), EPS_DEN, None)
            out = q * running_kv / den
            out = out.transpose(0, 2, 1, 3).reshape(B, T, Hid) @ w_out
            new_kv = running_kv[:, :, -1, :]
            new_ksum = running_ksum[:, :, -1, :]
            return (out, new_kv, new_ksum)
        return _reference_tuple_inner(x, w_qkv, w_out, decay_param)[0]

    def _L0_xattn_ref(query, key, value, encoding, Wq, bq, Wk, bk, Wv, bv, Wm, bm):
        import jax, jax.numpy as jnp
        import numpy as np
        B, D, N, H = (4, 256, 512, 16)
        HD = D // H

        def rotate_half(x):
            x1 = x[..., 0::2]
            x2 = x[..., 1::2]
            return jnp.stack((-x2, x1), axis=-1).reshape(x.shape)

        def apply_cached_rotary_emb(freqs, t):
            return t * freqs[0] + rotate_half(t) * freqs[1]
        b, d_model, n = query.shape

        def proj(W, bias, x):
            return jnp.einsum('oi,bin->bon', W, x) + bias[None, :, None]
        q = proj(Wq, bq, query).reshape(b, HD, H, n)
        k = proj(Wk, bk, key).reshape(b, HD, H, n)
        v = proj(Wv, bv, value).reshape(b, HD, H, n)
        q = jnp.transpose(apply_cached_rotary_emb(encoding, jnp.transpose(q, (0, 2, 3, 1))), (0, 3, 1, 2))
        k = jnp.transpose(apply_cached_rotary_emb(encoding, jnp.transpose(k, (0, 2, 3, 1))), (0, 3, 1, 2))
        scores = jnp.einsum('bdhn,bdhm->bhnm', q, k) / np.float32(np.sqrt(HD))
        prob = jax.nn.softmax(scores, axis=-1)
        x = jnp.einsum('bhnm,bdhm->bdhn', prob, v)
        out = jnp.einsum('oi,bin->bon', Wm, x.reshape(b, d_model, n)) + bm[None, :, None]
        return out

    def _L0_ffn_ref(x, router_w, w1, w2):
        import jax, jax.numpy as jnp
        import numpy as np
        H = 512
        I = 352
        E = 8
        K = 2
        B, S = (4, 512)

        def _moe(x, router_w, w1, w2):
            b, s, h = x.shape
            xf = x.reshape(-1, h)
            T = xf.shape[0]
            logits = xf @ router_w.T
            topk_vals, topk_idx = jax.lax.top_k(logits, K)
            topk_w = jax.nn.softmax(topk_vals, axis=-1)
            exp_id = topk_idx.reshape(-1)
            exp_w = topk_w.reshape(-1)
            order = jnp.argsort(exp_id)
            x_sorted = xf[order // K]
            counts = jnp.bincount(exp_id, length=E).astype(jnp.int32)
            y1 = jax.lax.ragged_dot(x_sorted, jnp.swapaxes(w1, 1, 2), counts)
            gate, up = jnp.split(y1, 2, axis=-1)
            y_act = jax.nn.silu(gate) * up
            y2 = jax.lax.ragged_dot(y_act, jnp.swapaxes(w2, 1, 2), counts)
            inv = jnp.argsort(order)
            y_pairs = y2[inv] * exp_w[:, None]
            y = y_pairs.reshape(T, K, h).sum(axis=1)
            return y.reshape(b, s, h)
        return _moe(x, router_w, w1, w2)
    x = x + _L0_attn_ref(_layernorm(x, axis=-1), L0_attn_w_qkv, L0_attn_w_out, L0_attn_decay_param)
    x = x + _L0_xattn_ref(_layernorm(x, axis=-1), ctx_2048, ctx_2048, L0_xattn_encoding, L0_xattn_Wq, L0_xattn_bq, L0_xattn_Wk, L0_xattn_bk, L0_xattn_Wv, L0_xattn_bv, L0_xattn_Wm, L0_xattn_bm)
    x = x + _L0_ffn_ref(_layernorm(x, axis=-1), L0_ffn_router_w, L0_ffn_w1, L0_ffn_w2)
    return x

_drawn_inputs = setup_inputs


def setup_inputs(seed=0):
    import zlib

    import numpy as np

    out = dict(_drawn_inputs(seed))
    spreads = {'L0_attn_decay_param': (0.949999988079071, 0.6)}
    factors = {'L0_attn_w_qkv': 8.0, 'L0_attn_w_out': 8.0, 'L0_ffn_router_w': 2.725}
    for name, (base, spread) in spreads.items():
        noise = np.random.default_rng([zlib.crc32(name.encode()), seed]).standard_normal(out[name].shape)
        drawn = base * np.exp(spread * noise) if base else spread * noise
        out[name] = jnp.asarray(drawn.astype(out[name].dtype))
    for name, factor in factors.items():
        out[name] = (out[name] * factor).astype(out[name].dtype)
    return out
```

```python
import concourse.bass as bass
from concourse import mybir
from contextlib import ExitStack

FP32 = mybir.dt.float32
BF16 = mybir.dt.bfloat16
I32 = mybir.dt.int32
U32 = mybir.dt.uint32
ALU = mybir.AluOpType
ACT = mybir.ActivationFunctionType
AX = mybir.AxisListType

P = 128
B, T, HID = 16, 256, 512
TT = T // P
HC = HID // P
H = 16
LN_EPS = 1e-05
DEN_EPS = 1e-06


class Count:

    def __init__(self, engine, sem):
        self.engine, self.sem, self.base, self.n = engine, sem, 0, 0

    def inc(self, instruction):
        instruction.then_inc(self.sem, 1)
        self.n += 1
        return self.base + self.n

    def wait(self, value):
        self.engine.wait_ge(self.sem, value)

    def link(self, instruction):
        self.wait(self.inc(instruction))


def layer_norm_stats(dve, count, x, stats, mean_var):
    last = None
    for t in range(x.shape[1]):
        last = dve.bn_stats(stats[:, t, :], x[:, t, :])
    count.link(last)
    dve.sem_inc(count.sem, 1)
    count.n += 1
    for t in range(x.shape[1]):
        last = dve.bn_aggr(mean_var[:, t, :], stats[:, t, :])
    return last


def build_stage_a(nc, x, w_qkv, w_out, decay_rows, ident_in, head_sum_in, head_spread_in, x1):
    with ExitStack() as ctx:
        def sb(name, shape, dt=FP32):
            return ctx.enter_context(nc.sbuf_tensor("a_" + name, shape, dt))

        def pb(name, shape=(P, 512), dt=FP32):
            return ctx.enter_context(nc.psum_tensor("a_" + name, list(shape), dt))

        def sem(name):
            return ctx.enter_context(nc.semaphore("a_" + name))

        wqkv = sb("wqkv", [P, HC, 3 * HID])
        wout = sb("wout", [P, HC, HID])
        ident = sb("ident", [P, P])
        head_sum = sb("head_sum", [P, HC, H])
        head_spread = sb("head_spread", [H, HC, P])
        decay_p = sb("decay_p", [P, HC])
        decay_1 = sb("decay_1", [P, HC])
        decay_2 = sb("decay_2", [P, HC])
        decay = sb("decay", [P, HC, T])
        half = sb("half", [P, TT])
        x_in = sb("x_in", [P, TT, HID])
        x_res = sb("x_res", [P, TT, HID])
        stats = sb("stats", [P, TT, 6])
        mean_var = sb("mean_var", [P, TT, 2])
        var_eps = sb("var_eps", [P, TT])
        rstd = sb("rstd", [P, TT])
        xn = sb("xn", [P, TT, HID])
        xT = sb("xT", [P, 2, HC, T])
        e_qk = sb("e_qk", [P, 2, 2, T])
        phi = sb("phi", [P, 2, 2, T])
        kv = sb("kv", [P, T])
        run_kv = sb("run_kv", [P, T])
        run_k = sb("run_k", [P, T])
        q_sum = sb("q_sum", [P, 2, HC, T])
        q_kv = sb("q_kv", [P, 2, HC, T])
        den = sb("den", [H, T])
        rden = sb("rden", [H, T])
        x1_sb = sb("x1_sb", [P, TT, HID])

        ps_qk = [pb(f"ps_qk{i}") for i in range(2)]
        ps_v = [pb(f"ps_v{i}") for i in range(2)]
        ps_t = [pb(f"ps_t{i}") for i in range(2)]
        ps_w = [pb(f"ps_w{i}") for i in range(2)]

        consts_in = sem("consts_in")
        x_loaded = sem("x_loaded")
        res_loaded = sem("res_loaded")
        x_free = sem("x_free")
        res_free = sem("res_free")
        stored = sem("stored")
        var_ready = sem("var_ready")
        rstd_ready = sem("rstd_ready")
        xn_ready = sem("xn_ready")
        xt_full = sem("xt_full")
        xt_ready = sem("xt_ready")
        qk_full, v_full = sem("qk_full"), sem("v_full")
        qkv_free = sem("qkv_free")
        exp_ready = sem("exp_ready")
        prod_ready = sem("prod_ready")
        den_full = sem("den_full")
        rden_ready = sem("rden_ready")
        spread_full = sem("spread_full")
        o_ready = sem("o_ready")
        out_full = sem("out_full")
        w_free = sem("w_free")
        x1_ready = sem("x1_ready")
        s_dve = sem("dve")

        def per_iteration(engine, body):
            body(0, 0, False, True)
            with engine.Fori(0, (B - 2) // 2) as i:
                body(i * 2 + 1, 1, True, True)
                body(i * 2 + 2, 0, True, True)
            body(B - 1, 1, True, False)
            body(B, 0, True, None)

        with nc.Block() as block:
            @block.sync
            def _(sp):
                sp.dma_start(x_in[:], x[0].rearrange("(t p) n -> p t n", p=P)).then_inc(x_loaded, 16)
                sp.dma_start(ident[:], ident_in).then_inc(consts_in, 16)
                sp.dma_start(decay_p[:], decay_rows).then_inc(consts_in, 16)
                sp.dma_start(wqkv[:], w_qkv.rearrange("(c p) n -> p c n", p=P)).then_inc(consts_in, 16)
                sp.dma_start(head_sum[:], head_sum_in).then_inc(consts_in, 16)
                sp.dma_start(head_spread[:], head_spread_in).then_inc(consts_in, 16)
                sp.dma_start(wout[:], w_out.rearrange("(c p) n -> p c n", p=P)).then_inc(consts_in, 16)

                def body(b, par, prev, nxt):
                    if nxt:
                        sp.wait_ge(x_free, b + 2)
                        sp.dma_start(x_in[:], x[bass.ds(b + 1, 1)].rearrange("a (t p) n -> p (a t) n", p=P)) \
                          .then_inc(x_loaded, 16)
                    if prev:
                        sp.wait_ge(res_free, b)
                        sp.dma_start(x_res[:], x[bass.ds(b - 1, 1)].rearrange("a (t p) n -> p (a t) n", p=P)) \
                          .then_inc(res_loaded, 16)
                        sp.wait_ge(x1_ready, b)
                        sp.dma_start(x1[bass.ds(b - 1, 1)].rearrange("a (t p) n -> p (a t) n", p=P), x1_sb[:]) \
                          .then_inc(stored, 16)

                per_iteration(sp, body)
                sp.wait_ge(stored, 16 * B)

            @block.gpsimd
            def _(pool):
                pool.memset(half[:], -0.5).then_inc(rstd_ready, 1)
                pool.wait_ge(rstd_ready, 1)

                def rstd_of(b):
                    pool.wait_ge(var_ready, b + 1)
                    pool.tensor_tensor(rstd[:], var_eps[:], half[:], ALU.pow).then_inc(rstd_ready, 1)

                def body(b, par, prev, nxt):
                    if nxt:
                        rstd_of(b + 1)

                rstd_of(0)
                per_iteration(pool, body)

            @block.tensor
            def _(pe):
                def transposes(b):
                    pe.wait_ge(xn_ready, b + 1)
                    for t in range(TT):
                        pe.wait_ge(xt_ready, 2 * b + t + 1)
                        for c in range(HC):
                            last = pe.transpose(ps_t[t][:, c * P:(c + 1) * P], xn[:, t, c * P:(c + 1) * P], ident[:])
                        last.then_inc(xt_full, 1)

                def qkv(b, par, c):
                    pe.wait_ge(qkv_free, 4 * b + c + 1)
                    for role, out in ((0, ps_qk[c % 2][:, 0:T]), (1, ps_qk[c % 2][:, T:2 * T]), (2, ps_v[c % 2][:, 0:T])):
                        for k in range(HC):
                            w = wqkv[:, k, role * HID + c * P:role * HID + (c + 1) * P]
                            last = pe.matmul(out, w, xT[:, par, k, :], start=(k == 0), stop=(k == HC - 1))
                        if role:
                            last.then_inc(qk_full if role == 1 else v_full, 1)

                def denominators(b, par):
                    pe.wait_ge(prod_ready, 4 * b + 4)
                    pe.wait_ge(w_free, 5 * b + 1)
                    for c in range(HC):
                        last = pe.matmul(ps_w[0][0:H, 0:T], head_sum[:, c, :], q_sum[:, par, c, :],
                                         start=(c == 0), stop=(c == HC - 1))
                    last.then_inc(den_full, 1)

                def spread(b):
                    pe.wait_ge(rden_ready, b + 1)
                    for g in range(2):
                        pe.wait_ge(w_free, 5 * b + 1 + g)
                        for k in range(2):
                            last = pe.matmul(ps_w[1 - g][:, k * T:(k + 1) * T], head_spread[:, 2 * g + k, :], rden[:],
                                             start=True, stop=True)
                        last.then_inc(spread_full, 1)

                def project(b, par):
                    pe.wait_ge(o_ready, b + 1)
                    for t in range(TT):
                        pe.wait_ge(w_free, 5 * b + 3 + t)
                        for c in range(HC):
                            last = pe.matmul(ps_w[1 - t][:, :], q_kv[:, par, c, t * P:(t + 1) * P], wout[:, c, :],
                                             start=(c == 0), stop=(c == HC - 1))
                        last.then_inc(out_full, 1)

                def body(b, par, prev, nxt):
                    for c in range(HC):
                        if nxt is not None:
                            if c == 0:
                                pe.wait_ge(xt_ready, 2 * b + 4)
                            qkv(b, par, c)
                        if prev and c == 0:
                            denominators(b - 1, 1 - par)
                        if prev and c == 1:
                            spread(b - 1)
                        if prev and c == 2:
                            project(b - 1, 1 - par)
                    if nxt:
                        transposes(b + 1)

                pe.wait_ge(consts_in, 96)
                transposes(0)
                per_iteration(pe, body)

            @block.scalar
            def _(act):
                act.wait_ge(consts_in, 96)
                act.activation(decay_1[:], decay_p[:], ACT.Exp, scale=-1.0).then_inc(exp_ready, 1)

                def keep_xT(b, par):
                    for t in range(TT):
                        act.wait_ge(xt_full, 2 * b + t + 1)
                        act.copy(xT[:, par, :, t * P:(t + 1) * P],
                                 ps_t[t][:].rearrange("p (c q) -> p c q", c=HC)).then_inc(xt_ready, 1)

                def body(b, par, prev, nxt):
                    if nxt is not None:
                        for c in range(HC):
                            act.wait_ge(qk_full, 4 * b + c + 1)
                            act.activation(e_qk[:, c % 2], ps_qk[c % 2][:].rearrange("p (r t) -> p r t", r=2), ACT.Exp) \
                               .then_inc(exp_ready, 1)
                    if nxt:
                        keep_xT(b + 1, 1 - par)

                keep_xT(0, 0)
                per_iteration(act, body)

            @block.vector
            def _(dve):
                chain = Count(dve, s_dve)
                chain.link(dve.memset(decay[:], 1.0))
                for s, n in ((x_free, 1), (res_free, 1), (xt_ready, 2), (qkv_free, 2), (w_free, 1)):
                    dve.sem_inc(s, n)

                def norm_stats(b):
                    dve.wait_ge(x_loaded, 16 * b + 16)
                    chain.link(layer_norm_stats(dve, chain, x_in, stats, mean_var))
                    dve.tensor_scalar(var_eps[:], mean_var[:, :, 1], LN_EPS, None, ALU.add).then_inc(var_ready, 1)

                def norm_apply(b):
                    dve.wait_ge(rstd_ready, b + 2)
                    for t in range(TT):
                        last = dve.tensor_scalar(xn[:, t, :], x_in[:, t, :], mean_var[:, t, 0:1], rstd[:, t:t + 1],
                                                 ALU.subtract, ALU.mult)
                        if t < TT - 1:
                            continue
                        last.then_inc(xn_ready, 1)
                    dve.wait_ge(xn_ready, b + 1)
                    dve.sem_inc(x_free, 1)

                def scans(b, par, c):
                    dve.wait_ge(exp_ready, 4 * b + c + 2)
                    e, f = e_qk[:, c % 2], phi[:, c % 2]
                    chain.link(dve.tensor_scalar(e, e, 1.0, None, ALU.min))
                    chain.link(dve.scalar_tensor_tensor(f, ps_qk[c % 2][:].rearrange("p (r t) -> p r t", r=2), 0.0, e,
                                                        ALU.max, ALU.add))
                    dve.wait_ge(v_full, 4 * b + c + 1)
                    dve.tensor_tensor(kv[:], f[:, 1, :], ps_v[c % 2][:, 0:T], ALU.mult).then_inc(qkv_free, 1)
                    summed = chain.inc(dve.tensor_tensor_scan(run_k[:], decay[:, c, :], f[:, 1, :], 0.0, ALU.mult, ALU.add))
                    dve.wait_ge(qkv_free, 4 * b + c + 3)
                    kv_summed = chain.inc(dve.tensor_tensor_scan(run_kv[:], decay[:, c, :], kv[:], 0.0, ALU.mult, ALU.add))
                    chain.wait(summed)
                    dve.tensor_tensor(q_sum[:, par, c, :], f[:, 0, :], run_k[:], ALU.mult)
                    chain.wait(kv_summed)
                    dve.tensor_tensor(q_kv[:, par, c, :], f[:, 0, :], run_kv[:], ALU.mult).then_inc(prod_ready, 1)

                def reciprocals(b):
                    dve.wait_ge(den_full, b + 1)
                    dve.tensor_scalar(den[:], ps_w[0][0:H, 0:T], DEN_EPS, None, ALU.max).then_inc(w_free, 1)
                    dve.wait_ge(w_free, 5 * b + 2)
                    dve.reciprocal(rden[:], den[:]).then_inc(rden_ready, 1)

                def divide(b, par):
                    dve.wait_ge(prod_ready, 4 * b + 4)
                    for g in range(2):
                        dve.wait_ge(spread_full, 2 * b + g + 1)
                        o = q_kv[:, par, 2 * g:2 * g + 2, :]
                        dve.tensor_tensor(o, o, ps_w[1 - g][:].rearrange("p (c t) -> p c t", c=2), ALU.mult) \
                           .then_inc(w_free, 1)
                    dve.wait_ge(w_free, 5 * b + 4)
                    dve.sem_inc(o_ready, 1)

                def residual(b):
                    dve.wait_ge(res_loaded, 16 * b + 16)
                    if not isinstance(b, int) or b >= 1:
                        dve.wait_ge(stored, 16 * b)
                    for t in range(TT):
                        dve.wait_ge(out_full, 2 * b + t + 1)
                        dve.tensor_tensor(x1_sb[:, t, :], ps_w[1 - t][:], x_res[:, t, :], ALU.add).then_inc(w_free, 1)
                    dve.wait_ge(w_free, 5 * b + 6)
                    dve.sem_inc(x1_ready, 1)
                    dve.sem_inc(res_free, 1)

                def body(b, par, prev, nxt):
                    first = chain.n
                    if nxt is not None:
                        scans(b, par, 0)
                    if nxt:
                        norm_stats(b + 1)
                    if prev:
                        reciprocals(b - 1)
                    if nxt is not None:
                        scans(b, par, 1)
                    if nxt:
                        norm_apply(b + 1)
                    if prev:
                        divide(b - 1, 1 - par)
                    if nxt is not None:
                        scans(b, par, 2)
                        scans(b, par, 3)
                    if prev:
                        residual(b - 1)
                    return chain.n - first

                norm_stats(0)
                norm_apply(0)
                dve.wait_ge(exp_ready, 1)
                chain.link(dve.tensor_scalar(decay_2[:], decay_1[:], 1.0, None, ALU.add))
                chain.link(dve.reciprocal(decay_1[:], decay_2[:]))
                for c in range(HC):
                    last = chain.inc(dve.tensor_scalar(decay[:, c, :], decay[:, c, :], decay_1[:, c:c + 1], None, ALU.mult))
                chain.wait(last)
                turn = 4 * 4 + 3
                body(0, 0, False, True)
                before = chain.n
                with dve.Fori(0, (B - 2) // 2) as i:
                    chain.base = i * (2 * turn)
                    assert body(i * 2 + 1, 1, True, True) == turn
                    assert body(i * 2 + 2, 0, True, True) == turn
                chain.base = 0
                chain.n = before + (B - 2) * turn
                body(B - 1, 1, True, False)
                body(B, 0, True, None)


HD = 16
N = HID
NJ = N // P
VH = HD + 1
Q_PARTS = (0, 0, 1, 1, 0, 2)
K_PARTS = (0, 1, 0, 1, 2, 0)
ROWS = len(Q_PARTS) * HD
MAX_ROWS = 3


def build_stage_b(nc, x1, ctx_in, wq, wk, wv, wm, bq_rows, bk_rows, bv_rows, bm_cols, enc, router_t, ident_in,
                  x2, xn2, logits):
    with ExitStack() as ctx:
        def sb(name, shape, dt=FP32):
            return ctx.enter_context(nc.sbuf_tensor("b_" + name, shape, dt))

        def pb(name, shape=(P, 512), dt=FP32):
            return ctx.enter_context(nc.psum_tensor("b_" + name, list(shape), dt))

        def sem(name):
            return ctx.enter_context(nc.semaphore("b_" + name))

        def dram(name, shape, dt=FP32):
            return nc.dram_tensor("b_" + name, shape, dt, kind="Internal").ap()

        w_q, w_k, w_v, w_m = (sb(n, [P, TT, T]) for n in ("w_q", "w_k", "w_v", "w_m"))
        bias_qk = sb("bias_qk", [P, 2 * T])
        bias_v = sb("bias_v", [P, T])
        bias_m = sb("bias_m", [P, TT])
        cos_f = sb("cos_f", [P, NJ, HD])
        sin_f = sb("sin_f", [P, NJ, HD])
        w_router = sb("w_router", [P, HC, 8])
        ident = sb("ident", [P, P])
        half = sb("half", [P, TT])
        x_in = sb("x_in", [P, TT, HID])
        ctx_sb = sb("ctx_sb", [P, TT, HID])
        x_res = sb("x_res", [P, TT, HID])
        stats = sb("stats", [P, TT, 6])
        mean_var = sb("mean_var", [P, TT, 2])
        var_eps = sb("var_eps", [P, TT])
        rstd = sb("rstd", [P, TT])
        stats2 = sb("stats2", [P, TT, 6])
        mean_var2 = sb("mean_var2", [P, TT, 2])
        var_eps2 = sb("var_eps2", [P, TT])
        rstd2 = sb("rstd2", [P, TT])
        xn = sb("xn", [P, TT, HID])
        qk_b = sb("qk_b", [P, 2 * T])
        rot_a = sb("rot_a", [P, 2 * T])
        rot_b = sb("rot_b", [P, 2 * T])
        qk_rot = sb("qk_rot", [P, NJ, 2 * T])
        part_rest = sb("part_rest", [P, N])
        parts = sb("parts", [P, 4, 3, N], BF16)
        q_stack = sb("q_stack", [ROWS + MAX_ROWS, 2, H, N], BF16)
        k_stack = sb("k_stack", [ROWS + MAX_ROWS, 2, H, N], BF16)
        v_sb = sb("v_sb", [P, 2, NJ, H, VH])
        row_max = sb("row_max", [P, P])
        neg_rest = sb("neg_rest", [H * NJ, P])
        neg_parts = sb("neg_parts", [H * NJ, MAX_ROWS, P], BF16)
        probs = sb("probs", [P, 2, NJ, N])
        o_sb = sb("o_sb", [VH, 2, 4, N])
        sums = sb("sums", [P, H * N // P])
        rsums = sb("rsums", [P, H * N // P])
        o_cat = sb("o_cat", [P, TT, N])
        r_cat = sb("r_cat", [P, TT, N])
        x2_sb = sb("x2_sb", [P, TT, HID])
        xn2_sb = sb("xn2_sb", [P, TT, HID])
        xn2_T = sb("xn2_T", [P, TT, HC, P])

        parts_dram = dram("parts_dram", (2, 3, 2 * P, N), BF16)
        neg_dram = dram("neg_dram", (MAX_ROWS, H * N), BF16)
        o_dram = dram("o_dram", (H, HD, N))
        sum_dram = dram("sum_dram", (H, N))
        rsum_dram = dram("rsum_dram", (H, N))
        rsum16_dram = dram("rsum16_dram", (H, HD, N))

        ps_s = [pb(f"ps_s{i}", (P, 2 * N)) for i in range(2)]
        ps_o = [pb(f"ps_o{i}") for i in range(2)]
        ps_w = [pb(f"ps_w{i}") for i in range(2)]

        consts_in = sem("consts_in")
        x_loaded, ctx_loaded, res_loaded = sem("x_loaded"), sem("ctx_loaded"), sem("res_loaded")
        x_free = sem("x_free")
        ctx_free = sem("ctx_free")
        res_free = sem("res_free")
        var_ready, rstd_ready, xn_ready = sem("var_ready"), sem("rstd_ready"), sem("xn_ready")
        var2_ready, rstd2_ready = sem("var2_ready"), sem("rstd2_ready")
        w_full = sem("w_full")
        w_free = sem("w_free")
        rot_ready = sem("rot_ready")
        parts_ready = sem("parts_ready")
        parts_stored = sem("parts_stored")
        stacks_in = sem("stacks_in")
        v_ready = sem("v_ready")
        max_ready = sem("max_ready")
        neg_ready, neg_stored, neg_in = sem("neg_ready"), sem("neg_stored"), sem("neg_in")
        s_full = sem("s_full")
        e_ready = sem("e_ready")
        pv_done = sem("pv_done")
        o_kept = sem("o_kept")
        o_stored = [sem(f"o_stored{i}") for i in range(2)]
        o_loaded, sums_loaded = sem("o_loaded"), sem("sums_loaded")
        rsums_ready, rsums_moved, r_loaded = sem("rsums_ready"), sem("rsums_moved"), sem("r_loaded")
        o_ready = sem("o_ready")
        o_used = sem("o_used")
        x2_ready, xn2_ready, x2_stored = sem("x2_ready"), sem("xn2_ready"), sem("x2_stored")
        xn2T_ready = sem("xn2T_ready")
        s_dve = sem("dve")
        passed = sem("passed")

        SLOT_QK = {1: (0, 1), 2: (2, 3)}
        SLOT_T = {3: (0, 1), 4: (2, 3)}
        SLOT_V, SLOT_MERGE, SLOT_NORM, SLOT_LOGITS = 5, 5, 7, 8
        SLOT_MAX = {8: 2, 9: 3, 10: 3, 11: 3, 12: 3, 13: 2}
        assert sum(SLOT_MAX.values()) == H
        PRE_USES = 4 + 4 + 2 + 4 * H + 1
        POST_USES = 2 + 2 + 1

        def slots(body_slot):
            first_max = 0
            for h in range(H):
                n = SLOT_MAX.get(h, 0)
                body_slot(h, range(first_max, first_max + n))
                first_max += n

        def batches(engine, body, count=None, turn=0):
            body(0, 0, False, True)
            before = count.n if count else 0
            with engine.Fori(0, (B - 2) // 2) as i:
                for k in range(2):
                    if count:
                        count.base = i * (2 * turn)
                    body(i * 2 + 1 + k, 1 - k, True, True)
                    if count:
                        assert count.n - before == (k + 1) * turn, (count.n - before, turn)
            if count:
                count.base, count.n = 0, before + (B - 2) * turn
            body(B - 1, 1, True, False)
            body(B, 0, True, None)

        def rows(ap, b):
            return ap[bass.ds(b, 1)].rearrange("a (t p) n -> p (a t) n", p=P)

        with nc.Block() as block:
            @block.sync
            def _(sp):
                def wait(s, value):
                    sp.wait_ge(s, value)
                    sp.sem_inc(passed, 1)

                def load_inputs(b):
                    if not isinstance(b, int) or b >= 1:
                        wait(x_free, b)
                        wait(ctx_free, b)
                    sp.dma_start(x_in[:], rows(x1, b)).then_inc(x_loaded, 16)
                    sp.dma_start(ctx_sb[:], rows(ctx_in, b)).then_inc(ctx_loaded, 16)

                def restack(b, par, side):
                    for t in (2 * side, 2 * side + 1):
                        wait(parts_ready, 4 * b + t + 1)
                        sp.dma_start(parts_dram[side, :, (t % 2) * P:(t % 2 + 1) * P, :].rearrange("s p n -> p s n"),
                                     parts[:, t]).then_inc(parts_stored, 16)
                    wait(parts_stored, 64 * b + 32 * side + 32)
                    stack, order = ((q_stack, Q_PARTS), (k_stack, K_PARTS))[side]
                    for s, part in enumerate(order):
                        sp.dma_start(stack[s * HD:(s + 1) * HD, par, :, :],
                                     parts_dram[side, part].rearrange("(h d) n -> d h n", d=HD)).then_inc(stacks_in, 16)

                def max_rows(b, par):
                    wait(neg_ready, b + 1)
                    sp.dma_start(neg_dram.rearrange("s (r n) -> r s n", n=P), neg_parts[:]).then_inc(neg_stored, 16)
                    wait(neg_stored, 16 * b + 16)
                    sp.dma_start(q_stack[ROWS:ROWS + MAX_ROWS, par, :, :],
                                 neg_dram.rearrange("s (h n) -> s h n", h=H)).then_inc(neg_in, 16)
                    wait(neg_in, 16 * b + 16)

                def outputs_in(b):
                    wait(o_stored[0], 64 * b + 64 + 32)
                    wait(o_stored[1], 64 * b + 64 + 32)
                    wait(o_used, b + 1)
                    sp.dma_start(sums[:], sum_dram.rearrange("h (q n) -> (h q) n", n=H * N // P)).then_inc(sums_loaded, 16)
                    sp.dma_start(o_cat[:], o_dram.rearrange("(t h) d n -> (h d) t n", t=TT)).then_inc(o_loaded, 16)
                    wait(res_free, b + 1)
                    sp.dma_start(x_res[:], rows(x1, b)).then_inc(res_loaded, 16)
                    wait(rsums_ready, b + 1)
                    sp.dma_start(rsum_dram.rearrange("h (q n) -> (h q) n", n=H * N // P), rsums[:]).then_inc(rsums_moved, 16)
                    wait(rsums_moved, 32 * b + 16)
                    sp.dma_start(rsum16_dram, rsum_dram.unsqueeze(1).to_broadcast([H, HD, N])).then_inc(rsums_moved, 16)
                    wait(rsums_moved, 32 * b + 32)
                    sp.dma_start(r_cat[:], rsum16_dram.rearrange("(t h) d n -> (h d) t n", t=TT)).then_inc(r_loaded, 16)
                    wait(r_loaded, 16 * b + 16)

                def results_out(b):
                    wait(x2_ready, b + 1)
                    sp.dma_start(rows(x2, b), x2_sb[:]).then_inc(x2_stored, 16)
                    wait(xn2_ready, b + 1)
                    sp.dma_start(rows(xn2, b), xn2_sb[:]).then_inc(x2_stored, 16)

                load_inputs(0)
                for tile, src in ((w_q, wq), (w_k, wk), (w_v, wv), (w_m, wm)):
                    sp.dma_start(tile[:], src.rearrange("(c p) n -> p c n", p=P)).then_inc(consts_in, 16)
                for tile, src in ((bias_qk[:, 0:T], bq_rows), (bias_qk[:, T:2 * T], bk_rows), (bias_v[:], bv_rows)):
                    sp.dma_start(tile, src.to_broadcast([P, T])).then_inc(consts_in, 16)
                sp.dma_start(cos_f[:], enc[0].rearrange("(j p) d -> p j d", p=P)).then_inc(consts_in, 16)
                sp.dma_start(sin_f[:], enc[1].rearrange("(j p) d -> p j d", p=P)).then_inc(consts_in, 16)
                sp.dma_start(w_router[:], router_t.rearrange("(c p) e -> p c e", p=P)).then_inc(consts_in, 16)
                sp.dma_start(ident[:], ident_in).then_inc(consts_in, 16)
                sp.dma_start(bias_m[:], bm_cols).then_inc(consts_in, 16)
                restack(0, 0, 0)
                restack(0, 0, 1)
                max_rows(0, 0)

                def body(b, par, prev, nxt):
                    if nxt:
                        load_inputs(b + 1)
                    if prev:
                        outputs_in(b - 1)
                    if nxt:
                        if prev:
                            wait(s_full, b * (2 * H))
                        restack(b + 1, 1 - par, 0)
                        restack(b + 1, 1 - par, 1)
                    if prev:
                        results_out(b - 1)
                    if nxt:
                        max_rows(b + 1, 1 - par)

                batches(sp, body)
                wait(x2_stored, 32 * B)

            @block.gpsimd
            def _(pool):
                pool.memset(half[:], -0.5).then_inc(rstd_ready, 1)
                pool.wait_ge(rstd_ready, 1)

                def rstd_of(b):
                    pool.wait_ge(var_ready, b + 1)
                    pool.tensor_tensor(rstd[:], var_eps[:], half[:], ALU.pow).then_inc(rstd_ready, 1)

                def normalise(b):
                    pool.wait_ge(o_loaded, 16 * b + 16)
                    pool.wait_ge(r_loaded, 16 * b + 16)
                    pool.tensor_tensor(o_cat[:], o_cat[:], r_cat[:], ALU.mult).then_inc(o_ready, 1)
                    pool.wait_ge(var2_ready, b + 1)
                    pool.tensor_tensor(rstd2[:], var_eps2[:], half[:], ALU.pow).then_inc(rstd2_ready, 1)

                def body(b, par, prev, nxt):
                    if nxt:
                        rstd_of(b + 1)
                    if prev:
                        normalise(b - 1)

                rstd_of(0)
                batches(pool, body)

            @block.scalar
            def _(act):
                for s in o_stored:
                    act.sem_inc(s, 32)
                act.sem_inc(e_ready, 2)
                act.sem_inc(o_kept, 2)

                def exps(b, par, h):
                    act.wait_ge(pv_done, H * b + h + 1)
                    for m in range(2):
                        act.wait_ge(s_full, 2 * H * b + 2 * h + m + 1)
                        act.activation(probs[:, h % 2, 2 * m:2 * m + 2, :], ps_s[m][:].rearrange("p (m n) -> p m n", m=2),
                                       ACT.Exp, scale=HD ** -0.5).then_inc(e_ready, 1)

                def keep(b, par, h, prev):
                    g = h // 4
                    if h % 4 == 0:
                        act.wait_ge(o_stored[g % 2], 64 * b + 32 * (g // 2) + 32)
                    act.wait_ge(pv_done, H * b + h + 3)
                    act.copy(o_sb[:, g % 2, h % 4, :], ps_o[h % 2][0:VH, :]).then_inc(o_kept, 1)
                    if h % 4 == 3:
                        if g == 0 and prev:
                            act.wait_ge(o_loaded, 16 * b)
                            act.wait_ge(sums_loaded, 16 * b)
                        act.wait_ge(o_kept, H * b + h + 3)
                        act.dma_start(o_dram[4 * g:4 * g + 4].rearrange("h d n -> d h n"), o_sb[0:HD, g % 2]).then_inc(o_stored[g % 2], 16)
                        act.dma_start(sum_dram[4 * g:4 * g + 4].unsqueeze(0), o_sb[HD:VH, g % 2]).then_inc(o_stored[g % 2], 16)

                def body(b, par, prev, nxt):
                    if nxt is None:
                        return
                    for h in range(H):
                        exps(b, par, h)
                        if h:
                            keep(b, par, h - 1, prev)
                    keep(b, par, H - 1, prev)

                batches(act, body)

            @block.tensor
            def _(pe):
                uses = Count(pe, w_full)

                def bank():
                    pe.wait_ge(w_free, uses.base + uses.n + 1)
                    return ps_w[uses.n % 2]

                def project_qk(b, j):
                    w = bank()
                    for side, (src, weight) in enumerate(((xn, w_q), (ctx_sb, w_k))):
                        for c in range(TT):
                            last = pe.matmul(w[:, side * T:(side + 1) * T], src[:, c, j * P:(j + 1) * P], weight[:, c, :],
                                             start=(c == 0), stop=(c == TT - 1))
                    uses.inc(last)

                def project_v(b):
                    for i in range(2):
                        w = bank()
                        for k in range(2):
                            j = 2 * i + k
                            for c in range(TT):
                                last = pe.matmul(w[:, k * T:(k + 1) * T], ctx_sb[:, c, j * P:(j + 1) * P], w_v[:, c, :],
                                                 start=(c == 0), stop=(c == TT - 1))
                        uses.inc(last)

                def transpose_qk(b, t):
                    if t == 0:
                        pe.wait_ge(rot_ready, 4 * b + 4)
                    w = bank()
                    for j in range(NJ):
                        last = pe.transpose(w[:, j * P:(j + 1) * P], qk_rot[:, j, t * P:(t + 1) * P], ident[:])
                    uses.inc(last)

                def maxima(b, par, h):
                    if h == 0:
                        pe.wait_ge(stacks_in, 192 * b + 192)
                    for j in range(NJ):
                        w = bank()
                        uses.inc(pe.matmul(w[:], q_stack[0:ROWS, par, h, j * P:(j + 1) * P], k_stack[0:ROWS, par, h, :],
                                           start=True, stop=True))

                def transpose_max(b):
                    pe.wait_ge(max_ready, b + 1)
                    w = bank()
                    uses.inc(pe.transpose(w[:, 0:P], row_max[:], ident[:]))

                def scores(b, par, h):
                    if h == 0:
                        pe.wait_ge(neg_in, 16 * b + 16)
                        pe.wait_ge(v_ready, 2 * b + 2)
                    for m in range(2):
                        pe.wait_ge(e_ready, 2 * H * b + 2 * h + m + 1)
                        for k in range(2):
                            j = 2 * m + k
                            last = pe.matmul(ps_s[m][:, k * N:(k + 1) * N], k_stack[:, par, h, j * P:(j + 1) * P],
                                             q_stack[:, par, h, :], start=True, stop=True)
                        last.then_inc(s_full, 1)

                def probs_v(b, par, h):
                    pe.wait_ge(o_kept, H * b + h + 1)
                    for m in range(2):
                        pe.wait_ge(e_ready, 2 * H * b + 2 * h + m + 3)
                        for j in (2 * m, 2 * m + 1):
                            last = pe.matmul(ps_o[h % 2][0:VH, :], v_sb[:, par, j, h, :], probs[:, h % 2, j, :],
                                             start=(j == 0), stop=(j == NJ - 1))
                    last.then_inc(pv_done, 1)

                def merge(b):
                    pe.wait_ge(o_ready, b + 1)
                    for t in range(TT):
                        w = bank()
                        for c in range(TT):
                            last = pe.matmul(w[:], w_m[:, c, t * P:(t + 1) * P], o_cat[:, c, :], start=(c == 0), stop=(c == TT - 1))
                        uses.inc(last)

                def transpose_xn2(b):
                    pe.wait_ge(xn2_ready, b + 1)
                    for t in range(TT):
                        w = bank()
                        for c in range(HC):
                            last = pe.transpose(w[:, c * P:(c + 1) * P], xn2_sb[:, t, c * P:(c + 1) * P], ident[:])
                        uses.inc(last)

                def route(b):
                    pe.wait_ge(xn2T_ready, 2 * b + 2)
                    w = bank()
                    for t in range(TT):
                        for c in range(HC):
                            last = pe.matmul(w[:, t * 8:(t + 1) * 8], xn2_T[:, t, c, :], w_router[:, c, :],
                                             start=(c == 0), stop=(c == HC - 1))
                    uses.inc(last)

                def body(b, par, prev, nxt):
                    def slot(h, maxima_of):
                        if nxt is not None:
                            scores(b, par, h)
                            if h:
                                probs_v(b, par, h - 1)
                        if nxt:
                            if h == 1:
                                pe.wait_ge(xn_ready, b + 2)
                                pe.wait_ge(ctx_loaded, 16 * b + 32)
                            for j in SLOT_QK.get(h, ()):
                                project_qk(b + 1, j)
                            for t in SLOT_T.get(h, ()):
                                transpose_qk(b + 1, t)
                            if h == SLOT_V:
                                project_v(b + 1)
                        if prev:
                            if h == SLOT_MERGE:
                                merge(b - 1)
                            if h == SLOT_NORM:
                                transpose_xn2(b - 1)
                            if h == SLOT_LOGITS:
                                route(b - 1)
                        if nxt:
                            for k in maxima_of:
                                maxima(b + 1, 1 - par, k)
                            if h == max(SLOT_MAX) + 1:
                                transpose_max(b + 1)

                    slots(slot)
                    if nxt is not None:
                        probs_v(b, par, H - 1)

                pe.wait_ge(consts_in, 16 * 12)
                pe.wait_ge(xn_ready, 1)
                pe.wait_ge(ctx_loaded, 16)
                for j in range(NJ):
                    project_qk(0, j)
                for t in range(4):
                    transpose_qk(0, t)
                project_v(0)
                for h in range(H):
                    maxima(0, 0, h)
                transpose_max(0)
                batches(pe, body, uses, PRE_USES + POST_USES)

            @block.vector
            def _(dve):
                chain = Count(dve, s_dve)
                taken = Count(dve, w_free)

                def bank():
                    dve.wait_ge(w_full, taken.base + taken.n + 1)
                    return ps_w[taken.n % 2]

                def norm(b):
                    dve.wait_ge(x_loaded, 16 * b + 16)
                    chain.link(layer_norm_stats(dve, chain, x_in, stats, mean_var))
                    dve.tensor_scalar(var_eps[:], mean_var[:, :, 1], LN_EPS, None, ALU.add).then_inc(var_ready, 1)
                    dve.wait_ge(rstd_ready, b + 2)
                    for t in range(TT):
                        last = dve.tensor_scalar(xn[:, t, :], x_in[:, t, :], mean_var[:, t, 0:1], rstd[:, t:t + 1],
                                                 ALU.subtract, ALU.mult)
                    last.then_inc(xn_ready, 1)
                    dve.wait_ge(xn_ready, b + 1)
                    dve.sem_inc(x_free, 1)

                def heads_of(ap):
                    return ap.rearrange("p (h k r) -> p h k r", h=2 * H, r=2)

                def rotate(b, j):
                    w = bank()
                    mark = taken.inc(dve.tensor_tensor(qk_b[:], w[:], bias_qk[:], ALU.add))
                    taken.wait(mark + 2)
                    t = qk_b[:].rearrange("p (h d) -> p h d", d=HD)
                    dve.tensor_tensor(rot_a[:].rearrange("p (h d) -> p h d", d=HD), t,
                                      cos_f[:, j, :].unsqueeze(1).to_broadcast([P, 2 * H, HD]), ALU.mult)
                    t, o = heads_of(qk_b[:]), heads_of(rot_b[:])
                    sin = sin_f[:, j, :].rearrange("p (k r) -> p k r", r=2)
                    for r in range(2):
                        last = dve.tensor_tensor(o[:, :, :, r], t[:, :, :, 1 - r],
                                                 sin[:, :, r].unsqueeze(1).to_broadcast([P, 2 * H, HD // 2]), ALU.mult)
                    chain.link(last)
                    dve.tensor_tensor(qk_rot[:, j, :], rot_a[:], rot_b[:], ALU.add).then_inc(rot_ready, 1)

                def split(b, t):
                    w = bank()
                    if t == 0 and not isinstance(b, int):
                        dve.wait_ge(parts_stored, 64 * b)
                    elif t == 0 and b >= 1:
                        dve.wait_ge(parts_stored, 64 * b)
                    p = parts[:, t]
                    chain.link(dve.tensor_copy(p[:, 0, :], w[:]))
                    mark = taken.inc(dve.tensor_tensor(part_rest[:], w[:], p[:, 0, :], ALU.subtract))
                    taken.wait(mark + 2)
                    chain.link(dve.tensor_copy(p[:, 1, :], part_rest[:]))
                    dve.tensor_tensor(p[:, 2, :], part_rest[:], p[:, 1, :], ALU.subtract).then_inc(parts_ready, 1)

                def keep_v(b, par):
                    for i in range(2):
                        w = bank()
                        mark = taken.inc(dve.tensor_tensor(
                            v_sb[:, par, 2 * i:2 * i + 2, :, 0:HD], w[:].rearrange("p (j h d) -> p j h d", j=2, d=HD),
                            bias_v[:].rearrange("p (h d) -> p h d", d=HD).unsqueeze(1).to_broadcast([P, 2, H, HD]), ALU.add))
                    taken.wait(mark + 2)
                    dve.sem_inc(v_ready, 2)
                    dve.sem_inc(ctx_free, 1)

                def reduce_max(b, h):
                    for j in range(NJ):
                        w = bank()
                        mark = taken.inc(dve.tensor_reduce(row_max[:, h * NJ + j:h * NJ + j + 1], w[:], AX.X, ALU.max))
                    return mark

                def negate_max(b, mark):
                    taken.wait(mark + 2)
                    dve.sem_inc(max_ready, 1)
                    w = bank()[0:H * NJ, 0:P]
                    chain.link(dve.tensor_scalar(neg_parts[:, 0, :], w, -1.0, None, ALU.mult))
                    mark = taken.inc(dve.scalar_tensor_tensor(neg_rest[:], w, -1.0, neg_parts[:, 0, :], ALU.mult, ALU.subtract))
                    taken.wait(mark + 2)
                    chain.link(dve.tensor_copy(neg_parts[:, 1, :], neg_rest[:]))
                    dve.tensor_tensor(neg_parts[:, 2, :], neg_rest[:], neg_parts[:, 1, :], ALU.subtract).then_inc(neg_ready, 1)

                def reciprocals(b):
                    dve.wait_ge(sums_loaded, 16 * b + 16)
                    dve.reciprocal(rsums[:], sums[:]).then_inc(rsums_ready, 1)

                def residual(b):
                    dve.wait_ge(res_loaded, 16 * b + 16)
                    if not isinstance(b, int) or b >= 1:
                        dve.wait_ge(x2_stored, 32 * b)
                    for t in range(TT):
                        w = bank()
                        mark = taken.inc(dve.scalar_tensor_tensor(x2_sb[:, t, :], w[:], bias_m[:, t:t + 1], x_res[:, t, :],
                                                                  ALU.add, ALU.add))
                    taken.wait(mark + 2)
                    dve.sem_inc(x2_ready, 1)
                    dve.sem_inc(res_free, 1)
                    dve.sem_inc(o_used, 1)
                    chain.link(layer_norm_stats(dve, chain, x2_sb, stats2, mean_var2))
                    dve.tensor_scalar(var_eps2[:], mean_var2[:, :, 1], LN_EPS, None, ALU.add).then_inc(var2_ready, 1)
                    dve.wait_ge(rstd2_ready, b + 1)
                    for t in range(TT):
                        last = dve.tensor_scalar(xn2_sb[:, t, :], x2_sb[:, t, :], mean_var2[:, t, 0:1], rstd2[:, t:t + 1],
                                                 ALU.subtract, ALU.mult)
                    last.then_inc(xn2_ready, 1)

                def keep_xn2_T(b):
                    for t in range(TT):
                        w = bank()
                        mark = taken.inc(dve.tensor_copy(xn2_T[:, t], w[:].rearrange("p (c q) -> p c q", c=HC)))
                    taken.wait(mark + 2)
                    dve.sem_inc(xn2T_ready, 2)

                def keep_logits(b):
                    w = bank()
                    taken.inc(dve.tensor_copy(logits[:, bass.ds(b * TT, TT), :],
                                              w[:, 0:TT * 8].rearrange("p (t e) -> p t e", t=TT)))

                TURN = 3 + 4 + 4 * 2 + 2 + 3

                def body(b, par, prev, nxt):
                    first, mark = chain.n, [None]
                    if nxt:
                        norm(b + 1)
                    if prev:
                        reciprocals(b - 1)

                    def slot(h, maxima_of):
                        if nxt:
                            for j in SLOT_QK.get(h, ()):
                                rotate(b + 1, j)
                            for t in SLOT_T.get(h, ()):
                                split(b + 1, t)
                            if h == SLOT_V:
                                keep_v(b + 1, 1 - par)
                        if prev:
                            if h == SLOT_MERGE:
                                residual(b - 1)
                            if h == SLOT_NORM:
                                keep_xn2_T(b - 1)
                            if h == SLOT_LOGITS:
                                keep_logits(b - 1)
                        if nxt:
                            for k in maxima_of:
                                mark[0] = reduce_max(b + 1, k)
                            if h == max(SLOT_MAX) + 1:
                                negate_max(b + 1, mark[0])

                    slots(slot)
                    return chain.n - first

                chain.inc(dve.memset(v_sb[:, :, :, :, HD:VH], 1.0))
                chain.inc(dve.memset(row_max[:], 0.0))
                chain.link(dve.memset(k_stack[ROWS:ROWS + MAX_ROWS], 1.0))
                for s, n in ((res_free, 1), (w_free, 2), (pv_done, 2), (o_used, 1)):
                    dve.sem_inc(s, n)
                dve.wait_ge(consts_in, 16 * 12)
                for j in range(NJ):
                    even = sin_f[:, j, :].rearrange("p (k r) -> p k r", r=2)[:, :, 0]
                    last = chain.inc(dve.tensor_scalar(even, even, -1.0, None, ALU.mult))
                chain.wait(last)
                norm(0)
                for j in range(NJ):
                    rotate(0, j)
                for t in range(4):
                    split(0, t)
                keep_v(0, 0)
                for h in range(H):
                    last = reduce_max(0, h)
                negate_max(0, last)

                body(0, 0, False, True)
                before, used = chain.n, taken.n
                assert used % 2 == 0
                with dve.Fori(0, (B - 2) // 2) as i:
                    for k in range(2):
                        chain.base, taken.base = i * (2 * TURN), i * (2 * (PRE_USES + POST_USES))
                        assert body(i * 2 + 1 + k, 1 - k, True, True) == TURN
                chain.base, chain.n = 0, before + (B - 2) * TURN
                taken.base, taken.n = 0, used + (B - 2) * (PRE_USES + POST_USES)
                body(B - 1, 1, True, False)
                body(B, 0, True, None)


E = 8
TOP = 2
F = 352
FC = (F + P - 1) // P
TOKENS = B * T
TILES = TOKENS // P
PAIRS = TOP * TILES
BLOCKS = PAIRS + E - 1
NOBODY = 2 * TOKENS


def build_stage_c(nc, xn2, logits, w1_t, w2_t, ident_in, before_in, numbers_in, out):
    with ExitStack() as ctx:
        def sb(name, shape, dt=FP32):
            return ctx.enter_context(nc.sbuf_tensor("c_" + name, shape, dt))

        def pb(name, shape=(P, 512), dt=FP32):
            return ctx.enter_context(nc.psum_tensor("c_" + name, list(shape), dt))

        def sem(name):
            return ctx.enter_context(nc.semaphore("c_" + name))

        W1 = HC * 2 * F
        W2 = FC * HID
        w1_sb = sb("w1", [P, E * W1])
        w2_sb = sb("w2", [P, E * W2])
        ident = sb("ident", [P, P])
        before = sb("before", [P, 2, P])
        numbers = sb("numbers", [P, P])
        token = sb("token", [P, TILES])
        best = sb("best", [P, TILES, E])
        best_at = sb("best_at", [P, TILES, E], U32)
        choice = sb("choice", [P, TOP, TILES])
        gap = sb("gap", [P, TILES])
        gate = sb("gate", [P, TOP, TILES])
        chosen = sb("chosen", [P, TOP, TILES, E])
        both = sb("both", [P, TILES, E])
        ones = sb("ones", [P, TILES])
        in_tile = sb("in_tile", [P, E, TILES])
        up_to = sb("up_to", [P, E, TILES])
        count_i = sb("count_i", [P, E], I32)
        n_blocks = sb("n_blocks", [P, E])
        block_end = sb("block_end", [P, E])
        start = sb("start", [P, E])
        place = sb("place", [P, TILES, E])
        pos = sb("pos", [P, TOP, TILES])
        pos_i = sb("pos_i", [P, TOP, TILES], I32)
        part_i = sb("part_i", [P, 2, TOP, TILES], I32)
        block_row = sb("block_row", [P, 2, TOP, TILES])
        ge = sb("ge", [1, BLOCKS, E])
        expert = sb("expert", [1, BLOCKS])
        expert_i = sb("expert_i", [1, BLOCKS], I32)
        is_row = sb("is_row", [P, 4, P])
        in_block = sb("in_block", [P, 4, 2, BLOCKS])
        ids = sb("ids", [P, BLOCKS], I32)
        gates = sb("gates", [P, BLOCKS])
        id_in = sb("id_in", [P, 2], I32)
        id_out = sb("id_out", [P, 2], I32)
        xb = sb("xb", [P, 2, HID])
        xbT = sb("xbT", [P, 2, HC, P])
        silu = sb("silu", [P, 2, F])
        hidden = sb("hidden", [P, 2, FC * P])
        hiddenT = sb("hiddenT", [P, 2, FC, P])
        yb = sb("yb", [P, 2, HID])

        ps_g = [pb(f"ps_g{i}") for i in range(2)]
        ps_u = [pb(f"ps_u{i}") for i in range(2)]
        ps_y = [pb(f"ps_y{i}") for i in range(2)]
        ps_xT, ps_hT = pb("ps_xT"), pb("ps_hT")

        consts_in, w_in = sem("consts_in"), sem("w_in")
        token_ready = sem("token_ready")
        gap_ready, gate_ready = sem("gap_ready"), sem("gate_ready")
        both_ready, ranks_full, places_full = sem("both_ready"), sem("ranks_full"), sem("places_full")
        onehots, onehots_used = sem("onehots"), sem("onehots_used")
        plan_ready = sem("plan_ready")
        id_free = sem("id_free")
        gathered = [sem(f"gathered{i}") for i in range(2)]
        scattered = sem("scattered")
        xT_full, xT_ready = sem("xT_full"), sem("xT_ready")
        g_full, u_full, silu_ready, hidden_ready = sem("g_full"), sem("u_full"), sem("silu_ready"), sem("hidden_ready")
        hT_full, hT_ready, y_full, y_ready = sem("hT_full"), sem("hT_ready"), sem("y_full"), sem("y_ready")
        id_ready, id_out_ready = sem("id_ready"), sem("id_out_ready")
        s_dve = sem("dve")
        passed = sem("passed")
        assert (BLOCKS - 5) % 2 == 0

        def done(i):
            return i + 3

        def blocks(engine, body):
            body(0, 0, False, True, True)
            body(1, 1, True, True, True)
            body(2, 0, True, True, True)
            with engine.Fori(0, (BLOCKS - 5) // 2) as n:
                body(n * 2 + 3, 1, True, True, True)
                body(n * 2 + 4, 0, True, True, True)
            body(BLOCKS - 2, (BLOCKS - 2) % 2, True, True, False)
            body(BLOCKS - 1, (BLOCKS - 1) % 2, True, False, False)
            body(BLOCKS, BLOCKS % 2, True, None, False)

        with nc.Block() as block:
            @block.sync
            def _(sp):
                sp.dma_start(ident[:], ident_in).then_inc(consts_in, 16)
                sp.dma_start(before[:], before_in).then_inc(consts_in, 16)
                sp.dma_start(numbers[:], numbers_in).then_inc(consts_in, 16)
                for e in range(E):
                    sp.dma_start(w1_sb[:, e * W1:(e + 1) * W1].rearrange("p (c n) -> p c n", c=HC),
                                 w1_t[e].rearrange("(c p) n -> p c n", p=P)).then_inc(w_in, 16)
                    for c in range(FC):
                        k = min(P, F - c * P)
                        sp.dma_start(w2_sb[0:k, e * W2 + c * HID:e * W2 + (c + 1) * HID],
                                     w2_t[e, c * P:c * P + k, :]).then_inc(w_in, 16)

            @block.gpsimd
            def _(pool):
                pool.iota(token[:], [[P, TILES]], base=-NOBODY, channel_multiplier=1,
                          allow_small_or_imprecise_dtypes=True).then_inc(token_ready, 1)

                def wait(s, value):
                    pool.wait_ge(s, value)
                    pool.sem_inc(passed, 1)

                def gather(i, par):
                    wait(xT_full, done(i - 2))
                    pool.tensor_copy(id_in[:, par:par + 1], ids[:, bass.ds(i, 1)]).then_inc(id_ready, 1)
                    wait(id_ready, i + 1)
                    pool.indirect_dma_start(xb[:, par, :], None, xn2, bass.IndirectOffsetOnAxis(ap=id_in[:, par:par + 1].bitcast(U32), axis=0),
                                            bounds_check=last_token, oob_is_err=False).then_inc(gathered[par], 16)

                def scatter(i, par):
                    if not isinstance(i, int) or i >= 1:
                        wait(scattered, 16 * i)
                    pool.tensor_copy(id_out[:, par:par + 1], ids[:, bass.ds(i, 1)]).then_inc(id_out_ready, 1)
                    wait(id_out_ready, i + 1)
                    wait(y_ready, done(i))
                    pool.indirect_dma_start(out, bass.IndirectOffsetOnAxis(ap=id_out[:, par:par + 1].bitcast(U32), axis=0), yb[:, par, :], None,
                                            bounds_check=last_token, oob_is_err=False, compute_op=ALU.add).then_inc(scattered, 16)

                def body(i, par, prev, nxt, nxt2):
                    if nxt2:
                        gather(i + 2, par)
                    if prev:
                        scatter(i - 1, 1 - par)

                last_token = pool.to_reg(TOKENS - 1)
                pool.wait_ge(plan_ready, 1)
                gather(0, 0)
                gather(1, 1)
                blocks(pool, body)
                pool.wait_ge(scattered, 16 * BLOCKS)

            @block.tensor
            def _(pe):
                pe.wait_ge(consts_in, 48)
                pe.wait_ge(both_ready, 1)
                o = both[:].rearrange("p t e -> p (t e)")
                pe.matmul(ps_g[0][:, 0:TILES * E], before[:, 0, :], o, start=True, stop=True)
                pe.matmul(ps_g[1][:, 0:TILES * E], before[:, 1, :], o, start=True, stop=True).then_inc(ranks_full, 1)
                for n in range(PAIRS):
                    pe.wait_ge(onehots, n + 1)
                    pe.matmul(ps_y[0][:, 0:2 * BLOCKS], is_row[:, n % 4, :], in_block[:, n % 4].rearrange("p k n -> p (k n)"),
                              start=(n == 0), stop=(n == PAIRS - 1)).then_inc(onehots_used, 1)

                def transpose_x(i, par):
                    pe.wait_ge(gathered[par], gathers_of(i, par))
                    pe.wait_ge(xT_ready, done(i - 1))
                    for c in range(HC):
                        last = pe.transpose(ps_xT[:, c * P:(c + 1) * P], xb[:, par, c * P:(c + 1) * P], ident[:])
                    last.then_inc(xT_full, 1)

                def gathers_of(i, par):
                    return (i - par) * 8 + 16

                def up(i, par):
                    e = pe.value_load(expert_i[0:1, bass.ds(i, 1)], min_val=0, max_val=E - 1)
                    pe.wait_ge(xT_ready, done(i))
                    for half, (ps, free, full) in enumerate(((ps_g, silu_ready, g_full), (ps_u, hidden_ready, u_full))):
                        pe.wait_ge(free, done(i - 2))
                        for c in range(HC):
                            last = pe.matmul(ps[par][:, 0:F], xbT[:, par, c, :],
                                             w1_sb[:, bass.ds(e * W1 + (c * 2 + half) * F, F)], start=(c == 0), stop=(c == HC - 1))
                        last.then_inc(full, 1)

                def transpose_hidden(i, par):
                    pe.wait_ge(hidden_ready, done(i))
                    pe.wait_ge(hT_ready, done(i - 1))
                    for c in range(FC):
                        last = pe.transpose(ps_hT[:, c * P:(c + 1) * P], hidden[:, par, c * P:(c + 1) * P], ident[:])
                    last.then_inc(hT_full, 1)

                def down(i, par):
                    e = pe.value_load(expert_i[0:1, bass.ds(i, 1)], min_val=0, max_val=E - 1)
                    pe.wait_ge(hT_ready, done(i))
                    pe.wait_ge(y_ready, done(i - 2))
                    for c in range(FC):
                        k = min(P, F - c * P)
                        last = pe.matmul(ps_y[par][:, :], hiddenT[0:k, par, c, :], w2_sb[0:k, bass.ds(e * W2 + c * HID, HID)],
                                         start=(c == 0), stop=(c == FC - 1))
                    last.then_inc(y_full, 1)

                def body(i, par, prev, nxt, nxt2):
                    if nxt is not None:
                        up(i, par)
                    if prev:
                        transpose_hidden(i - 1, 1 - par)
                    if nxt:
                        transpose_x(i + 1, 1 - par)
                    if prev:
                        down(i - 1, 1 - par)

                pe.wait_ge(plan_ready, 1)
                pe.wait_ge(w_in, 16 * (1 + FC) * E)
                transpose_x(0, 0)
                blocks(pe, body)

            @block.scalar
            def _(act):
                act.wait_ge(gap_ready, 1)
                act.activation(gate[:, 1, :], gap[:], ACT.Exp).then_inc(gate_ready, 1)

                def keep_xT(i, par):
                    act.wait_ge(xT_full, done(i))
                    act.wait_ge(u_full, done(i - 2))
                    act.copy(xbT[:, par], ps_xT[:].rearrange("p (c q) -> p c q", c=HC)).then_inc(xT_ready, 1)

                def body(i, par, prev, nxt, nxt2):
                    if nxt is not None:
                        act.wait_ge(g_full, done(i))
                        act.wait_ge(hidden_ready, done(i - 2))
                        act.activation(silu[:, par, :], ps_g[par][:, 0:F], ACT.Silu).then_inc(silu_ready, 1)
                    if nxt:
                        keep_xT(i + 1, 1 - par)

                keep_xT(0, 0)
                blocks(act, body)

            @block.vector
            def _(dve):
                chain = Count(dve, s_dve)
                for s in (xT_full, xT_ready, g_full, u_full, silu_ready, hidden_ready, hT_full, hT_ready, y_full, y_ready):
                    dve.sem_inc(s, 2)
                dve.memset(xb[:], 0.0)
                dve.memset(hidden[:], 0.0)
                chain.link(dve.memset(ones[:], 1.0))
                for t in range(TILES):
                    last = chain.inc(dve.max(best[:, t, :], logits[:, t, :]))
                chain.wait(last)
                for t in range(TILES):
                    last = chain.inc(dve.max_index(best_at[:, t, :], best[:, t, :], logits[:, t, :]))
                dve.tensor_tensor(gap[:], best[:, :, 1], best[:, :, 0], ALU.subtract).then_inc(gap_ready, 1)
                chain.wait(last)
                for k in range(TOP):
                    last = chain.inc(dve.tensor_copy(choice[:, k, :], best_at[:, :, k]))
                chain.wait(last)
                dve.wait_ge(consts_in, 48)
                each = numbers[:, 0:E].unsqueeze(1).to_broadcast([P, TILES, E])
                for k in range(TOP):
                    last = chain.inc(dve.tensor_tensor(chosen[:, k], choice[:, k, :].unsqueeze(2).to_broadcast([P, TILES, E]), each, ALU.is_equal))
                chain.wait(last)
                dve.tensor_tensor(both[:], chosen[:, 0], chosen[:, 1], ALU.add).then_inc(both_ready, 1)
                dve.wait_ge(gate_ready, 1)
                chain.link(dve.tensor_scalar(gap[:], gate[:, 1, :], 1.0, None, ALU.add))
                chain.link(dve.reciprocal(gate[:, 0, :], gap[:]))
                chain.link(dve.tensor_tensor(gate[:, 1, :], gate[:, 1, :], gate[:, 0, :], ALU.mult))
                dve.wait_ge(ranks_full, 1)
                chain.link(dve.tensor_copy(in_tile[:], ps_g[1][:, 0:TILES * E].rearrange("p (t e) -> p e t", e=E)))
                for e in range(E):
                    last = chain.inc(dve.tensor_tensor_scan(up_to[:, e, :], ones[:], in_tile[:, e, :], 0.0, ALU.mult, ALU.add))
                chain.wait(last)
                chain.link(dve.tensor_scalar(count_i[:], up_to[:, :, TILES - 1], float(P - 1), None, ALU.add))
                chain.link(dve.tensor_scalar(count_i[:], count_i[:], P.bit_length() - 1, None, ALU.logical_shift_right))
                chain.link(dve.tensor_copy(n_blocks[:], count_i[:]))
                chain.link(dve.tensor_tensor_scan(block_end[:], ones[:, 0:E], n_blocks[:], 0.0, ALU.mult, ALU.add))
                chain.link(dve.tensor_tensor(start[:], block_end[:], n_blocks[:], ALU.subtract))
                chain.link(dve.tensor_scalar(start[:], start[:], float(P), None, ALU.mult))
                chain.link(dve.tensor_tensor(up_to[:], up_to[:], in_tile[:], ALU.subtract))
                chain.link(dve.tensor_tensor(up_to[:], up_to[:], start[:].unsqueeze(2).to_broadcast([P, E, TILES]), ALU.add))
                chain.link(dve.tensor_tensor(place[:], ps_g[0][:, 0:TILES * E].rearrange("p (t e) -> p t e", e=E),
                                             up_to[:].rearrange("p e t -> p t e"), ALU.add))
                for k in range(TOP):
                    last = chain.inc(dve.tensor_tensor(chosen[:, k], chosen[:, k], place[:], ALU.mult))
                chain.wait(last)
                for k in range(TOP):
                    last = chain.inc(dve.tensor_reduce(pos[:, k, :], chosen[:, k], AX.X, ALU.add))
                chain.wait(last)
                chain.link(dve.tensor_copy(pos_i[:], pos[:]))
                chain.inc(dve.tensor_scalar(part_i[:, 0], pos_i[:], P.bit_length() - 1, None, ALU.logical_shift_right))
                chain.link(dve.tensor_scalar(part_i[:, 1], pos_i[:], P - 1, None, ALU.bitwise_and))
                chain.link(dve.tensor_copy(block_row[:], part_i[:]))
                chain.link(dve.tensor_tensor(ge[:], numbers[0:1, 0:BLOCKS].unsqueeze(2).to_broadcast([1, BLOCKS, E]),
                                             block_end[0:1, :].unsqueeze(1).to_broadcast([1, BLOCKS, E]), ALU.is_ge))
                chain.link(dve.tensor_reduce(expert[:], ge[:], AX.X, ALU.add))
                chain.link(dve.tensor_scalar(expert_i[:], expert[:], float(E - 1), None, ALU.min))
                dve.wait_ge(token_ready, 1)
                for n in range(PAIRS):
                    k, t, s = n // TILES, n % TILES, n % 4
                    if n >= 4:
                        dve.wait_ge(onehots_used, n - 3)
                    dve.tensor_scalar(is_row[:, s, :], numbers[:], block_row[:, 1, k, t:t + 1], None, ALU.is_equal)
                    at = block_row[:, 0, k, t:t + 1]
                    dve.tensor_scalar(in_block[:, s, 0, :], numbers[:, 0:BLOCKS], at, token[:, t:t + 1], ALU.is_equal, ALU.mult)
                    dve.tensor_scalar(in_block[:, s, 1, :], numbers[:, 0:BLOCKS], at, gate[:, k, t:t + 1], ALU.is_equal, ALU.mult) \
                       .then_inc(onehots, 1)
                dve.wait_ge(onehots_used, PAIRS)
                chain.inc(dve.tensor_scalar(ids[:], ps_y[0][:, 0:BLOCKS], float(NOBODY), None, ALU.add))
                chain.link(dve.tensor_copy(gates[:], ps_y[0][:, BLOCKS:2 * BLOCKS]))
                dve.sem_inc(plan_ready, 1)

                def body(i, par, prev, nxt, nxt2):
                    if prev:
                        dve.wait_ge(hT_full, done(i - 1))
                        dve.wait_ge(y_full, done(i - 3))
                        dve.tensor_copy(hiddenT[:, 1 - par], ps_hT[:, 0:FC * P].rearrange("p (c q) -> p c q", c=FC)) \
                           .then_inc(hT_ready, 1)
                    if nxt is not None:
                        dve.wait_ge(silu_ready, done(i))
                        dve.wait_ge(u_full, done(i))
                        dve.wait_ge(hT_full, done(i - 2))
                        dve.tensor_tensor(hidden[:, par, 0:F], silu[:, par, :], ps_u[par][:, 0:F], ALU.mult).then_inc(hidden_ready, 1)
                    if prev:
                        dve.wait_ge(y_full, done(i - 1))
                        if not isinstance(i, int) or i >= 3:
                            dve.wait_ge(scattered, 16 * (i - 2))
                        dve.tensor_scalar(yb[:, 1 - par, :], ps_y[1 - par][:], gates[:, bass.ds(i - 1, 1)], None, ALU.mult) \
                           .then_inc(y_ready, 1)

                blocks(dve, body)


def build(nc, x, ctx_in, w_qkv, w_out, decay_rows, enc, wq, bq, wk, bk, wv, bv, wm, bm, router_t, w1_t, w2_t,
          ident, head_sum, head_spread, before, numbers, out):
    x1 = nc.dram_tensor("x1", (B, T, HID), FP32, kind="Internal").ap()
    xn2 = nc.dram_tensor("xn2", (B, T, HID), FP32, kind="Internal").ap()
    with nc.sbuf_tensor("logits", [P, TILES, E], FP32) as logits:
        build_stage_a(nc, x, w_qkv, w_out, decay_rows, ident, head_sum, head_spread, x1)
        build_stage_b(nc, x1, ctx_in, wq, wk, wv, wm, bq, bk, bv, bm, enc, router_t, ident, out, xn2, logits)
        build_stage_c(nc, xn2.rearrange("b t n -> (b t) n"), logits, w1_t, w2_t, ident, before, numbers,
                      out.rearrange("b t n -> (b t) n"))


def kernel(**inputs):
    import numpy as _np
    import concourse.bacc as _bacc
    from concourse import mybir as _mybir
    from concourse.bass_utils import run_bass_kernel_spmd as _run

    a = {k: _np.asarray(v) for k, v in inputs.items()}

    def head_major(w):
        return w.reshape(HD, H, -1).transpose(2, 1, 0).reshape(-1, HD * H)

    head_sum = (_np.arange(HC)[:, None] * 4 + _np.arange(P) // 32)[:, :, None] == _np.arange(H)
    head_sum = head_sum.transpose(1, 0, 2).astype(_np.float32)
    arrays = {
        "x": a["x"], "ctx": a["ctx_2048"], "w_qkv": a["L0_attn_w_qkv"], "w_out": a["L0_attn_w_out"],
        "decay": _np.repeat(a["L0_attn_decay_param"], HID // H).reshape(HC, P).T,
        "enc": a["L0_xattn_encoding"].reshape(2, HID, HD),
        "wq": head_major(a["L0_xattn_Wq"]), "bq": head_major(a["L0_xattn_bq"]),
        "wk": head_major(a["L0_xattn_Wk"]), "bk": head_major(a["L0_xattn_bk"]),
        "wv": head_major(a["L0_xattn_Wv"]), "bv": head_major(a["L0_xattn_bv"]),
        "wm": a["L0_xattn_Wm"].reshape(-1, HD, H).transpose(2, 1, 0).reshape(HD * H, -1),
        "bm": a["L0_xattn_bm"].reshape(TT, P).T,
        "router": a["L0_ffn_router_w"].T,
        "w1": a["L0_ffn_w1"].transpose(0, 2, 1), "w2": a["L0_ffn_w2"].transpose(0, 2, 1),
        "ident": _np.eye(P, dtype=_np.float32), "head_sum": head_sum, "head_spread": head_sum.transpose(2, 1, 0),
        "before": _np.stack([_np.triu(_np.ones((P, P), _np.float32), 1), _np.ones((P, P), _np.float32)], 1),
        "numbers": _np.tile(_np.arange(P, dtype=_np.float32), (P, 1)),
    }
    arrays = {k: _np.ascontiguousarray(v) for k, v in arrays.items()}
    nc = _bacc.Bacc("TRN2", target_bir_lowering=False, num_devices=1)
    args = [nc.dram_tensor(k, v.shape, _mybir.dt.from_np(v.dtype), kind="ExternalInput").ap() for k, v in arrays.items()]
    out = nc.dram_tensor("out", (B, T, HID), FP32, kind="ExternalOutput").ap()
    build(nc, *args, out)
    r = _run(nc, [arrays], core_ids=[0])
    return r.results[0]["out"]
```

```python
import concourse.bass as bass
from concourse import mybir
from contextlib import ExitStack

FP32 = mybir.dt.float32
FP32R = mybir.dt.float32r
BF16 = mybir.dt.bfloat16
I32 = mybir.dt.int32
U32 = mybir.dt.uint32
ALU = mybir.AluOpType
ACT = mybir.ActivationFunctionType
AX = mybir.AxisListType

P = 128
B, T, HID = 16, 256, 512
TT = T // P
HC = HID // P
H = 16
LN_EPS = 1e-05
DEN_EPS = 1e-06


class Count:

    def __init__(self, engine, sem):
        self.engine, self.sem, self.base, self.n = engine, sem, 0, 0

    def inc(self, instruction):
        instruction.then_inc(self.sem, 1)
        self.n += 1
        return self.base + self.n

    def wait(self, value):
        self.engine.wait_ge(self.sem, value)

    def link(self, instruction):
        self.wait(self.inc(instruction))


def layer_norm_stats(dve, count, x, stats, mean_var):
    last = None
    for t in range(x.shape[1]):
        last = dve.bn_stats(stats[:, t, :], x[:, t, :])
    count.link(last)
    dve.sem_inc(count.sem, 1)
    count.n += 1
    for t in range(x.shape[1]):
        last = dve.bn_aggr(mean_var[:, t, :], stats[:, t, :])
    return last


def build_stage_a(nc, x, w_qkv, w_out, decay_rows, ident_in, head_sum_in, head_spread_in, x1, xn1):
    with ExitStack() as ctx:
        def sb(name, shape, dt=FP32):
            return ctx.enter_context(nc.sbuf_tensor("a_" + name, shape, dt))

        def pb(name, shape=(P, 512), dt=FP32):
            return ctx.enter_context(nc.psum_tensor("a_" + name, list(shape), dt))

        def sem(name):
            return ctx.enter_context(nc.semaphore("a_" + name))

        weights = sb("weights", [P, HC, 4 * HID])
        w_hi = sb("w_hi", [P, HC, 4 * HID], FP32R)
        w_lo = sb("w_lo", [P, HC, 4 * HID], FP32R)
        ident = sb("ident", [P, P])
        head_sum = sb("head_sum", [P, HC, H])
        head_spread = sb("head_spread", [H, HC, P])
        decay_p = sb("decay_p", [P, HC])
        decay_1 = sb("decay_1", [P, HC])
        decay_2 = sb("decay_2", [P, HC])
        decay = sb("decay", [P, HC, T])
        half = sb("half", [P, TT])
        x_in = sb("x_in", [P, TT, HID])
        x_res = sb("x_res", [P, TT, HID])
        stats = sb("stats", [P, TT, 6])
        mean_var = sb("mean_var", [P, TT, 2])
        var_eps = sb("var_eps", [P, TT])
        rstd = sb("rstd", [P, TT])
        xn = sb("xn", [P, TT, HID])
        xT_hi = sb("xT_hi", [P, 2, HC, T], FP32R)
        xT_lo = sb("xT_lo", [P, 2, HC, T], FP32R)
        e_qk = sb("e_qk", [P, 2, 2, T])
        phi = sb("phi", [P, 2, 2, T])
        kv = sb("kv", [P, T])
        run_kv = sb("run_kv", [P, T])
        run_k = sb("run_k", [P, T])
        q_sum = sb("q_sum", [P, 2, HC, T])
        q_kv = sb("q_kv", [P, 2, HC, T])
        o_hi = sb("o_hi", [P, HC, T], FP32R)
        o_lo = sb("o_lo", [P, HC, T], FP32R)
        den = sb("den", [H, T])
        rden = sb("rden", [H, T])
        x1_sb = sb("x1_sb", [P, TT, HID])
        stats1 = sb("stats1", [P, TT, 6])
        mean_var1 = sb("mean_var1", [P, TT, 2])
        var_eps1 = sb("var_eps1", [P, TT])
        rstd1 = sb("rstd1", [P, TT])
        xn1_sb = sb("xn1_sb", [P, TT, HID])

        ps_qk = [pb(f"ps_qk{i}") for i in range(2)]
        ps_v = [pb(f"ps_v{i}") for i in range(2)]
        ps_t = [pb(f"ps_t{i}") for i in range(2)]
        ps_w = [pb(f"ps_w{i}") for i in range(2)]

        consts_in = sem("consts_in")
        x_loaded = sem("x_loaded")
        res_loaded = sem("res_loaded")
        x_free = sem("x_free")
        res_free = sem("res_free")
        stored = sem("stored")
        var1_ready, rstd1_ready, xn1_ready = sem("var1_ready"), sem("rstd1_ready"), sem("xn1_ready")
        var_ready = sem("var_ready")
        rstd_ready = sem("rstd_ready")
        xn_ready = sem("xn_ready")
        xt_full = sem("xt_full")
        xt_rounded = sem("xt_rounded")
        xt_ready = sem("xt_ready")
        w_in = [sem(f"w_in{k}") for k in range(HC)]
        w_rounded = sem("w_rounded")
        w_split = sem("w_split")
        qk_full, v_full = sem("qk_full"), sem("v_full")
        qkv_free = sem("qkv_free")
        exp_ready = sem("exp_ready")
        prod_ready = sem("prod_ready")
        den_full = sem("den_full")
        rden_ready = sem("rden_ready")
        spread_full = sem("spread_full")
        o_rounded = sem("o_rounded")
        o_ready = sem("o_ready")
        out_full = sem("out_full")
        w_free = sem("w_free")
        x1_ready = sem("x1_ready")
        s_dve = sem("dve")

        W_LO_BY_POOL = (HC - 1,)

        def split_weights(engine, k):
            engine.wait_ge(w_rounded, k + 1)
            engine.tensor_tensor(w_lo[:, k, :], weights[:, k, :], w_hi[:, k, :], ALU.subtract).then_inc(w_split, 1)

        def per_iteration(engine, body):
            body(0, 0, False, True)
            with engine.Fori(0, (B - 2) // 2) as i:
                body(i * 2 + 1, 1, True, True)
                body(i * 2 + 2, 0, True, True)
            body(B - 1, 1, True, False)
            body(B, 0, True, None)

        with nc.Block() as block:
            @block.sync
            def _(sp):
                sp.dma_start(x_in[:], x[0].rearrange("(t p) n -> p t n", p=P)).then_inc(x_loaded, 16)
                sp.dma_start(ident[:], ident_in).then_inc(consts_in, 16)
                sp.dma_start(decay_p[:], decay_rows).then_inc(consts_in, 16)
                for k in range(HC):
                    sp.dma_start(weights[:, k, 0:3 * HID], w_qkv[k * P:(k + 1) * P, :]).then_inc(w_in[k], 16)
                    sp.dma_start(weights[:, k, 3 * HID:], w_out[k * P:(k + 1) * P, :]).then_inc(w_in[k], 16)
                sp.dma_start(head_sum[:], head_sum_in).then_inc(consts_in, 16)
                sp.dma_start(head_spread[:], head_spread_in).then_inc(consts_in, 16)

                def body(b, par, prev, nxt):
                    if nxt:
                        sp.wait_ge(x_free, b + 2)
                        sp.dma_start(x_in[:], x[bass.ds(b + 1, 1)].rearrange("a (t p) n -> p (a t) n", p=P)) \
                          .then_inc(x_loaded, 16)
                    if prev:
                        sp.wait_ge(res_free, b)
                        sp.dma_start(x_res[:], x[bass.ds(b - 1, 1)].rearrange("a (t p) n -> p (a t) n", p=P)) \
                          .then_inc(res_loaded, 16)
                        sp.wait_ge(x1_ready, b)
                        sp.dma_start(x1[bass.ds(b - 1, 1)].rearrange("a (t p) n -> p (a t) n", p=P), x1_sb[:]) \
                          .then_inc(stored, 16)
                        sp.wait_ge(xn1_ready, b)
                        sp.dma_start(xn1[bass.ds(b - 1, 1)].rearrange("a (t p) n -> p (a t) n", p=P), xn1_sb[:]) \
                          .then_inc(stored, 16)

                per_iteration(sp, body)
                sp.wait_ge(stored, 32 * B + 32)

            @block.gpsimd
            def _(pool):
                pool.memset(half[:], -0.5).then_inc(rstd_ready, 1)
                pool.wait_ge(rstd_ready, 1)

                def rstd_of(b):
                    pool.wait_ge(var_ready, b + 1)
                    pool.tensor_tensor(rstd[:], var_eps[:], half[:], ALU.pow).then_inc(rstd_ready, 1)

                def body(b, par, prev, nxt):
                    if nxt:
                        rstd_of(b + 1)
                    if prev:
                        pool.wait_ge(var1_ready, b)
                        pool.tensor_tensor(rstd1[:], var_eps1[:], half[:], ALU.pow).then_inc(rstd1_ready, 1)

                rstd_of(0)
                for k in W_LO_BY_POOL:
                    split_weights(pool, k)
                per_iteration(pool, body)

            @block.tensor
            def _(pe):
                def transposes(b):
                    pe.wait_ge(xn_ready, b + 1)
                    for t in range(TT):
                        pe.wait_ge(xt_ready, 2 * b + t + 1)
                        for c in range(HC):
                            last = pe.transpose(ps_t[t][:, c * P:(c + 1) * P], xn[:, t, c * P:(c + 1) * P], ident[:])
                        last.then_inc(xt_full, 1)

                def qkv(b, par, c):
                    pe.wait_ge(qkv_free, 4 * b + c + 1)
                    for role, out in ((0, ps_qk[c % 2][:, 0:T]), (1, ps_qk[c % 2][:, T:2 * T]), (2, ps_v[c % 2][:, 0:T])):
                        features = slice(role * HID + c * P, role * HID + (c + 1) * P)
                        for k in range(HC):
                            w, x = w_hi[:, k, features], xT_hi[:, par, k, :]
                            pe.matmul(out, w, x, start=(k == 0), stop=False)
                            pe.matmul(out, w, xT_lo[:, par, k, :], start=False, stop=False)
                            last = pe.matmul(out, w_lo[:, k, features], x, start=False, stop=(k == HC - 1))
                        if role:
                            last.then_inc(qk_full if role == 1 else v_full, 1)

                def denominators(b, par):
                    pe.wait_ge(prod_ready, 4 * b + 4)
                    pe.wait_ge(w_free, 5 * b + 1)
                    for c in range(HC):
                        last = pe.matmul(ps_w[0][0:H, 0:T], head_sum[:, c, :], q_sum[:, par, c, :],
                                         start=(c == 0), stop=(c == HC - 1))
                    last.then_inc(den_full, 1)

                def spread(b):
                    pe.wait_ge(rden_ready, b + 1)
                    for g in range(2):
                        pe.wait_ge(w_free, 5 * b + 1 + g)
                        for k in range(2):
                            last = pe.matmul(ps_w[1 - g][:, k * T:(k + 1) * T], head_spread[:, 2 * g + k, :], rden[:],
                                             start=True, stop=True)
                        last.then_inc(spread_full, 1)

                def project(b):
                    pe.wait_ge(o_ready, 2 * b + 2)
                    for t in range(TT):
                        pe.wait_ge(w_free, 5 * b + 3 + t)
                        for c in range(HC):
                            times = slice(t * P, (t + 1) * P)
                            o, w = o_hi[:, c, times], w_hi[:, c, 3 * HID:]
                            pe.matmul(ps_w[1 - t][:, :], o, w, start=(c == 0), stop=False)
                            pe.matmul(ps_w[1 - t][:, :], o, w_lo[:, c, 3 * HID:], start=False, stop=False)
                            last = pe.matmul(ps_w[1 - t][:, :], o_lo[:, c, times], w, start=False, stop=(c == HC - 1))
                        last.then_inc(out_full, 1)

                def body(b, par, prev, nxt):
                    for c in range(HC):
                        if nxt is not None:
                            if c == 0:
                                pe.wait_ge(xt_ready, 2 * b + 4)
                            qkv(b, par, c)
                        if prev and c == 0:
                            denominators(b - 1, 1 - par)
                        if prev and c == 1:
                            spread(b - 1)
                        if nxt and c == 2:
                            transposes(b + 1)
                        if prev and c == 3:
                            project(b - 1)

                pe.wait_ge(consts_in, 64)
                transposes(0)
                pe.wait_ge(w_rounded, HC)
                pe.wait_ge(w_split, HC)
                per_iteration(pe, body)

            @block.scalar
            def _(act):
                act.wait_ge(consts_in, 64)
                act.activation(decay_1[:], decay_p[:], ACT.Exp, scale=-1.0).then_inc(exp_ready, 1)

                def keep_xT(b, par):
                    for t in range(TT):
                        act.wait_ge(xt_full, 2 * b + t + 1)
                        act.copy(xT_hi[:, par, :, t * P:(t + 1) * P],
                                 ps_t[t][:].rearrange("p (c q) -> p c q", c=HC)).then_inc(xt_rounded, 1)

                def round_o(b, par):
                    for g in range(2):
                        act.wait_ge(w_free, 5 * b + 3 + g)
                        act.copy(o_hi[:, 2 * g:2 * g + 2, :], q_kv[:, par, 2 * g:2 * g + 2, :]).then_inc(o_rounded, 1)

                def body(b, par, prev, nxt):
                    for c in range(HC):
                        if nxt is not None:
                            act.wait_ge(qk_full, 4 * b + c + 1)
                            act.activation(e_qk[:, c % 2], ps_qk[c % 2][:].rearrange("p (r t) -> p r t", r=2), ACT.Exp) \
                               .then_inc(exp_ready, 1)
                        if prev and c == 1:
                            round_o(b - 1, 1 - par)
                        if nxt and c == 2:
                            keep_xT(b + 1, 1 - par)

                for k in range(HC):
                    if k == 1:
                        keep_xT(0, 0)
                    act.wait_ge(w_in[k], 32)
                    act.copy(w_hi[:, k, :], weights[:, k, :]).then_inc(w_rounded, 1)
                per_iteration(act, body)

            @block.vector
            def _(dve):
                chain = Count(dve, s_dve)
                chain.link(dve.memset(decay[:], 1.0))
                for s, n in ((x_free, 1), (res_free, 1), (xt_ready, 2), (qkv_free, 2), (w_free, 1), (stored, 32)):
                    dve.sem_inc(s, n)

                def norm_stats(b):
                    dve.wait_ge(x_loaded, 16 * b + 16)
                    chain.link(layer_norm_stats(dve, chain, x_in, stats, mean_var))
                    dve.tensor_scalar(var_eps[:], mean_var[:, :, 1], LN_EPS, None, ALU.add).then_inc(var_ready, 1)

                def norm_apply(b):
                    dve.wait_ge(rstd_ready, b + 2)
                    for t in range(TT):
                        last = dve.tensor_scalar(xn[:, t, :], x_in[:, t, :], mean_var[:, t, 0:1], rstd[:, t:t + 1],
                                                 ALU.subtract, ALU.mult)
                        if t < TT - 1:
                            continue
                        last.then_inc(xn_ready, 1)
                    dve.wait_ge(xn_ready, b + 1)
                    dve.sem_inc(x_free, 1)

                def scans(b, par, c):
                    dve.wait_ge(exp_ready, 4 * b + c + 2)
                    e, f = e_qk[:, c % 2], phi[:, c % 2]
                    chain.link(dve.tensor_scalar(e, e, 1.0, None, ALU.min))
                    chain.link(dve.scalar_tensor_tensor(f, ps_qk[c % 2][:].rearrange("p (r t) -> p r t", r=2), 0.0, e,
                                                        ALU.max, ALU.add))
                    dve.wait_ge(v_full, 4 * b + c + 1)
                    dve.tensor_tensor(kv[:], f[:, 1, :], ps_v[c % 2][:, 0:T], ALU.mult).then_inc(qkv_free, 1)
                    summed = chain.inc(dve.tensor_tensor_scan(run_k[:], decay[:, c, :], f[:, 1, :], 0.0, ALU.mult, ALU.add))
                    dve.wait_ge(qkv_free, 4 * b + c + 3)
                    kv_summed = chain.inc(dve.tensor_tensor_scan(run_kv[:], decay[:, c, :], kv[:], 0.0, ALU.mult, ALU.add))
                    chain.wait(summed)
                    dve.tensor_tensor(q_sum[:, par, c, :], f[:, 0, :], run_k[:], ALU.mult)
                    chain.wait(kv_summed)
                    dve.tensor_tensor(q_kv[:, par, c, :], f[:, 0, :], run_kv[:], ALU.mult).then_inc(prod_ready, 1)

                def reciprocals(b):
                    dve.wait_ge(den_full, b + 1)
                    dve.tensor_scalar(den[:], ps_w[0][0:H, 0:T], DEN_EPS, None, ALU.max).then_inc(w_free, 1)
                    dve.wait_ge(w_free, 5 * b + 2)
                    dve.reciprocal(rden[:], den[:]).then_inc(rden_ready, 1)

                def divide(b, par):
                    dve.wait_ge(prod_ready, 4 * b + 4)
                    for g in range(2):
                        dve.wait_ge(spread_full, 2 * b + g + 1)
                        o = q_kv[:, par, 2 * g:2 * g + 2, :]
                        dve.tensor_tensor(o, o, ps_w[1 - g][:].rearrange("p (c t) -> p c t", c=2), ALU.mult) \
                           .then_inc(w_free, 1)

                def split_o(b, par):
                    for g in range(2):
                        dve.wait_ge(o_rounded, 2 * b + g + 1)
                        chunks = slice(2 * g, 2 * g + 2)
                        dve.tensor_tensor(o_lo[:, chunks, :], q_kv[:, par, chunks, :], o_hi[:, chunks, :], ALU.subtract) \
                           .then_inc(o_ready, 1)

                def split_xT(b, par):
                    for t in range(TT):
                        dve.wait_ge(xt_rounded, 2 * b + t + 1)
                        times = slice(t * P, (t + 1) * P)
                        dve.tensor_tensor(xT_lo[:, par, :, times], ps_t[t][:].rearrange("p (c q) -> p c q", c=HC),
                                          xT_hi[:, par, :, times], ALU.subtract).then_inc(xt_ready, 1)

                def residual(b):
                    dve.wait_ge(res_loaded, 16 * b + 16)
                    dve.wait_ge(stored, 32 * b + 32)
                    for t in range(TT):
                        dve.wait_ge(out_full, 2 * b + t + 1)
                        dve.tensor_tensor(x1_sb[:, t, :], ps_w[1 - t][:], x_res[:, t, :], ALU.add).then_inc(w_free, 1)
                    dve.wait_ge(w_free, 5 * b + 6)
                    dve.sem_inc(x1_ready, 1)
                    dve.sem_inc(res_free, 1)
                    chain.link(layer_norm_stats(dve, chain, x1_sb, stats1, mean_var1))
                    dve.tensor_scalar(var_eps1[:], mean_var1[:, :, 1], LN_EPS, None, ALU.add).then_inc(var1_ready, 1)
                    dve.wait_ge(rstd1_ready, b + 1)
                    for t in range(TT):
                        last = dve.tensor_scalar(xn1_sb[:, t, :], x1_sb[:, t, :], mean_var1[:, t, 0:1], rstd1[:, t:t + 1],
                                                 ALU.subtract, ALU.mult)
                    last.then_inc(xn1_ready, 1)

                def body(b, par, prev, nxt):
                    first = chain.n
                    if nxt is not None:
                        scans(b, par, 0)
                    if prev:
                        reciprocals(b - 1)
                    if nxt:
                        norm_stats(b + 1)
                    if nxt is not None:
                        scans(b, par, 1)
                    if nxt:
                        norm_apply(b + 1)
                    if prev:
                        divide(b - 1, 1 - par)
                    if nxt is not None:
                        scans(b, par, 2)
                    if prev:
                        split_o(b - 1, 1 - par)
                    if nxt:
                        split_xT(b + 1, 1 - par)
                    if nxt is not None:
                        scans(b, par, 3)
                    if prev:
                        residual(b - 1)
                    return chain.n - first

                norm_stats(0)
                norm_apply(0)
                for k in range(HC):
                    if k == 1:
                        split_xT(0, 0)
                    if k not in W_LO_BY_POOL:
                        split_weights(dve, k)
                dve.wait_ge(exp_ready, 1)
                chain.link(dve.tensor_scalar(decay_2[:], decay_1[:], 1.0, None, ALU.add))
                chain.link(dve.reciprocal(decay_1[:], decay_2[:]))
                for c in range(HC):
                    last = chain.inc(dve.tensor_scalar(decay[:, c, :], decay[:, c, :], decay_1[:, c:c + 1], None, ALU.mult))
                chain.wait(last)
                turn = 4 * 4 + 2 * 3
                body(0, 0, False, True)
                before = chain.n
                with dve.Fori(0, (B - 2) // 2) as i:
                    chain.base = i * (2 * turn)
                    assert body(i * 2 + 1, 1, True, True) == turn
                    assert body(i * 2 + 2, 0, True, True) == turn
                chain.base = 0
                chain.n = before + (B - 2) * turn
                body(B - 1, 1, True, False)
                body(B, 0, True, None)


HD = 16
N = HID
NJ = N // P
VH = 2 * HD + 1
RING = 4
LAG = 2
Q_PARTS = (0, 1, 2, 0, 1, 0)
K_PARTS = (0, 0, 0, 1, 1, 2)
ROWS = len(Q_PARTS) * HD
MAX_ROWS = 3


def build_stage_b(nc, x1, xn1, ctx_in, wq, wk, wv, wm, bq_rows, bk_rows, bv_rows, bm_cols, enc, router_t, ident_in,
                  x2, xn2, logits):
    with ExitStack() as ctx:
        def sb(name, shape, dt=FP32):
            return ctx.enter_context(nc.sbuf_tensor("b_" + name, shape, dt))

        def pb(name, shape=(P, 512), dt=FP32):
            return ctx.enter_context(nc.psum_tensor("b_" + name, list(shape), dt))

        def sem(name):
            return ctx.enter_context(nc.semaphore("b_" + name))

        def dram(name, shape, dt=FP32):
            return nc.dram_tensor("b_" + name, shape, dt, kind="Internal").ap()

        MH = H // 2 * NJ
        w_q, w_k, w_v, w_m = (sb(n, [P, TT, T]) for n in ("w_q", "w_k", "w_v", "w_m"))
        bias_qk = sb("bias_qk", [P, 2 * T])
        bias_v = sb("bias_v", [P, T])
        bias_m = sb("bias_m", [P, TT])
        cos_f = sb("cos_f", [P, NJ, HD])
        sin_f = sb("sin_f", [P, NJ, HD])
        w_router = sb("w_router", [P, HC, 8])
        ident = sb("ident", [P, P])
        half = sb("half", [P, TT])
        xn = sb("xn", [P, TT, HID])
        ctx_sb = sb("ctx_sb", [P, TT, HID])
        stats2 = sb("stats2", [P, TT, 6])
        mean_var2 = sb("mean_var2", [P, TT, 2])
        var_eps2 = sb("var_eps2", [P, TT])
        rstd2 = sb("rstd2", [P, TT])
        qk_b = sb("qk_b", [P, 2 * T])
        rot = sb("rot", [P, 2, 2 * T])
        qk_rot = sb("qk_rot", [P, NJ, 2 * T])
        parts = sb("parts", [P, 4, 3, N], BF16)
        q_stack = sb("q_stack", [ROWS + MAX_ROWS, 2, H, N], BF16)
        k_stack = sb("k_stack", [ROWS + MAX_ROWS, 2, H, N], BF16)
        v_sb = sb("v_sb", [P, 2, NJ, H, VH], FP32R)
        v_full = qk_b[:].rearrange("p (j h d) -> p j h d", j=2, d=HD)
        row_max = sb("row_max", [P, 2, P])
        neg_rest = sb("neg_rest", [MH, P])
        neg_parts = sb("neg_parts", [MH, MAX_ROWS, P], BF16)
        probs = sb("probs", [P, RING, 2, N])
        probs_hi = sb("probs_hi", [P, RING, 2, N], FP32R)
        probs_lo = sb("probs_lo", [P, RING, 2, N], FP32R)
        o_sb = sb("o_sb", [VH, 2, 4, N])
        sums = sb("sums", [P, H * N // P])
        rsums = sb("rsums", [P, H * N // P])
        o_cat = sb("o_cat", [P, TT, N])
        x2_sb = sb("x2_sb", [P, TT, HID])
        r_cat = x2_sb
        xn2_sb = sb("xn2_sb", [P, TT, HID])
        x_res = xn2_sb
        xn2_T = rot[:].rearrange("p t (c q) -> p t c q", c=HC)

        parts_dram = dram("parts_dram", (2, 2, 3, P, N), BF16)
        neg_dram = dram("neg_dram", (MAX_ROWS, H * N), BF16)
        o_dram = dram("o_dram", (H, HD, N))
        o_lo_dram = dram("o_lo_dram", (H, HD, N))
        sum_dram = dram("sum_dram", (H, N))
        rsum_dram = dram("rsum_dram", (H, N))
        rsum16_dram = dram("rsum16_dram", (H, HD, N))

        ps_s = [pb(f"ps_s{i}", (P, 2 * N)) for i in range(2)]
        ps_o = [pb(f"ps_o{i}") for i in range(2)]
        ps_w = [pb(f"ps_w{i}") for i in range(2)]

        consts_in = sem("consts_in")
        xn_loaded, ctx_loaded, res_loaded = sem("xn_loaded"), sem("ctx_loaded"), sem("res_loaded")
        inputs_free = sem("inputs_free")
        half_ready = sem("half_ready")
        var2_ready, rstd2_ready = sem("var2_ready"), sem("rstd2_ready")
        w_full = sem("w_full")
        w_free = sem("w_free")
        rot_ready = sem("rot_ready")
        parts_ready = sem("parts_ready")
        parts_stored = [sem(f"parts_stored{i}") for i in range(2)]
        stacks_in = [sem(f"stacks_in{i}") for i in range(2)]
        v_ready = sem("v_ready")
        max_ready = sem("max_ready")
        neg_ready, neg_stored = sem("neg_ready"), sem("neg_stored")
        neg_in = [sem(f"neg_in{i}") for i in range(2)]
        s_full = sem("s_full")
        e_ready = sem("e_ready")
        hi_ready = sem("hi_ready")
        lo_ready = sem("lo_ready")
        pv_done = sem("pv_done")
        o_kept = sem("o_kept")
        o_stored = [sem(f"o_stored{i}") for i in range(2)]
        o_loaded, o_added, sums_loaded = sem("o_loaded"), sem("o_added"), sem("sums_loaded")
        rsums_ready, rsums_moved, r_loaded = sem("rsums_ready"), sem("rsums_moved"), sem("r_loaded")
        o_ready = sem("o_ready")
        o_used = sem("o_used")
        x2_ready, xn2_ready = sem("x2_ready"), sem("xn2_ready")
        x2_stored = sem("x2_stored")
        xn2T_ready = sem("xn2T_ready")
        s_dve = sem("dve")
        passed, pool_passed = sem("passed"), sem("pool_passed")

        def maxima_of(first, end):
            return tuple(("max", k) for k in range(first, end))

        STEPS = {
            0: (("qk", 0), ("qk", 1)), 1: (("qk", 2), ("qk", 3)), 2: (("split", 0), ("split", 1)),
            3: (("split", 2), ("split", 3)), 4: (("v", 0),), 5: (("v", 1),) + maxima_of(0, 4), 6: maxima_of(4, 12),
            7: (("merge", 0), ("merge", 1)) + maxima_of(12, 17), 8: maxima_of(17, 25),
            9: (("norm2", 0),) + maxima_of(25, 30), 10: maxima_of(30, 34),
            11: (("neg", 0), ("turn2", 0), ("turn2", 1)) + maxima_of(34, 39),
            12: (("route", 0),) + maxima_of(39, 45), 13: maxima_of(45, 49), 14: maxima_of(49, 57), 15: maxima_of(57, 64) + (("neg", 1),),
        }
        FOR_PREVIOUS = ("merge", "norm2", "turn2", "route")
        PRE_USES = 4 + 4 + 2 + NJ * H + 2
        POST_USES = 2 + 2 + 1

        def steps_beside(h, prev, nxt):
            if h not in STEPS:
                return []
            return [(name, k) for name, k in STEPS[h] if (prev if name in FOR_PREVIOUS else nxt)]

        def head_before(b, par, h):
            return (b, par, h - LAG) if h >= LAG else (b - 1, 1 - par, h - LAG + H)

        def interleaved(main, beside):
            order, done = [], 0
            for n, item in enumerate(main):
                order.append(item)
                upto = (n + 1) * len(beside) // len(main)
                order += beside[done:upto]
                done = upto
            return order + beside[done:]

        def batches(engine, body, count=None, turn=0):
            body(0, 0, False, True)
            before = count.n if count else 0
            with engine.Fori(0, (B - 2) // 2) as i:
                for k in range(2):
                    if count:
                        count.base = i * (2 * turn)
                    body(i * 2 + 1 + k, 1 - k, True, True)
                    if count:
                        assert count.n - before == (k + 1) * turn, (count.n - before, turn)
            if count:
                count.base, count.n = 0, before + (B - 2) * turn
            body(B - 1, 1, True, False)
            body(B, 0, True, None)

        def rows(ap, b):
            return ap[bass.ds(b, 1)].rearrange("a (t p) n -> p (a t) n", p=P)

        with nc.Block() as block:
            @block.sync
            def _(sp):
                def wait(s, value):
                    sp.wait_ge(s, value)
                    sp.sem_inc(passed, 1)

                def load_inputs(b):
                    if not isinstance(b, int) or b >= 1:
                        wait(inputs_free, b)
                    sp.dma_start(xn[:], rows(xn1, b)).then_inc(xn_loaded, 16)
                    sp.dma_start(ctx_sb[:], rows(ctx_in, b)).then_inc(ctx_loaded, 16)

                def parts_out(b, half, side):
                    n = 2 * half + side
                    wait(parts_ready, 4 * b + n + 1)
                    sp.dma_start(parts_dram[side, half].rearrange("s p n -> p s n"),
                                 parts[:, n]).then_inc(parts_stored[side], 16)

                def restack(b, par, half, side):
                    wait(parts_stored[side], 32 * b + 16 * half + 16)
                    heads = slice(half * H // 2, (half + 1) * H // 2)
                    stack, order = ((q_stack, Q_PARTS), (k_stack, K_PARTS))[side]
                    for first, end in ((0, 3), (3, 5), (5, 6)):
                        part = order[first]
                        n = end - first
                        channels = parts_dram[side, half].rearrange("s (d h) n -> s d (h n)", d=HD)
                        if side == 0:
                            src = channels[part:part + n]
                        else:
                            src = channels[part:part + 1].to_broadcast([n, HD, H // 2 * N])
                        sp.dma_start(stack[first * HD:end * HD, par, heads, :].rearrange("q h n -> q (h n)"), src) \
                          .then_inc(stacks_in[half], 16)

                def max_rows(b, par, half):
                    heads = slice(half * H // 2, (half + 1) * H // 2)
                    wait(neg_ready, 2 * b + half + 1)
                    sp.dma_start(neg_dram[:, half * MH * P:(half + 1) * MH * P].rearrange("s (r n) -> r s n", n=P),
                                 neg_parts[:]).then_inc(neg_stored, 16)
                    wait(neg_stored, 32 * b + 16 * half + 16)
                    sp.dma_start(q_stack[ROWS:ROWS + MAX_ROWS, par, heads, :],
                                 neg_dram.rearrange("s (h n) -> s h n", h=H)[:, heads]).then_inc(neg_in[half], 16)

                def outputs_in(b):
                    wait(o_stored[0], 96 * b + 96 + 48)
                    wait(o_stored[1], 96 * b + 96 + 48)
                    wait(o_used, b + 1)
                    sp.dma_start(sums[:], sum_dram.rearrange("h (q n) -> (h q) n", n=H * N // P)).then_inc(sums_loaded, 16)
                    sp.dma_start(o_cat[:], o_dram.rearrange("(t h) d n -> (h d) t n", t=TT)).then_inc(o_loaded, 16)
                    if not isinstance(b, int) or b >= 1:
                        wait(xn2T_ready, 2 * b)
                        wait(x2_stored, 32 * b + 32)
                    sp.dma_start(x_res[:], rows(x1, b)).then_inc(res_loaded, 16)

                def rsums_out(b):
                    if not isinstance(b, int) or b >= 1:
                        wait(r_loaded, 16 * b)
                    wait(rsums_ready, b + 1)
                    sp.dma_start(rsum_dram.rearrange("h (q n) -> (h q) n", n=H * N // P), rsums[:]).then_inc(rsums_moved, 16)

                def rsums_spread(b):
                    wait(rsums_moved, 32 * b + 16)
                    sp.dma_start(rsum16_dram, rsum_dram.unsqueeze(1).to_broadcast([H, HD, N])).then_inc(rsums_moved, 16)

                def rsums_in(b):
                    wait(rsums_moved, 32 * b + 32)
                    sp.dma_start(r_cat[:], rsum16_dram.rearrange("(t h) d n -> (h d) t n", t=TT)).then_inc(r_loaded, 16)

                def results_out(b):
                    wait(x2_ready, b + 1)
                    sp.dma_start(rows(x2, b), x2_sb[:]).then_inc(x2_stored, 16)
                    wait(xn2_ready, b + 1)
                    sp.dma_start(rows(xn2, b), xn2_sb[:]).then_inc(x2_stored, 16)

                load_inputs(0)
                for tile, src in ((w_q, wq), (w_k, wk), (w_v, wv), (w_m, wm)):
                    sp.dma_start(tile[:], src.rearrange("(c p) n -> p c n", p=P)).then_inc(consts_in, 16)
                for tile, src in ((bias_qk[:, 0:T], bq_rows), (bias_qk[:, T:2 * T], bk_rows), (bias_v[:], bv_rows)):
                    sp.dma_start(tile, src.to_broadcast([P, T])).then_inc(consts_in, 16)
                sp.dma_start(cos_f[:], enc[0].rearrange("(j p) d -> p j d", p=P)).then_inc(consts_in, 16)
                sp.dma_start(sin_f[:], enc[1].rearrange("(j p) d -> p j d", p=P)).then_inc(consts_in, 16)
                sp.dma_start(w_router[:], router_t.rearrange("(c p) e -> p c e", p=P)).then_inc(consts_in, 16)
                sp.dma_start(ident[:], ident_in).then_inc(consts_in, 16)
                sp.dma_start(bias_m[:], bm_cols).then_inc(consts_in, 16)
                for half in range(2):
                    for side in range(2):
                        parts_out(0, half, side)
                    for side in range(2):
                        restack(0, 0, half, side)

                def body(b, par, has_results, prev, nxt):
                    if nxt:
                        load_inputs(b + 1)
                    if has_results:
                        results_out(b - 2)
                    if nxt is not None:
                        max_rows(b, par, 0)
                        max_rows(b, par, 1)
                    if prev:
                        outputs_in(b - 1)
                    if nxt:
                        parts_out(b + 1, 0, 0)
                        parts_out(b + 1, 0, 1)
                    if prev:
                        rsums_out(b - 1)
                    if nxt:
                        if prev:
                            wait(s_full, b * (2 * H))
                        restack(b + 1, 1 - par, 0, 0)
                        restack(b + 1, 1 - par, 0, 1)
                    if prev:
                        rsums_spread(b - 1)
                    if nxt:
                        parts_out(b + 1, 1, 0)
                        parts_out(b + 1, 1, 1)
                    if prev:
                        rsums_in(b - 1)
                    if nxt:
                        restack(b + 1, 1 - par, 1, 0)
                        restack(b + 1, 1 - par, 1, 1)

                body(0, 0, False, False, True)
                body(1, 1, False, True, True)
                with sp.Fori(0, (B - 4) // 2) as i:
                    body(i * 2 + 2, 0, True, True, True)
                    body(i * 2 + 3, 1, True, True, True)
                body(B - 2, 0, True, True, True)
                body(B - 1, 1, True, True, False)
                body(B, 0, True, True, None)
                results_out(B - 1)
                wait(x2_stored, 32 * B + 32)

            @block.gpsimd
            def _(pool):
                pool.memset(half[:], -0.5).then_inc(half_ready, 1)
                pool.wait_ge(half_ready, 1)

                def wait(s, value):
                    pool.wait_ge(s, value)
                    pool.sem_inc(pool_passed, 1)

                def remainder(b, h, m):
                    pair = 2 * h + m
                    pool.wait_ge(hi_ready, 2 * H * b + pair + 1)
                    at = pair % RING
                    pool.tensor_tensor(probs_lo[:, at], probs[:, at], probs_hi[:, at], ALU.subtract).then_inc(lo_ready, 1)

                def body(b, par, prev, nxt):
                    for h in range(H):
                        if nxt is not None:
                            for m in range(2):
                                remainder(b, h, m)
                        if h == 3 and prev:
                            wait(o_loaded, 16 * b)
                            pool.dma_start(o_cat[:], o_lo_dram.rearrange("(t h) d n -> (h d) t n", t=TT), accum_op=ALU.add) \
                                .then_inc(o_added, 16)
                        if h == 5 and prev:
                            pool.wait_ge(o_added, 16 * b)
                            pool.wait_ge(r_loaded, 16 * b)
                            pool.tensor_tensor(o_cat[:], o_cat[:], r_cat[:], ALU.mult).then_inc(o_ready, 1)
                        if h == 7 and prev:
                            pool.wait_ge(var2_ready, b)
                            pool.tensor_tensor(rstd2[:], var_eps2[:], half[:], ALU.pow).then_inc(rstd2_ready, 1)

                batches(pool, body)

            @block.scalar
            def _(act):
                for s in o_stored:
                    act.sem_inc(s, 48)
                act.sem_inc(e_ready, 2)
                act.sem_inc(o_kept, 2)

                def exps(b, par, h, m):
                    pair = 2 * h + m
                    act.wait_ge(s_full, 2 * H * b + pair + 1)
                    act.wait_ge(pv_done, 2 * H * b + pair + 1)
                    act.activation(probs[:, pair % RING], ps_s[m][:].rearrange("p (m n) -> p m n", m=2),
                                   ACT.Exp, scale=HD ** -0.5).then_inc(e_ready, 1)

                def rounded(b, h, m):
                    pair = 2 * h + m
                    act.wait_ge(e_ready, 2 * H * b + pair + 3)
                    act.copy(probs_hi[:, pair % RING], probs[:, pair % RING]).then_inc(hi_ready, 1)

                def keep(b, h, first):
                    g = h // 4
                    stored = o_stored[g % 2]
                    if h % 4 == 0:
                        act.wait_ge(stored, 96 * b + 48 * (g // 2) + 48)
                    act.wait_ge(pv_done, 2 * H * b + 2 * h + 2 + RING)
                    act.copy(o_sb[:, g % 2, h % 4, :], ps_o[h % 2][0:VH, :]).then_inc(o_kept, 1)
                    if h % 4 == 3:
                        if g == 0 and not first:
                            act.wait_ge(o_added, 16 * b)
                            act.wait_ge(sums_loaded, 16 * b)
                        act.wait_ge(o_kept, H * b + h + 3)
                        heads = slice(4 * g, 4 * g + 4)
                        act.dma_start(o_dram[heads].rearrange("h d n -> d h n"), o_sb[0:HD, g % 2]).then_inc(stored, 16)
                        act.dma_start(sum_dram[heads].unsqueeze(0), o_sb[HD:HD + 1, g % 2]).then_inc(stored, 16)
                        act.dma_start(o_lo_dram[heads].rearrange("h d n -> d h n"), o_sb[HD + 1:VH, g % 2]).then_inc(stored, 16)

                def body(b, par, prev, nxt):
                    for h in range(H):
                        if nxt is not None:
                            for m in range(2):
                                exps(b, par, h, m)
                                rounded(b, h, m)
                        if (prev if h < LAG else nxt is not None):
                            before, _, head = head_before(b, par, h)
                            keep(before, head, not prev)

                batches(act, body)

            @block.tensor
            def _(pe):
                uses = Count(pe, w_full)

                def bank():
                    pe.wait_ge(w_free, uses.base + uses.n + 1)
                    return ps_w[uses.n % 2]

                def project_qk(b, j):
                    w = bank()
                    for side, (src, weight) in enumerate(((xn, w_q), (ctx_sb, w_k))):
                        for c in range(TT):
                            last = pe.matmul(w[:, side * T:(side + 1) * T], src[:, c, j * P:(j + 1) * P], weight[:, c, :],
                                             start=(c == 0), stop=(c == TT - 1))
                    uses.inc(last)

                def project_v(b, i):
                    w = bank()
                    for k in range(2):
                        j = 2 * i + k
                        for c in range(TT):
                            last = pe.matmul(w[:, k * T:(k + 1) * T], ctx_sb[:, c, j * P:(j + 1) * P], w_v[:, c, :],
                                             start=(c == 0), stop=(c == TT - 1))
                    uses.inc(last)

                def transpose_qk(b, t):
                    if t == 0:
                        pe.wait_ge(rot_ready, 4 * b + 4)
                    w = bank()
                    half, side = t // 2, t % 2
                    block = 2 * side + half
                    for j in range(NJ):
                        last = pe.transpose(w[:, j * P:(j + 1) * P], qk_rot[:, j, block * P:(block + 1) * P], ident[:])
                    uses.inc(last)

                def maxima(b, par, h, j):
                    if h % (H // 2) == 0 and j == 0:
                        pe.wait_ge(stacks_in[h // (H // 2)], 96 * b + 96)
                    w = bank()
                    uses.inc(pe.matmul(w[:], q_stack[0:ROWS, par, h, j * P:(j + 1) * P], k_stack[0:ROWS, par, h, :],
                                       start=True, stop=True))

                def transpose_max(b, half):
                    pe.wait_ge(max_ready, 2 * b + half + 1)
                    w = bank()
                    uses.inc(pe.transpose(w[:, 0:P], row_max[:, half, :], ident[:]))

                def scores(b, par, h, j):
                    m = j // 2
                    if h % (H // 2) == 0 and j == 0:
                        pe.wait_ge(neg_in[h // (H // 2)], 16 * b + 16)
                    if h == 0 and j == 0:
                        pe.wait_ge(v_ready, 2 * b + 2)
                    if j % 2 == 0:
                        pe.wait_ge(e_ready, 2 * H * b + 2 * h + m + 1)
                    last = pe.matmul(ps_s[m][:, (j % 2) * N:(j % 2 + 1) * N], k_stack[:, par, h, j * P:(j + 1) * P],
                                     q_stack[:, par, h, :], start=True, stop=True)
                    if j % 2:
                        last.then_inc(s_full, 1)

                def probs_v(b, par, h, j):
                    m, k = j // 2, j % 2
                    pair = 2 * h + m
                    if j == 0:
                        pe.wait_ge(o_kept, H * b + h + 1)
                    if k == 0:
                        pe.wait_ge(lo_ready, 2 * H * b + pair + 1)
                    v = v_sb[:, par, j, h, :]
                    pe.matmul(ps_o[h % 2][0:VH, :], v, probs_hi[:, pair % RING, k, :], start=(j == 0), stop=False)
                    last = pe.matmul(ps_o[h % 2][0:VH, :], v, probs_lo[:, pair % RING, k, :], start=False, stop=(j == NJ - 1))
                    if k:
                        last.then_inc(pv_done, 1)

                def merge(b, t):
                    if t == 0:
                        pe.wait_ge(o_ready, b + 1)
                    w = bank()
                    for c in range(TT):
                        last = pe.matmul(w[:], w_m[:, c, t * P:(t + 1) * P], o_cat[:, c, :], start=(c == 0), stop=(c == TT - 1))
                    uses.inc(last)

                def transpose_xn2(b, t):
                    if t == 0:
                        pe.wait_ge(xn2_ready, b + 1)
                    w = bank()
                    for c in range(HC):
                        last = pe.transpose(w[:, c * P:(c + 1) * P], xn2_sb[:, t, c * P:(c + 1) * P], ident[:])
                    uses.inc(last)

                def route(b):
                    pe.wait_ge(xn2T_ready, 2 * b + 2)
                    w = bank()
                    for t in range(TT):
                        for c in range(HC):
                            last = pe.matmul(w[:, t * 8:(t + 1) * 8], xn2_T[:, t, c, :], w_router[:, c, :],
                                             start=(c == 0), stop=(c == HC - 1))
                    uses.inc(last)

                def step(name, k, b, par):
                    if name == "qk":
                        if k == 0:
                            pe.wait_ge(xn_loaded, 16 * b + 16)
                            pe.wait_ge(ctx_loaded, 16 * b + 16)
                        project_qk(b, k)
                    elif name == "split":
                        transpose_qk(b, k)
                    elif name == "v":
                        project_v(b, k)
                    elif name == "max":
                        maxima(b, par, k // NJ, k % NJ)
                    elif name == "neg":
                        transpose_max(b, k)
                    elif name == "merge":
                        merge(b, k)
                    elif name == "turn2":
                        transpose_xn2(b, k)
                    elif name == "route":
                        route(b)

                def body(b, par, prev, nxt):
                    for h in range(H):
                        main = []
                        for m in range(2):
                            if (prev if h < LAG else nxt is not None):
                                main += [("probs_v", 2 * m), ("probs_v", 2 * m + 1)]
                            if nxt is not None:
                                main += [("scores", 2 * m), ("scores", 2 * m + 1)]
                        for name, k in interleaved(main, steps_beside(h, prev, nxt)):
                            if name == "scores":
                                scores(b, par, h, k)
                            elif name == "probs_v":
                                probs_v(*head_before(b, par, h), k)
                            else:
                                step(name, k, b - 1 if name in FOR_PREVIOUS else b + 1, 1 - par)

                pe.wait_ge(consts_in, 16 * 12)
                for h in range(H):
                    for name, k in steps_beside(h, False, True):
                        step(name, k, 0, 0)
                batches(pe, body, uses, PRE_USES + POST_USES)

            @block.vector
            def _(dve):
                chain = Count(dve, s_dve)
                taken = Count(dve, w_free)

                def bank():
                    dve.wait_ge(w_full, taken.base + taken.n + 1)
                    return ps_w[taken.n % 2]

                def pairs_of(ap):
                    return ap.rearrange("p (g k r h) -> p g k r h", g=4, r=2, h=H // 2)

                def rotate(b, j):
                    w = bank()
                    mark = taken.inc(dve.tensor_tensor(qk_b[:], w[:], bias_qk[:], ALU.add))
                    taken.wait(mark + 2)
                    dve.tensor_tensor(rot[:, 0].rearrange("p (g d h) -> p g d h", g=4, d=HD),
                                      qk_b[:].rearrange("p (g d h) -> p g d h", g=4, d=HD),
                                      cos_f[:, j, :].unsqueeze(1).unsqueeze(3).to_broadcast([P, 4, HD, H // 2]), ALU.mult)
                    t, o = pairs_of(qk_b[:]), pairs_of(rot[:, 1])
                    sin = sin_f[:, j, :].rearrange("p (k r) -> p k r", r=2)
                    for r in range(2):
                        last = dve.tensor_tensor(o[:, :, :, r], t[:, :, :, 1 - r],
                                                 sin[:, :, r].unsqueeze(1).unsqueeze(3).to_broadcast([P, 4, HD // 2, H // 2]),
                                                 ALU.mult)
                    chain.link(last)
                    dve.tensor_tensor(qk_rot[:, j, :], rot[:, 0], rot[:, 1], ALU.add).then_inc(rot_ready, 1)

                def split(b, t):
                    w = bank()
                    if t == 0 and (not isinstance(b, int) or b >= 1):
                        for side in range(2):
                            dve.wait_ge(parts_stored[side], 32 * b)
                    p = parts[:, t]
                    chain.link(dve.tensor_copy(p[:, 0, :], w[:]))
                    mark = taken.inc(dve.tensor_tensor(qk_b[:], w[:], p[:, 0, :], ALU.subtract))
                    taken.wait(mark + 2)
                    chain.link(dve.tensor_copy(p[:, 1, :], qk_b[:]))
                    dve.tensor_tensor(p[:, 2, :], qk_b[:], p[:, 1, :], ALU.subtract).then_inc(parts_ready, 1)

                def keep_v(b, par, i):
                    w = bank()
                    if i == 0:
                        dve.wait_ge(parts_ready, 4 * b + 4)
                    mark = taken.inc(dve.tensor_tensor(
                        v_full, w[:].rearrange("p (j h d) -> p j h d", j=2, d=HD),
                        bias_v[:].rearrange("p (h d) -> p h d", d=HD).unsqueeze(1).to_broadcast([P, 2, H, HD]), ALU.add))
                    taken.wait(mark + 2)
                    v = v_sb[:, par, 2 * i:2 * i + 2]
                    chain.link(dve.tensor_copy(v[:, :, :, 0:HD], v_full))
                    chain.link(dve.tensor_tensor(v[:, :, :, HD + 1:VH], v_full, v[:, :, :, 0:HD], ALU.subtract))
                    dve.sem_inc(v_ready, 1)
                    if i == 1:
                        dve.sem_inc(inputs_free, 1)

                def reduce_max(b, h, j):
                    w = bank()
                    at = h % (H // 2) * NJ + j
                    mark = taken.inc(dve.tensor_reduce(row_max[:, h // (H // 2), at:at + 1], w[:], AX.X, ALU.max))
                    if h % (H // 2) == H // 2 - 1 and j == NJ - 1:
                        taken.wait(mark + 2)
                        dve.sem_inc(max_ready, 1)

                def negate_max(b, half):
                    w = bank()[0:MH, 0:P]
                    if half or not isinstance(b, int) or b >= 1:
                        dve.wait_ge(neg_stored, 32 * b + 16 * half)
                    chain.link(dve.tensor_scalar(neg_parts[:, 0, :], w, -1.0, None, ALU.mult))
                    mark = taken.inc(dve.scalar_tensor_tensor(neg_rest[:], w, -1.0, neg_parts[:, 0, :], ALU.mult, ALU.subtract))
                    taken.wait(mark + 2)
                    chain.link(dve.tensor_copy(neg_parts[:, 1, :], neg_rest[:]))
                    dve.tensor_tensor(neg_parts[:, 2, :], neg_rest[:], neg_parts[:, 1, :], ALU.subtract).then_inc(neg_ready, 1)

                def reciprocals(b):
                    dve.wait_ge(sums_loaded, 16 * b + 16)
                    dve.reciprocal(rsums[:], sums[:]).then_inc(rsums_ready, 1)

                def residual(b, t):
                    if t == 0:
                        dve.wait_ge(res_loaded, 16 * b + 16)
                        dve.wait_ge(x2_stored, 32 * b + 32)
                    w = bank()
                    mark = taken.inc(dve.scalar_tensor_tensor(x2_sb[:, t, :], w[:], bias_m[:, t:t + 1], x_res[:, t, :],
                                                              ALU.add, ALU.add))
                    if t < TT - 1:
                        return
                    taken.wait(mark + 2)
                    dve.sem_inc(x2_ready, 1)
                    dve.sem_inc(o_used, 1)
                    chain.link(layer_norm_stats(dve, chain, x2_sb, stats2, mean_var2))
                    dve.tensor_scalar(var_eps2[:], mean_var2[:, :, 1], LN_EPS, None, ALU.add).then_inc(var2_ready, 1)

                def norm2_apply(b):
                    dve.wait_ge(rstd2_ready, b + 1)
                    for t in range(TT):
                        last = dve.tensor_scalar(xn2_sb[:, t, :], x2_sb[:, t, :], mean_var2[:, t, 0:1], rstd2[:, t:t + 1],
                                                 ALU.subtract, ALU.mult)
                    last.then_inc(xn2_ready, 1)

                def keep_xn2_T(b, t):
                    w = bank()
                    taken.inc(dve.tensor_copy(xn2_T[:, t], w[:].rearrange("p (c q) -> p c q", c=HC)))
                    taken.wait(taken.base + taken.n + 2)
                    dve.sem_inc(xn2T_ready, 1)

                def keep_logits(b):
                    w = bank()
                    taken.inc(dve.tensor_copy(logits[:, bass.ds(b * TT, TT), :],
                                              w[:, 0:TT * 8].rearrange("p (t e) -> p t e", t=TT)))

                TURN = 4 + 4 * 2 + 4 + 2 * 2 + 3

                def step(name, k, b, par):
                    if name == "qk":
                        rotate(b, k)
                    elif name == "split":
                        split(b, k)
                    elif name == "v":
                        keep_v(b, par, k)
                    elif name == "max":
                        reduce_max(b, k // NJ, k % NJ)
                    elif name == "neg":
                        negate_max(b, k)
                    elif name == "merge":
                        residual(b, k)
                    elif name == "norm2":
                        norm2_apply(b)
                    elif name == "turn2":
                        keep_xn2_T(b, k)
                    elif name == "route":
                        keep_logits(b)

                def body(b, par, prev, nxt):
                    first = chain.n
                    for h in range(H):
                        if h == 3 and prev:
                            reciprocals(b - 1)
                        for name, k in steps_beside(h, prev, nxt):
                            step(name, k, b - 1 if name in FOR_PREVIOUS else b + 1, 1 - par)
                    return chain.n - first

                chain.link(dve.memset(v_full, 1.0))
                for par in range(2):
                    chain.inc(dve.tensor_copy(v_sb[:, par, :, :, HD], v_full[:, 0, 0:NJ, :].rearrange("p j h -> p j h")))
                chain.inc(dve.memset(row_max[:], 0.0))
                chain.link(dve.memset(k_stack[ROWS:ROWS + MAX_ROWS], 1.0))
                for s, n in ((w_free, 2), (pv_done, RING), (o_used, 1), (x2_stored, 32)):
                    dve.sem_inc(s, n)
                dve.wait_ge(consts_in, 16 * 12)
                for j in range(NJ):
                    even = sin_f[:, j, :].rearrange("p (k r) -> p k r", r=2)[:, :, 0]
                    last = chain.inc(dve.tensor_scalar(even, even, -1.0, None, ALU.mult))
                chain.wait(last)
                for h in range(H):
                    for name, k in steps_beside(h, False, True):
                        step(name, k, 0, 0)

                body(0, 0, False, True)
                before, used = chain.n, taken.n
                assert used % 2 == 0
                with dve.Fori(0, (B - 2) // 2) as i:
                    for k in range(2):
                        chain.base, taken.base = i * (2 * TURN), i * (2 * (PRE_USES + POST_USES))
                        assert body(i * 2 + 1 + k, 1 - k, True, True) == TURN
                chain.base, chain.n = 0, before + (B - 2) * TURN
                taken.base, taken.n = 0, used + (B - 2) * (PRE_USES + POST_USES)
                body(B - 1, 1, True, False)
                body(B, 0, True, None)


E = 8
TOP = 2
F = 352
FC = (F + P - 1) // P
TOKENS = B * T
TILES = TOKENS // P
PAIRS = TOP * TILES
BLOCKS = PAIRS + E - 1
NOBODY = 2 * TOKENS


def build_stage_c(nc, xn2, logits, w1_t, w2_t, ident_in, before_in, numbers_in, out):
    with ExitStack() as ctx:
        def sb(name, shape, dt=FP32):
            return ctx.enter_context(nc.sbuf_tensor("c_" + name, shape, dt))

        def pb(name, shape=(P, 512), dt=FP32):
            return ctx.enter_context(nc.psum_tensor("c_" + name, list(shape), dt))

        def sem(name):
            return ctx.enter_context(nc.semaphore("c_" + name))

        W1 = HC * 2 * F
        W2 = FC * HID
        w1_sb = sb("w1", [P, E * W1])
        w2_sb = sb("w2", [P, E * W2])
        ident = sb("ident", [P, P])
        before = sb("before", [P, 2, P])
        numbers = sb("numbers", [P, P])
        token = sb("token", [P, TILES])
        best = sb("best", [P, TILES, E])
        best_at = sb("best_at", [P, TILES, E], U32)
        choice = sb("choice", [P, TOP, TILES])
        gap = sb("gap", [P, TILES])
        gate = sb("gate", [P, TOP, TILES])
        chosen = sb("chosen", [P, TOP, TILES, E])
        both = sb("both", [P, TILES, E])
        ones = sb("ones", [P, TILES])
        in_tile = sb("in_tile", [P, E, TILES])
        up_to = sb("up_to", [P, E, TILES])
        count_i = sb("count_i", [P, E], I32)
        n_blocks = sb("n_blocks", [P, E])
        block_end = sb("block_end", [P, E])
        start = sb("start", [P, E])
        place = sb("place", [P, TILES, E])
        pos = sb("pos", [P, TOP, TILES])
        pos_i = sb("pos_i", [P, TOP, TILES], I32)
        part_i = sb("part_i", [P, 2, TOP, TILES], I32)
        block_row = sb("block_row", [P, 2, TOP, TILES])
        ge = sb("ge", [1, BLOCKS, E])
        expert = sb("expert", [1, BLOCKS])
        expert_i = sb("expert_i", [1, BLOCKS], I32)
        is_row = sb("is_row", [P, 4, P])
        in_block = sb("in_block", [P, 4, 2, BLOCKS])
        ids = sb("ids", [P, BLOCKS], I32)
        gates = sb("gates", [P, BLOCKS])
        id_in = sb("id_in", [P, 2], I32)
        id_out = sb("id_out", [P, 2], I32)
        xb = sb("xb", [P, 2, HID])
        xbT = sb("xbT", [P, 2, HC, P])
        silu = sb("silu", [P, 2, F])
        hidden = sb("hidden", [P, 2, FC * P])
        hiddenT = sb("hiddenT", [P, 2, FC, P])
        yb = sb("yb", [P, 2, HID])

        ps_g = [pb(f"ps_g{i}") for i in range(2)]
        ps_u = [pb(f"ps_u{i}") for i in range(2)]
        ps_y = [pb(f"ps_y{i}") for i in range(2)]
        ps_xT, ps_hT = pb("ps_xT"), pb("ps_hT")

        consts_in, w_in = sem("consts_in"), sem("w_in")
        token_ready = sem("token_ready")
        gap_ready, gate_ready = sem("gap_ready"), sem("gate_ready")
        both_ready, ranks_full, places_full = sem("both_ready"), sem("ranks_full"), sem("places_full")
        onehots, onehots_used = sem("onehots"), sem("onehots_used")
        plan_ready = sem("plan_ready")
        id_free = sem("id_free")
        gathered = [sem(f"gathered{i}") for i in range(2)]
        scattered = sem("scattered")
        xT_full, xT_ready = sem("xT_full"), sem("xT_ready")
        g_full, u_full, silu_ready, hidden_ready = sem("g_full"), sem("u_full"), sem("silu_ready"), sem("hidden_ready")
        hT_full, hT_ready, y_full, y_ready = sem("hT_full"), sem("hT_ready"), sem("y_full"), sem("y_ready")
        id_ready, id_out_ready = sem("id_ready"), sem("id_out_ready")
        s_dve = sem("dve")
        passed = sem("passed")
        assert (BLOCKS - 5) % 2 == 0

        def done(i):
            return i + 3

        def blocks(engine, body):
            body(0, 0, False, True, True)
            body(1, 1, True, True, True)
            body(2, 0, True, True, True)
            with engine.Fori(0, (BLOCKS - 5) // 2) as n:
                body(n * 2 + 3, 1, True, True, True)
                body(n * 2 + 4, 0, True, True, True)
            body(BLOCKS - 2, (BLOCKS - 2) % 2, True, True, False)
            body(BLOCKS - 1, (BLOCKS - 1) % 2, True, False, False)
            body(BLOCKS, BLOCKS % 2, True, None, False)

        with nc.Block() as block:
            @block.sync
            def _(sp):
                sp.dma_start(ident[:], ident_in).then_inc(consts_in, 16)
                sp.dma_start(before[:], before_in).then_inc(consts_in, 16)
                sp.dma_start(numbers[:], numbers_in).then_inc(consts_in, 16)
                for e in range(E):
                    sp.dma_start(w1_sb[:, e * W1:(e + 1) * W1].rearrange("p (c n) -> p c n", c=HC),
                                 w1_t[e].rearrange("(c p) n -> p c n", p=P)).then_inc(w_in, 16)
                    for c in range(FC):
                        k = min(P, F - c * P)
                        sp.dma_start(w2_sb[0:k, e * W2 + c * HID:e * W2 + (c + 1) * HID],
                                     w2_t[e, c * P:c * P + k, :]).then_inc(w_in, 16)

            @block.gpsimd
            def _(pool):
                pool.iota(token[:], [[P, TILES]], base=-NOBODY, channel_multiplier=1,
                          allow_small_or_imprecise_dtypes=True).then_inc(token_ready, 1)

                def wait(s, value):
                    pool.wait_ge(s, value)
                    pool.sem_inc(passed, 1)

                def gather(i, par):
                    wait(xT_full, done(i - 2))
                    pool.tensor_copy(id_in[:, par:par + 1], ids[:, bass.ds(i, 1)]).then_inc(id_ready, 1)
                    wait(id_ready, i + 1)
                    pool.indirect_dma_start(xb[:, par, :], None, xn2, bass.IndirectOffsetOnAxis(ap=id_in[:, par:par + 1].bitcast(U32), axis=0),
                                            bounds_check=last_token, oob_is_err=False).then_inc(gathered[par], 16)

                def scatter(i, par):
                    if not isinstance(i, int) or i >= 1:
                        wait(scattered, 16 * i)
                    pool.tensor_copy(id_out[:, par:par + 1], ids[:, bass.ds(i, 1)]).then_inc(id_out_ready, 1)
                    wait(id_out_ready, i + 1)
                    wait(y_ready, done(i))
                    pool.indirect_dma_start(out, bass.IndirectOffsetOnAxis(ap=id_out[:, par:par + 1].bitcast(U32), axis=0), yb[:, par, :], None,
                                            bounds_check=last_token, oob_is_err=False, compute_op=ALU.add).then_inc(scattered, 16)

                def body(i, par, prev, nxt, nxt2):
                    if nxt2:
                        gather(i + 2, par)
                    if prev:
                        scatter(i - 1, 1 - par)

                last_token = pool.to_reg(TOKENS - 1)
                pool.wait_ge(plan_ready, 1)
                gather(0, 0)
                gather(1, 1)
                blocks(pool, body)
                pool.wait_ge(scattered, 16 * BLOCKS)

            @block.tensor
            def _(pe):
                pe.wait_ge(consts_in, 48)
                pe.wait_ge(both_ready, 1)
                o = both[:].rearrange("p t e -> p (t e)")
                pe.matmul(ps_g[0][:, 0:TILES * E], before[:, 0, :], o, start=True, stop=True)
                pe.matmul(ps_g[1][:, 0:TILES * E], before[:, 1, :], o, start=True, stop=True).then_inc(ranks_full, 1)
                for n in range(PAIRS):
                    pe.wait_ge(onehots, n + 1)
                    pe.matmul(ps_y[0][:, 0:2 * BLOCKS], is_row[:, n % 4, :], in_block[:, n % 4].rearrange("p k n -> p (k n)"),
                              start=(n == 0), stop=(n == PAIRS - 1)).then_inc(onehots_used, 1)

                def transpose_x(i, par):
                    pe.wait_ge(gathered[par], gathers_of(i, par))
                    pe.wait_ge(xT_ready, done(i - 1))
                    for c in range(HC):
                        last = pe.transpose(ps_xT[:, c * P:(c + 1) * P], xb[:, par, c * P:(c + 1) * P], ident[:])
                    last.then_inc(xT_full, 1)

                def gathers_of(i, par):
                    return (i - par) * 8 + 16

                def up(i, par):
                    e = pe.value_load(expert_i[0:1, bass.ds(i, 1)], min_val=0, max_val=E - 1)
                    pe.wait_ge(xT_ready, done(i))
                    for half, (ps, free, full) in enumerate(((ps_g, silu_ready, g_full), (ps_u, hidden_ready, u_full))):
                        pe.wait_ge(free, done(i - 2))
                        for c in range(HC):
                            last = pe.matmul(ps[par][:, 0:F], xbT[:, par, c, :],
                                             w1_sb[:, bass.ds(e * W1 + (c * 2 + half) * F, F)], start=(c == 0), stop=(c == HC - 1))
                        last.then_inc(full, 1)

                def transpose_hidden(i, par):
                    pe.wait_ge(hidden_ready, done(i))
                    pe.wait_ge(hT_ready, done(i - 1))
                    for c in range(FC):
                        last = pe.transpose(ps_hT[:, c * P:(c + 1) * P], hidden[:, par, c * P:(c + 1) * P], ident[:])
                    last.then_inc(hT_full, 1)

                def down(i, par):
                    e = pe.value_load(expert_i[0:1, bass.ds(i, 1)], min_val=0, max_val=E - 1)
                    pe.wait_ge(hT_ready, done(i))
                    pe.wait_ge(y_ready, done(i - 2))
                    for c in range(FC):
                        k = min(P, F - c * P)
                        last = pe.matmul(ps_y[par][:, :], hiddenT[0:k, par, c, :], w2_sb[0:k, bass.ds(e * W2 + c * HID, HID)],
                                         start=(c == 0), stop=(c == FC - 1))
                    last.then_inc(y_full, 1)

                def body(i, par, prev, nxt, nxt2):
                    if nxt is not None:
                        up(i, par)
                    if prev:
                        transpose_hidden(i - 1, 1 - par)
                    if nxt:
                        transpose_x(i + 1, 1 - par)
                    if prev:
                        down(i - 1, 1 - par)

                pe.wait_ge(plan_ready, 1)
                pe.wait_ge(w_in, 16 * (1 + FC) * E)
                transpose_x(0, 0)
                blocks(pe, body)

            @block.scalar
            def _(act):
                act.wait_ge(gap_ready, 1)
                act.activation(gate[:, 1, :], gap[:], ACT.Exp).then_inc(gate_ready, 1)

                def keep_xT(i, par):
                    act.wait_ge(xT_full, done(i))
                    act.wait_ge(u_full, done(i - 2))
                    act.copy(xbT[:, par], ps_xT[:].rearrange("p (c q) -> p c q", c=HC)).then_inc(xT_ready, 1)

                def body(i, par, prev, nxt, nxt2):
                    if nxt is not None:
                        act.wait_ge(g_full, done(i))
                        act.wait_ge(hidden_ready, done(i - 2))
                        act.activation(silu[:, par, :], ps_g[par][:, 0:F], ACT.Silu).then_inc(silu_ready, 1)
                    if nxt:
                        keep_xT(i + 1, 1 - par)

                keep_xT(0, 0)
                blocks(act, body)

            @block.vector
            def _(dve):
                chain = Count(dve, s_dve)
                for s in (xT_full, xT_ready, g_full, u_full, silu_ready, hidden_ready, hT_full, hT_ready, y_full, y_ready):
                    dve.sem_inc(s, 2)
                dve.memset(xb[:], 0.0)
                dve.memset(hidden[:], 0.0)
                chain.link(dve.memset(ones[:], 1.0))
                for t in range(TILES):
                    last = chain.inc(dve.max(best[:, t, :], logits[:, t, :]))
                chain.wait(last)
                for t in range(TILES):
                    last = chain.inc(dve.max_index(best_at[:, t, :], best[:, t, :], logits[:, t, :]))
                dve.tensor_tensor(gap[:], best[:, :, 1], best[:, :, 0], ALU.subtract).then_inc(gap_ready, 1)
                chain.wait(last)
                for k in range(TOP):
                    last = chain.inc(dve.tensor_copy(choice[:, k, :], best_at[:, :, k]))
                chain.wait(last)
                dve.wait_ge(consts_in, 48)
                each = numbers[:, 0:E].unsqueeze(1).to_broadcast([P, TILES, E])
                for k in range(TOP):
                    last = chain.inc(dve.tensor_tensor(chosen[:, k], choice[:, k, :].unsqueeze(2).to_broadcast([P, TILES, E]), each, ALU.is_equal))
                chain.wait(last)
                dve.tensor_tensor(both[:], chosen[:, 0], chosen[:, 1], ALU.add).then_inc(both_ready, 1)
                dve.wait_ge(gate_ready, 1)
                chain.link(dve.tensor_scalar(gap[:], gate[:, 1, :], 1.0, None, ALU.add))
                chain.link(dve.reciprocal(gate[:, 0, :], gap[:]))
                chain.link(dve.tensor_tensor(gate[:, 1, :], gate[:, 1, :], gate[:, 0, :], ALU.mult))
                dve.wait_ge(ranks_full, 1)
                chain.link(dve.tensor_copy(in_tile[:], ps_g[1][:, 0:TILES * E].rearrange("p (t e) -> p e t", e=E)))
                for e in range(E):
                    last = chain.inc(dve.tensor_tensor_scan(up_to[:, e, :], ones[:], in_tile[:, e, :], 0.0, ALU.mult, ALU.add))
                chain.wait(last)
                chain.link(dve.tensor_scalar(count_i[:], up_to[:, :, TILES - 1], float(P - 1), None, ALU.add))
                chain.link(dve.tensor_scalar(count_i[:], count_i[:], P.bit_length() - 1, None, ALU.logical_shift_right))
                chain.link(dve.tensor_copy(n_blocks[:], count_i[:]))
                chain.link(dve.tensor_tensor_scan(block_end[:], ones[:, 0:E], n_blocks[:], 0.0, ALU.mult, ALU.add))
                chain.link(dve.tensor_tensor(start[:], block_end[:], n_blocks[:], ALU.subtract))
                chain.link(dve.tensor_scalar(start[:], start[:], float(P), None, ALU.mult))
                chain.link(dve.tensor_tensor(up_to[:], up_to[:], in_tile[:], ALU.subtract))
                chain.link(dve.tensor_tensor(up_to[:], up_to[:], start[:].unsqueeze(2).to_broadcast([P, E, TILES]), ALU.add))
                chain.link(dve.tensor_tensor(place[:], ps_g[0][:, 0:TILES * E].rearrange("p (t e) -> p t e", e=E),
                                             up_to[:].rearrange("p e t -> p t e"), ALU.add))
                for k in range(TOP):
                    last = chain.inc(dve.tensor_tensor(chosen[:, k], chosen[:, k], place[:], ALU.mult))
                chain.wait(last)
                for k in range(TOP):
                    last = chain.inc(dve.tensor_reduce(pos[:, k, :], chosen[:, k], AX.X, ALU.add))
                chain.wait(last)
                chain.link(dve.tensor_copy(pos_i[:], pos[:]))
                chain.inc(dve.tensor_scalar(part_i[:, 0], pos_i[:], P.bit_length() - 1, None, ALU.logical_shift_right))
                chain.link(dve.tensor_scalar(part_i[:, 1], pos_i[:], P - 1, None, ALU.bitwise_and))
                chain.link(dve.tensor_copy(block_row[:], part_i[:]))
                chain.link(dve.tensor_tensor(ge[:], numbers[0:1, 0:BLOCKS].unsqueeze(2).to_broadcast([1, BLOCKS, E]),
                                             block_end[0:1, :].unsqueeze(1).to_broadcast([1, BLOCKS, E]), ALU.is_ge))
                chain.link(dve.tensor_reduce(expert[:], ge[:], AX.X, ALU.add))
                chain.link(dve.tensor_scalar(expert_i[:], expert[:], float(E - 1), None, ALU.min))
                dve.wait_ge(token_ready, 1)
                for n in range(PAIRS):
                    k, t, s = n // TILES, n % TILES, n % 4
                    if n >= 4:
                        dve.wait_ge(onehots_used, n - 3)
                    dve.tensor_scalar(is_row[:, s, :], numbers[:], block_row[:, 1, k, t:t + 1], None, ALU.is_equal)
                    at = block_row[:, 0, k, t:t + 1]
                    dve.tensor_scalar(in_block[:, s, 0, :], numbers[:, 0:BLOCKS], at, token[:, t:t + 1], ALU.is_equal, ALU.mult)
                    dve.tensor_scalar(in_block[:, s, 1, :], numbers[:, 0:BLOCKS], at, gate[:, k, t:t + 1], ALU.is_equal, ALU.mult) \
                       .then_inc(onehots, 1)
                dve.wait_ge(onehots_used, PAIRS)
                chain.inc(dve.tensor_scalar(ids[:], ps_y[0][:, 0:BLOCKS], float(NOBODY), None, ALU.add))
                chain.link(dve.tensor_copy(gates[:], ps_y[0][:, BLOCKS:2 * BLOCKS]))
                dve.sem_inc(plan_ready, 1)

                def body(i, par, prev, nxt, nxt2):
                    if prev:
                        dve.wait_ge(hT_full, done(i - 1))
                        dve.wait_ge(y_full, done(i - 3))
                        dve.tensor_copy(hiddenT[:, 1 - par], ps_hT[:, 0:FC * P].rearrange("p (c q) -> p c q", c=FC)) \
                           .then_inc(hT_ready, 1)
                    if nxt is not None:
                        dve.wait_ge(silu_ready, done(i))
                        dve.wait_ge(u_full, done(i))
                        dve.wait_ge(hT_full, done(i - 2))
                        dve.tensor_tensor(hidden[:, par, 0:F], silu[:, par, :], ps_u[par][:, 0:F], ALU.mult).then_inc(hidden_ready, 1)
                    if prev:
                        dve.wait_ge(y_full, done(i - 1))
                        if not isinstance(i, int) or i >= 3:
                            dve.wait_ge(scattered, 16 * (i - 2))
                        dve.tensor_scalar(yb[:, 1 - par, :], ps_y[1 - par][:], gates[:, bass.ds(i - 1, 1)], None, ALU.mult) \
                           .then_inc(y_ready, 1)

                blocks(dve, body)


def build(nc, x, ctx_in, w_qkv, w_out, decay_rows, enc, wq, bq, wk, bk, wv, bv, wm, bm, router_t, w1_t, w2_t,
          ident, head_sum, head_spread, before, numbers, out):
    x1 = nc.dram_tensor("x1", (B, T, HID), FP32, kind="Internal").ap()
    xn1 = nc.dram_tensor("xn1", (B, T, HID), FP32, kind="Internal").ap()
    xn2 = nc.dram_tensor("xn2", (B, T, HID), FP32, kind="Internal").ap()
    with nc.sbuf_tensor("logits", [P, TILES, E], FP32) as logits:
        build_stage_a(nc, x, w_qkv, w_out, decay_rows, ident, head_sum, head_spread, x1, xn1)
        build_stage_b(nc, x1, xn1, ctx_in, wq, wk, wv, wm, bq, bk, bv, bm, enc, router_t, ident, out, xn2, logits)
        build_stage_c(nc, xn2.rearrange("b t n -> (b t) n"), logits, w1_t, w2_t, ident, before, numbers,
                      out.rearrange("b t n -> (b t) n"))


def kernel(**inputs):
    import numpy as _np
    import concourse.bacc as _bacc
    from concourse import mybir as _mybir
    from concourse.bass_utils import run_bass_kernel_spmd as _run

    a = {k: _np.asarray(v) for k, v in inputs.items()}

    def head_major(w):
        return w.reshape(HD, H, -1).transpose(2, 1, 0).reshape(-1, HD * H)

    def in_halves(w):
        return w.reshape(HD, 2, H // 2, -1).transpose(3, 1, 0, 2).reshape(-1, HD * H)

    head_sum = (_np.arange(HC)[:, None] * 4 + _np.arange(P) // 32)[:, :, None] == _np.arange(H)
    head_sum = head_sum.transpose(1, 0, 2).astype(_np.float32)
    arrays = {
        "x": a["x"], "ctx": a["ctx_2048"], "w_qkv": a["L0_attn_w_qkv"], "w_out": a["L0_attn_w_out"],
        "decay": _np.repeat(a["L0_attn_decay_param"], HID // H).reshape(HC, P).T,
        "enc": a["L0_xattn_encoding"].reshape(2, HID, HD),
        "wq": in_halves(a["L0_xattn_Wq"]), "bq": in_halves(a["L0_xattn_bq"]),
        "wk": in_halves(a["L0_xattn_Wk"]), "bk": in_halves(a["L0_xattn_bk"]),
        "wv": head_major(a["L0_xattn_Wv"]), "bv": head_major(a["L0_xattn_bv"]),
        "wm": a["L0_xattn_Wm"].reshape(-1, HD, H).transpose(2, 1, 0).reshape(HD * H, -1),
        "bm": a["L0_xattn_bm"].reshape(TT, P).T,
        "router": a["L0_ffn_router_w"].T,
        "w1": a["L0_ffn_w1"].transpose(0, 2, 1), "w2": a["L0_ffn_w2"].transpose(0, 2, 1),
        "ident": _np.eye(P, dtype=_np.float32), "head_sum": head_sum, "head_spread": head_sum.transpose(2, 1, 0),
        "before": _np.stack([_np.triu(_np.ones((P, P), _np.float32), 1), _np.ones((P, P), _np.float32)], 1),
        "numbers": _np.tile(_np.arange(P, dtype=_np.float32), (P, 1)),
    }
    arrays = {k: _np.ascontiguousarray(v) for k, v in arrays.items()}
    nc = _bacc.Bacc("TRN2", target_bir_lowering=False, num_devices=1)
    args = [nc.dram_tensor(k, v.shape, _mybir.dt.from_np(v.dtype), kind="ExternalInput").ap() for k, v in arrays.items()]
    out = nc.dram_tensor("out", (B, T, HID), FP32, kind="ExternalOutput").ap()
    build(nc, *args, out)
    r = _run(nc, [arrays], core_ids=[0])
    return r.results[0]["out"]
```

```python
import concourse.bass as bass
from concourse import mybir
from contextlib import ExitStack

FP32 = mybir.dt.float32
FP32R = mybir.dt.float32r
BF16 = mybir.dt.bfloat16
I32 = mybir.dt.int32
U32 = mybir.dt.uint32
ALU = mybir.AluOpType
ACT = mybir.ActivationFunctionType
AX = mybir.AxisListType

P = 128
B, T, HID = 16, 256, 512
TT = T // P
HC = HID // P
H = 16
LN_EPS = 1e-05
DEN_EPS = 1e-06


class Count:

    def __init__(self, engine, sem):
        self.engine, self.sem, self.base, self.n = engine, sem, 0, 0

    def inc(self, instruction):
        instruction.then_inc(self.sem, 1)
        self.n += 1
        return self.base + self.n

    def wait(self, value):
        self.engine.wait_ge(self.sem, value)

    def link(self, instruction):
        self.wait(self.inc(instruction))


def layer_norm_stats(dve, count, x, stats, mean_var):
    last = None
    for t in range(x.shape[1]):
        last = dve.bn_stats(stats[:, t, :], x[:, t, :])
    count.link(last)
    dve.sem_inc(count.sem, 1)
    count.n += 1
    for t in range(x.shape[1]):
        last = dve.bn_aggr(mean_var[:, t, :], stats[:, t, :])
    return last


def build_stage_a(nc, x, w_qkv, w_out, decay_rows, ident_in, head_sum_in, head_spread_in, x1, xn1):
    with ExitStack() as ctx:
        def sb(name, shape, dt=FP32):
            return ctx.enter_context(nc.sbuf_tensor("a_" + name, shape, dt))

        def pb(name, shape=(P, 512), dt=FP32):
            return ctx.enter_context(nc.psum_tensor("a_" + name, list(shape), dt))

        def sem(name):
            return ctx.enter_context(nc.semaphore("a_" + name))

        weights = sb("weights", [P, HC, 4 * HID])
        w_hi = sb("w_hi", [P, HC, 4 * HID], FP32R)
        w_lo = sb("w_lo", [P, HC, 4 * HID], FP32R)
        ident = sb("ident", [P, P])
        head_sum = sb("head_sum", [P, HC, H])
        head_spread = sb("head_spread", [H, HC, P])
        decay_p = sb("decay_p", [P, HC])
        decay_1 = sb("decay_1", [P, HC])
        decay_2 = sb("decay_2", [P, HC])
        decay = sb("decay", [P, HC, T])
        half = sb("half", [P, TT])
        x_in = sb("x_in", [P, TT, HID])
        x_res = sb("x_res", [P, TT, HID])
        stats = sb("stats", [P, TT, 6])
        mean_var = sb("mean_var", [P, TT, 2])
        var_eps = sb("var_eps", [P, TT])
        rstd = sb("rstd", [P, TT])
        xn = sb("xn", [P, TT, HID])
        xT_hi = sb("xT_hi", [P, 2, HC, T], FP32R)
        xT_lo = sb("xT_lo", [P, 2, HC, T], FP32R)
        e_qk = sb("e_qk", [P, 2, 2, T])
        phi = sb("phi", [P, 2, 2, T])
        kv = sb("kv", [P, T])
        run_kv = sb("run_kv", [P, T])
        run_k = sb("run_k", [P, T])
        q_sum = sb("q_sum", [P, 2, HC, T])
        q_kv = sb("q_kv", [P, 2, HC, T])
        o_hi = sb("o_hi", [P, HC, T], FP32R)
        o_lo = sb("o_lo", [P, HC, T], FP32R)
        den = sb("den", [H, T])
        rden = sb("rden", [H, T])
        x1_sb = sb("x1_sb", [P, TT, HID])
        stats1 = sb("stats1", [P, TT, 6])
        mean_var1 = sb("mean_var1", [P, TT, 2])
        var_eps1 = sb("var_eps1", [P, TT])
        rstd1 = sb("rstd1", [P, TT])
        xn1_sb = sb("xn1_sb", [P, TT, HID])

        ps_qk = [pb(f"ps_qk{i}") for i in range(2)]
        ps_v = [pb(f"ps_v{i}") for i in range(2)]
        ps_t = [pb(f"ps_t{i}") for i in range(2)]
        ps_w = [pb(f"ps_w{i}") for i in range(2)]

        consts_in = sem("consts_in")
        x_loaded = sem("x_loaded")
        res_loaded = sem("res_loaded")
        x_free = sem("x_free")
        res_free = sem("res_free")
        stored = sem("stored")
        var1_ready, rstd1_ready, xn1_ready = sem("var1_ready"), sem("rstd1_ready"), sem("xn1_ready")
        var_ready = sem("var_ready")
        rstd_ready = sem("rstd_ready")
        xn_ready = sem("xn_ready")
        xt_full = sem("xt_full")
        xt_rounded = sem("xt_rounded")
        xt_ready = sem("xt_ready")
        w_in = [sem(f"w_in{k}") for k in range(HC)]
        w_rounded = sem("w_rounded")
        w_split = sem("w_split")
        qk_full, v_full = sem("qk_full"), sem("v_full")
        qkv_free = sem("qkv_free")
        exp_ready = sem("exp_ready")
        prod_ready = sem("prod_ready")
        den_full = sem("den_full")
        rden_ready = sem("rden_ready")
        spread_full = sem("spread_full")
        o_rounded = sem("o_rounded")
        o_ready = sem("o_ready")
        out_full = sem("out_full")
        w_free = sem("w_free")
        x1_ready = sem("x1_ready")
        s_dve = sem("dve")

        def per_iteration(engine, body):
            body(0, 0, False, True)
            with engine.Fori(0, (B - 2) // 2) as i:
                body(i * 2 + 1, 1, True, True)
                body(i * 2 + 2, 0, True, True)
            body(B - 1, 1, True, False)
            body(B, 0, True, None)

        with nc.Block() as block:
            @block.sync
            def _(sp):
                sp.dma_start(x_in[:], x[0].rearrange("(t p) n -> p t n", p=P)).then_inc(x_loaded, 16)
                sp.dma_start(ident[:], ident_in).then_inc(consts_in, 16)
                sp.dma_start(decay_p[:], decay_rows).then_inc(consts_in, 16)
                sp.dma_start(head_sum[:], head_sum_in).then_inc(consts_in, 16)
                sp.dma_start(head_spread[:], head_spread_in).then_inc(consts_in, 16)
                for k in range(HC):
                    sp.dma_start(weights[:, k, 0:3 * HID], w_qkv[k * P:(k + 1) * P, :]).then_inc(w_in[k], 16)
                    sp.dma_start(weights[:, k, 3 * HID:], w_out[k * P:(k + 1) * P, :]).then_inc(w_in[k], 16)

                def body(b, par, prev, nxt):
                    if nxt:
                        sp.wait_ge(x_free, b + 2)
                        sp.dma_start(x_in[:], x[bass.ds(b + 1, 1)].rearrange("a (t p) n -> p (a t) n", p=P)) \
                          .then_inc(x_loaded, 16)
                    if prev:
                        sp.wait_ge(res_free, b)
                        sp.dma_start(x_res[:], x[bass.ds(b - 1, 1)].rearrange("a (t p) n -> p (a t) n", p=P)) \
                          .then_inc(res_loaded, 16)
                        sp.wait_ge(x1_ready, b)
                        sp.dma_start(x1[bass.ds(b - 1, 1)].rearrange("a (t p) n -> p (a t) n", p=P), x1_sb[:]) \
                          .then_inc(stored, 16)
                        sp.wait_ge(xn1_ready, b)
                        sp.dma_start(xn1[bass.ds(b - 1, 1)].rearrange("a (t p) n -> p (a t) n", p=P), xn1_sb[:]) \
                          .then_inc(stored, 16)

                per_iteration(sp, body)
                sp.wait_ge(stored, 32 * B + 32)

            @block.gpsimd
            def _(pool):
                pool.memset(half[:], -0.5).then_inc(rstd_ready, 1)
                pool.wait_ge(rstd_ready, 1)

                def rstd_of(b):
                    pool.wait_ge(var_ready, b + 1)
                    pool.tensor_tensor(rstd[:], var_eps[:], half[:], ALU.pow).then_inc(rstd_ready, 1)

                def body(b, par, prev, nxt):
                    if nxt:
                        rstd_of(b + 1)
                    if prev:
                        pool.wait_ge(var1_ready, b)
                        pool.tensor_tensor(rstd1[:], var_eps1[:], half[:], ALU.pow).then_inc(rstd1_ready, 1)

                rstd_of(0)
                per_iteration(pool, body)

            @block.tensor
            def _(pe):
                def transposes(b):
                    pe.wait_ge(xn_ready, b + 1)
                    for t in range(TT):
                        pe.wait_ge(xt_ready, 2 * b + t + 1)
                        for c in range(HC):
                            last = pe.transpose(ps_t[t][:, c * P:(c + 1) * P], xn[:, t, c * P:(c + 1) * P], ident[:])
                        last.then_inc(xt_full, 1)

                def qkv(b, par, c):
                    pe.wait_ge(qkv_free, 4 * b + c + 1)
                    for role, out in ((0, ps_qk[c % 2][:, 0:T]), (1, ps_qk[c % 2][:, T:2 * T]), (2, ps_v[c % 2][:, 0:T])):
                        features = slice(role * HID + c * P, role * HID + (c + 1) * P)
                        for k in range(HC):
                            w, x = w_hi[:, k, features], xT_hi[:, par, k, :]
                            pe.matmul(out, w, x, start=(k == 0), stop=False)
                            pe.matmul(out, w, xT_lo[:, par, k, :], start=False, stop=False)
                            last = pe.matmul(out, w_lo[:, k, features], x, start=False, stop=(k == HC - 1))
                        if role:
                            last.then_inc(qk_full if role == 1 else v_full, 1)

                def denominators(b, par):
                    pe.wait_ge(prod_ready, 4 * b + 4)
                    pe.wait_ge(w_free, 5 * b + 1)
                    for c in range(HC):
                        last = pe.matmul(ps_w[0][0:H, 0:T], head_sum[:, c, :], q_sum[:, par, c, :],
                                         start=(c == 0), stop=(c == HC - 1))
                    last.then_inc(den_full, 1)

                def spread(b):
                    pe.wait_ge(rden_ready, b + 1)
                    for g in range(2):
                        pe.wait_ge(w_free, 5 * b + 1 + g)
                        for k in range(2):
                            last = pe.matmul(ps_w[1 - g][:, k * T:(k + 1) * T], head_spread[:, 2 * g + k, :], rden[:],
                                             start=True, stop=True)
                        last.then_inc(spread_full, 1)

                def project(b):
                    pe.wait_ge(o_ready, 2 * b + 2)
                    for t in range(TT):
                        pe.wait_ge(w_free, 5 * b + 3 + t)
                        for c in range(HC):
                            times = slice(t * P, (t + 1) * P)
                            o, w = o_hi[:, c, times], w_hi[:, c, 3 * HID:]
                            pe.matmul(ps_w[1 - t][:, :], o, w, start=(c == 0), stop=False)
                            pe.matmul(ps_w[1 - t][:, :], o, w_lo[:, c, 3 * HID:], start=False, stop=False)
                            last = pe.matmul(ps_w[1 - t][:, :], o_lo[:, c, times], w, start=False, stop=(c == HC - 1))
                        last.then_inc(out_full, 1)

                def body(b, par, prev, nxt):
                    for c in range(HC):
                        if nxt is not None:
                            if c == 0:
                                pe.wait_ge(xt_ready, 2 * b + 4)
                            qkv(b, par, c)
                        if prev and c == 0:
                            denominators(b - 1, 1 - par)
                        if prev and c == 1:
                            spread(b - 1)
                        if nxt and c == 2:
                            transposes(b + 1)
                        if prev and c == 3:
                            project(b - 1)

                pe.wait_ge(consts_in, 64)
                transposes(0)
                pe.wait_ge(w_rounded, HC)
                pe.wait_ge(w_split, HC)
                per_iteration(pe, body)

            @block.scalar
            def _(act):
                act.wait_ge(consts_in, 64)
                act.activation(decay_1[:], decay_p[:], ACT.Exp, scale=-1.0).then_inc(exp_ready, 1)

                def keep_xT(b, par):
                    for t in range(TT):
                        act.wait_ge(xt_full, 2 * b + t + 1)
                        act.copy(xT_hi[:, par, :, t * P:(t + 1) * P],
                                 ps_t[t][:].rearrange("p (c q) -> p c q", c=HC)).then_inc(xt_rounded, 1)

                def round_o(b, par):
                    for g in range(2):
                        act.wait_ge(w_free, 5 * b + 3 + g)
                        act.copy(o_hi[:, 2 * g:2 * g + 2, :], q_kv[:, par, 2 * g:2 * g + 2, :]).then_inc(o_rounded, 1)

                def body(b, par, prev, nxt):
                    for c in range(HC):
                        if nxt is not None:
                            act.wait_ge(qk_full, 4 * b + c + 1)
                            act.activation(e_qk[:, c % 2], ps_qk[c % 2][:].rearrange("p (r t) -> p r t", r=2), ACT.Exp) \
                               .then_inc(exp_ready, 1)
                        if prev and c == 1:
                            round_o(b - 1, 1 - par)
                        if nxt and c == 2:
                            keep_xT(b + 1, 1 - par)

                for k in range(HC):
                    if k == 1:
                        keep_xT(0, 0)
                    act.wait_ge(w_in[k], 32)
                    act.copy(w_hi[:, k, :], weights[:, k, :]).then_inc(w_rounded, 1)
                per_iteration(act, body)

            @block.vector
            def _(dve):
                chain = Count(dve, s_dve)
                chain.link(dve.memset(decay[:], 1.0))
                for s, n in ((x_free, 1), (res_free, 1), (xt_ready, 2), (qkv_free, 2), (w_free, 1), (stored, 32)):
                    dve.sem_inc(s, n)

                def norm_stats(b):
                    dve.wait_ge(x_loaded, 16 * b + 16)
                    chain.link(layer_norm_stats(dve, chain, x_in, stats, mean_var))
                    dve.tensor_scalar(var_eps[:], mean_var[:, :, 1], LN_EPS, None, ALU.add).then_inc(var_ready, 1)

                def norm_apply(b):
                    dve.wait_ge(rstd_ready, b + 2)
                    for t in range(TT):
                        last = dve.tensor_scalar(xn[:, t, :], x_in[:, t, :], mean_var[:, t, 0:1], rstd[:, t:t + 1],
                                                 ALU.subtract, ALU.mult)
                        if t < TT - 1:
                            continue
                        last.then_inc(xn_ready, 1)
                    dve.wait_ge(xn_ready, b + 1)
                    dve.sem_inc(x_free, 1)

                def scans(b, par, c):
                    dve.wait_ge(exp_ready, 4 * b + c + 2)
                    e, f = e_qk[:, c % 2], phi[:, c % 2]
                    chain.link(dve.tensor_scalar(e, e, 1.0, None, ALU.min))
                    chain.link(dve.scalar_tensor_tensor(f, ps_qk[c % 2][:].rearrange("p (r t) -> p r t", r=2), 0.0, e,
                                                        ALU.max, ALU.add))
                    dve.wait_ge(v_full, 4 * b + c + 1)
                    dve.tensor_tensor(kv[:], f[:, 1, :], ps_v[c % 2][:, 0:T], ALU.mult).then_inc(qkv_free, 1)
                    summed = chain.inc(dve.tensor_tensor_scan(run_k[:], decay[:, c, :], f[:, 1, :], 0.0, ALU.mult, ALU.add))
                    dve.wait_ge(qkv_free, 4 * b + c + 3)
                    kv_summed = chain.inc(dve.tensor_tensor_scan(run_kv[:], decay[:, c, :], kv[:], 0.0, ALU.mult, ALU.add))
                    chain.wait(summed)
                    dve.tensor_tensor(q_sum[:, par, c, :], f[:, 0, :], run_k[:], ALU.mult)
                    chain.wait(kv_summed)
                    dve.tensor_tensor(q_kv[:, par, c, :], f[:, 0, :], run_kv[:], ALU.mult).then_inc(prod_ready, 1)

                def reciprocals(b):
                    dve.wait_ge(den_full, b + 1)
                    dve.tensor_scalar(den[:], ps_w[0][0:H, 0:T], DEN_EPS, None, ALU.max).then_inc(w_free, 1)
                    dve.wait_ge(w_free, 5 * b + 2)
                    dve.reciprocal(rden[:], den[:]).then_inc(rden_ready, 1)

                def divide(b, par):
                    dve.wait_ge(prod_ready, 4 * b + 4)
                    for g in range(2):
                        dve.wait_ge(spread_full, 2 * b + g + 1)
                        o = q_kv[:, par, 2 * g:2 * g + 2, :]
                        dve.tensor_tensor(o, o, ps_w[1 - g][:].rearrange("p (c t) -> p c t", c=2), ALU.mult) \
                           .then_inc(w_free, 1)

                def split_o(b, par):
                    for g in range(2):
                        dve.wait_ge(o_rounded, 2 * b + g + 1)
                        chunks = slice(2 * g, 2 * g + 2)
                        dve.tensor_tensor(o_lo[:, chunks, :], q_kv[:, par, chunks, :], o_hi[:, chunks, :], ALU.subtract) \
                           .then_inc(o_ready, 1)

                def split_xT(b, par):
                    for t in range(TT):
                        dve.wait_ge(xt_rounded, 2 * b + t + 1)
                        times = slice(t * P, (t + 1) * P)
                        dve.tensor_tensor(xT_lo[:, par, :, times], ps_t[t][:].rearrange("p (c q) -> p c q", c=HC),
                                          xT_hi[:, par, :, times], ALU.subtract).then_inc(xt_ready, 1)

                def residual(b):
                    dve.wait_ge(res_loaded, 16 * b + 16)
                    dve.wait_ge(stored, 32 * b + 32)
                    for t in range(TT):
                        dve.wait_ge(out_full, 2 * b + t + 1)
                        dve.tensor_tensor(x1_sb[:, t, :], ps_w[1 - t][:], x_res[:, t, :], ALU.add).then_inc(w_free, 1)
                    dve.wait_ge(w_free, 5 * b + 6)
                    dve.sem_inc(x1_ready, 1)
                    dve.sem_inc(res_free, 1)
                    chain.link(layer_norm_stats(dve, chain, x1_sb, stats1, mean_var1))
                    dve.tensor_scalar(var_eps1[:], mean_var1[:, :, 1], LN_EPS, None, ALU.add).then_inc(var1_ready, 1)
                    dve.wait_ge(rstd1_ready, b + 1)
                    for t in range(TT):
                        last = dve.tensor_scalar(xn1_sb[:, t, :], x1_sb[:, t, :], mean_var1[:, t, 0:1], rstd1[:, t:t + 1],
                                                 ALU.subtract, ALU.mult)
                    last.then_inc(xn1_ready, 1)

                def body(b, par, prev, nxt):
                    first = chain.n
                    if nxt is not None:
                        scans(b, par, 0)
                    if prev:
                        reciprocals(b - 1)
                    if nxt:
                        norm_stats(b + 1)
                    if nxt is not None:
                        scans(b, par, 1)
                    if nxt:
                        norm_apply(b + 1)
                    if prev:
                        divide(b - 1, 1 - par)
                        split_o(b - 1, 1 - par)
                    if nxt is not None:
                        scans(b, par, 2)
                    if nxt:
                        split_xT(b + 1, 1 - par)
                    if nxt is not None:
                        scans(b, par, 3)
                    if prev:
                        residual(b - 1)
                    return chain.n - first

                norm_stats(0)
                norm_apply(0)
                for k in range(HC):
                    if k == 1:
                        split_xT(0, 0)
                    dve.wait_ge(w_rounded, k + 1)
                    dve.tensor_tensor(w_lo[:, k, :], weights[:, k, :], w_hi[:, k, :], ALU.subtract).then_inc(w_split, 1)
                dve.wait_ge(exp_ready, 1)
                chain.link(dve.tensor_scalar(decay_2[:], decay_1[:], 1.0, None, ALU.add))
                chain.link(dve.reciprocal(decay_1[:], decay_2[:]))
                for c in range(HC):
                    last = chain.inc(dve.tensor_scalar(decay[:, c, :], decay[:, c, :], decay_1[:, c:c + 1], None, ALU.mult))
                chain.wait(last)
                turn = 4 * 4 + 2 * 3
                body(0, 0, False, True)
                before = chain.n
                with dve.Fori(0, (B - 2) // 2) as i:
                    chain.base = i * (2 * turn)
                    assert body(i * 2 + 1, 1, True, True) == turn
                    assert body(i * 2 + 2, 0, True, True) == turn
                chain.base = 0
                chain.n = before + (B - 2) * turn
                body(B - 1, 1, True, False)
                body(B, 0, True, None)


HD = 16
N = HID
NJ = N // P
VH = 2 * HD + 1
RING = 4
LAG = 2
Q_PARTS = (0, 1, 2, 0, 1, 0)
K_PARTS = (0, 0, 0, 1, 1, 2)
ROWS = len(Q_PARTS) * HD
MAX_ROWS = 3


def build_stage_b(nc, x1, xn1, ctx_in, wq, wk, wv, wm, bq_rows, bk_rows, bv_rows, bm_cols, enc, router_t, ident_in,
                  x2, xn2, logits):
    with ExitStack() as ctx:
        def sb(name, shape, dt=FP32):
            return ctx.enter_context(nc.sbuf_tensor("b_" + name, shape, dt))

        def pb(name, shape=(P, 512), dt=FP32):
            return ctx.enter_context(nc.psum_tensor("b_" + name, list(shape), dt))

        def sem(name):
            return ctx.enter_context(nc.semaphore("b_" + name))

        def dram(name, shape, dt=FP32):
            return nc.dram_tensor("b_" + name, shape, dt, kind="Internal").ap()

        MH = H // 2 * NJ
        w_q, w_k, w_v, w_m = (sb(n, [P, TT, T]) for n in ("w_q", "w_k", "w_v", "w_m"))
        bias_qk = sb("bias_qk", [P, 2 * T])
        bias_v = sb("bias_v", [P, T])
        bias_m = sb("bias_m", [P, TT])
        cos_f = sb("cos_f", [P, NJ, HD])
        sin_f = sb("sin_f", [P, NJ, HD])
        w_router = sb("w_router", [P, HC, 8])
        ident = sb("ident", [P, P])
        half = sb("half", [P, TT])
        xn = sb("xn", [P, TT, HID])
        ctx_sb = sb("ctx_sb", [P, TT, HID])
        stats2 = sb("stats2", [P, TT, 6])
        mean_var2 = sb("mean_var2", [P, TT, 2])
        var_eps2 = sb("var_eps2", [P, TT])
        rstd2 = sb("rstd2", [P, TT])
        qk_b = sb("qk_b", [P, 2 * T])
        rot = sb("rot", [P, 2, 2 * T])
        qk_rot = sb("qk_rot", [P, NJ, 2 * T])
        parts = sb("parts", [P, 4, 3, N], BF16)
        q_stack = sb("q_stack", [ROWS + MAX_ROWS, 2, H, N], BF16)
        k_stack = sb("k_stack", [ROWS + MAX_ROWS, 2, H, N], BF16)
        v_sb = sb("v_sb", [P, 2, NJ, H, VH], FP32R)
        v_full = qk_b[:].rearrange("p (j h d) -> p j h d", j=2, d=HD)
        row_max = sb("row_max", [P, 2, P])
        neg_rest = sb("neg_rest", [MH, P])
        neg_parts = sb("neg_parts", [MH, MAX_ROWS, P], BF16)
        probs = sb("probs", [P, RING, 2, N])
        probs_hi = sb("probs_hi", [P, RING, 2, N], FP32R)
        probs_lo = sb("probs_lo", [P, RING, 2, N], FP32R)
        o_sb = sb("o_sb", [VH, 2, 4, N])
        sums = sb("sums", [P, H * N // P])
        rsums = sb("rsums", [P, H * N // P])
        o_cat = sb("o_cat", [P, TT, N])
        x2_sb = sb("x2_sb", [P, TT, HID])
        r_cat = x2_sb
        xn2_sb = sb("xn2_sb", [P, TT, HID])
        x_res = xn2_sb
        xn2_T = rot[:].rearrange("p t (c q) -> p t c q", c=HC)

        parts_dram = dram("parts_dram", (2, 2, 3, P, N), BF16)
        neg_dram = dram("neg_dram", (MAX_ROWS, H * N), BF16)
        o_dram = dram("o_dram", (H, HD, N))
        o_lo_dram = dram("o_lo_dram", (H, HD, N))
        sum_dram = dram("sum_dram", (H, N))
        rsum_dram = dram("rsum_dram", (H, N))
        rsum16_dram = dram("rsum16_dram", (H, HD, N))

        ps_s = [pb(f"ps_s{i}", (P, 2 * N)) for i in range(2)]
        ps_o = [pb(f"ps_o{i}") for i in range(2)]
        ps_w = [pb(f"ps_w{i}") for i in range(2)]

        consts_in = sem("consts_in")
        xn_loaded, ctx_loaded, res_loaded = sem("xn_loaded"), sem("ctx_loaded"), sem("res_loaded")
        inputs_free = sem("inputs_free")
        half_ready = sem("half_ready")
        ones_ready = sem("ones_ready")
        var2_ready, rstd2_ready = sem("var2_ready"), sem("rstd2_ready")
        w_full = sem("w_full")
        w_free = sem("w_free")
        rot_ready = sem("rot_ready")
        parts_ready = sem("parts_ready")
        parts_stored = [sem(f"parts_stored{i}") for i in range(2)]
        stacks_in = [sem(f"stacks_in{i}") for i in range(2)]
        v_ready = sem("v_ready")
        max_ready = sem("max_ready")
        neg_ready, neg_stored = sem("neg_ready"), sem("neg_stored")
        neg_in = [sem(f"neg_in{i}") for i in range(2)]
        s_full = sem("s_full")
        e_ready = sem("e_ready")
        hi_ready = sem("hi_ready")
        lo_ready = sem("lo_ready")
        lo2_ready = sem("lo2_ready")
        pv_done = sem("pv_done")
        o_kept = sem("o_kept")
        o_stored = [sem(f"o_stored{i}") for i in range(2)]
        o_loaded, o_added, sums_loaded = sem("o_loaded"), sem("o_added"), sem("sums_loaded")
        rsums_ready, rsums_moved, r_loaded = sem("rsums_ready"), sem("rsums_moved"), sem("r_loaded")
        o_ready = sem("o_ready")
        o_used = sem("o_used")
        x2_ready, xn2_ready = sem("x2_ready"), sem("xn2_ready")
        x2_stored = sem("x2_stored")
        xn2T_ready = sem("xn2T_ready")
        s_dve = sem("dve")
        passed, pool_passed = sem("passed"), sem("pool_passed")

        def maxima_of(first, end, own=False):
            return tuple(("own max" if own else "max", k) for k in range(first, end))

        STEPS = {
            0: maxima_of(39, 45, own=True),
            1: (("qk", 0), ("qk", 1)),
            2: maxima_of(45, 52, own=True),
            3: maxima_of(52, 55, own=True),
            4: (("qk", 2), ("qk", 3)) + maxima_of(55, 57, own=True),
            5: maxima_of(57, 64, own=True),
            6: (("remainder", 5), ("own neg", 1), ("v", 0)),
            7: (("split", 0), ("split", 1), ("merge", 0)),
            8: (("remainder", 7), ("merge", 1), ("split", 2)),
            9: (("v", 1), ("split", 3)) + maxima_of(0, 1),
            10: (("norm2", 0),) + maxima_of(1, 3),
            11: maxima_of(3, 10),
            12: (("turn2", 0), ("turn2", 1)) + maxima_of(10, 16),
            13: (("route", 0),) + maxima_of(16, 24),
            14: maxima_of(24, 32),
            15: (("neg", 0),) + maxima_of(32, 39),
        }
        OFFSETS = {"merge": -1, "norm2": -1, "turn2": -1, "route": -1, "own max": 0, "own neg": 0, "remainder": 0}
        BY_VECTOR = tuple(2 * k + 1 for h in range(H) for name, k in STEPS[h] if name == "remainder")
        USES = 4 + 4 + 2 + NJ * H + 2 + 2 + 2 + 1

        def steps_beside(h, prev, own, nxt):
            wanted = {-1: prev, 0: own, 1: nxt}
            return [(name.removeprefix("own "), k, OFFSETS.get(name, 1)) for name, k in STEPS[h] if wanted[OFFSETS.get(name, 1)]]

        def head_before(b, par, h):
            return (b, par, h - LAG) if h >= LAG else (b - 1, 1 - par, h - LAG + H)

        def remainder_ready(b, pair):
            before = sum(p < pair for p in BY_VECTOR)
            if pair in BY_VECTOR:
                return lo2_ready, len(BY_VECTOR) * b + before + 1
            return lo_ready, (2 * H - len(BY_VECTOR)) * b + pair - before + 1

        def interleaved(main, beside):
            order, done = [], 0
            for n, item in enumerate(main):
                order.append(item)
                upto = (n + 1) * len(beside) // len(main)
                order += beside[done:upto]
                done = upto
            return order + beside[done:]

        def batches(engine, body, count=None, turn=0):
            body(0, 0, False, True)
            before = count.n if count else 0
            with engine.Fori(0, (B - 2) // 2) as i:
                for k in range(2):
                    if count:
                        count.base = i * (2 * turn)
                    body(i * 2 + 1 + k, 1 - k, True, True)
                    if count:
                        assert count.n - before == (k + 1) * turn, (count.n - before, turn)
            if count:
                count.base, count.n = 0, before + (B - 2) * turn
            body(B - 1, 1, True, False)
            body(B, 0, True, None)

        def rows(ap, b):
            return ap[bass.ds(b, 1)].rearrange("a (t p) n -> p (a t) n", p=P)

        with nc.Block() as block:
            @block.sync
            def _(sp):
                def wait(s, value):
                    sp.wait_ge(s, value)
                    sp.sem_inc(passed, 1)

                def load_inputs(b):
                    if not isinstance(b, int) or b >= 1:
                        wait(inputs_free, b)
                    sp.dma_start(xn[:], rows(xn1, b)).then_inc(xn_loaded, 16)
                    sp.dma_start(ctx_sb[:], rows(ctx_in, b)).then_inc(ctx_loaded, 16)

                def parts_out(b, half, side):
                    n = 2 * half + side
                    wait(parts_ready, 4 * b + n + 1)
                    sp.dma_start(parts_dram[side, half].rearrange("s p n -> p s n"),
                                 parts[:, n]).then_inc(parts_stored[side], 16)

                def restack(b, par, half, side):
                    wait(parts_stored[side], 32 * b + 16 * half + 16)
                    heads = slice(half * H // 2, (half + 1) * H // 2)
                    stack, order = ((q_stack, Q_PARTS), (k_stack, K_PARTS))[side]
                    for first, end in ((0, 3), (3, 5), (5, 6)):
                        part = order[first]
                        n = end - first
                        channels = parts_dram[side, half].rearrange("s (d h) n -> s d (h n)", d=HD)
                        if side == 0:
                            src = channels[part:part + n]
                        else:
                            src = channels[part:part + 1].to_broadcast([n, HD, H // 2 * N])
                        sp.dma_start(stack[first * HD:end * HD, par, heads, :].rearrange("q h n -> q (h n)"), src) \
                          .then_inc(stacks_in[half], 16)

                def max_rows(b, par, half):
                    heads = slice(half * H // 2, (half + 1) * H // 2)
                    wait(neg_ready, 2 * b + half + 1)
                    sp.dma_start(neg_dram[:, half * MH * P:(half + 1) * MH * P].rearrange("s (r n) -> r s n", n=P),
                                 neg_parts[:]).then_inc(neg_stored, 16)
                    wait(neg_stored, 32 * b + 16 * half + 16)
                    sp.dma_start(q_stack[ROWS:ROWS + MAX_ROWS, par, heads, :],
                                 neg_dram.rearrange("s (h n) -> s h n", h=H)[:, heads]).then_inc(neg_in[half], 16)

                def outputs_in(b):
                    wait(o_stored[0], 96 * b + 96 + 48)
                    wait(o_stored[1], 96 * b + 96 + 48)
                    wait(o_used, b + 1)
                    sp.dma_start(sums[:], sum_dram.rearrange("h (q n) -> (h q) n", n=H * N // P)).then_inc(sums_loaded, 16)
                    sp.dma_start(o_cat[:], o_dram.rearrange("(t h) d n -> (h d) t n", t=TT)).then_inc(o_loaded, 16)
                    if not isinstance(b, int) or b >= 1:
                        wait(xn2T_ready, 2 * b)
                        wait(x2_stored, 32 * b + 32)
                    sp.dma_start(x_res[:], rows(x1, b)).then_inc(res_loaded, 16)

                def rsums_out(b):
                    if not isinstance(b, int) or b >= 1:
                        wait(r_loaded, 16 * b)
                    wait(rsums_ready, b + 1)
                    sp.dma_start(rsum_dram.rearrange("h (q n) -> (h q) n", n=H * N // P), rsums[:]).then_inc(rsums_moved, 16)

                def rsums_spread(b):
                    wait(rsums_moved, 32 * b + 16)
                    sp.dma_start(rsum16_dram, rsum_dram.unsqueeze(1).to_broadcast([H, HD, N])).then_inc(rsums_moved, 16)

                def rsums_in(b):
                    wait(rsums_moved, 32 * b + 32)
                    sp.dma_start(r_cat[:], rsum16_dram.rearrange("(t h) d n -> (h d) t n", t=TT)).then_inc(r_loaded, 16)

                def results_out(b):
                    wait(x2_ready, b + 1)
                    sp.dma_start(rows(x2, b), x2_sb[:]).then_inc(x2_stored, 16)
                    wait(xn2_ready, b + 1)
                    sp.dma_start(rows(xn2, b), xn2_sb[:]).then_inc(x2_stored, 16)

                load_inputs(0)
                for tile, src in ((w_q, wq), (w_k, wk), (w_v, wv), (w_m, wm)):
                    sp.dma_start(tile[:], src.rearrange("(c p) n -> p c n", p=P)).then_inc(consts_in, 16)
                for tile, src in ((bias_qk[:, 0:T], bq_rows), (bias_qk[:, T:2 * T], bk_rows), (bias_v[:], bv_rows)):
                    sp.dma_start(tile, src.to_broadcast([P, T])).then_inc(consts_in, 16)
                sp.dma_start(cos_f[:], enc[0].rearrange("(j p) d -> p j d", p=P)).then_inc(consts_in, 16)
                sp.dma_start(sin_f[:], enc[1].rearrange("(j p) d -> p j d", p=P)).then_inc(consts_in, 16)
                sp.dma_start(w_router[:], router_t.rearrange("(c p) e -> p c e", p=P)).then_inc(consts_in, 16)
                sp.dma_start(ident[:], ident_in).then_inc(consts_in, 16)
                sp.dma_start(bias_m[:], bm_cols).then_inc(consts_in, 16)
                for half in range(2):
                    for side in range(2):
                        parts_out(0, half, side)
                    for side in range(2):
                        restack(0, 0, half, side)

                def body(b, par, has_results, prev, nxt):
                    if nxt:
                        load_inputs(b + 1)
                    if has_results:
                        results_out(b - 2)
                    if nxt is not None:
                        max_rows(b, par, 0)
                    if prev:
                        outputs_in(b - 1)
                        rsums_out(b - 1)
                        rsums_spread(b - 1)
                        rsums_in(b - 1)
                    if nxt is not None:
                        max_rows(b, par, 1)
                    if nxt:
                        if prev:
                            wait(s_full, b * (2 * H))
                        for half in range(2):
                            for side in range(2):
                                parts_out(b + 1, half, side)
                            for side in range(2):
                                restack(b + 1, 1 - par, half, side)

                body(0, 0, False, False, True)
                body(1, 1, False, True, True)
                with sp.Fori(0, (B - 4) // 2) as i:
                    body(i * 2 + 2, 0, True, True, True)
                    body(i * 2 + 3, 1, True, True, True)
                body(B - 2, 0, True, True, True)
                body(B - 1, 1, True, True, False)
                body(B, 0, True, True, None)
                results_out(B - 1)
                wait(x2_stored, 32 * B + 32)

            @block.gpsimd
            def _(pool):
                pool.memset(half[:], -0.5).then_inc(half_ready, 1)
                pool.wait_ge(half_ready, 1)
                pool.memset(k_stack[ROWS:ROWS + MAX_ROWS], 1.0).then_inc(ones_ready, 1)
                pool.wait_ge(ones_ready, 1)

                def wait(s, value):
                    pool.wait_ge(s, value)
                    pool.sem_inc(pool_passed, 1)

                def remainder(b, h, m):
                    pair = 2 * h + m
                    if pair in BY_VECTOR:
                        return
                    pool.wait_ge(hi_ready, 2 * H * b + pair + 1)
                    at = pair % RING
                    pool.tensor_tensor(probs_lo[:, at], probs[:, at], probs_hi[:, at], ALU.subtract).then_inc(lo_ready, 1)

                def body(b, par, prev, nxt):
                    for h in range(H):
                        if nxt is not None:
                            for m in range(2):
                                remainder(b, h, m)
                        if h == 3 and prev:
                            wait(o_loaded, 16 * b)
                            pool.dma_start(o_cat[:], o_lo_dram.rearrange("(t h) d n -> (h d) t n", t=TT), accum_op=ALU.add) \
                                .then_inc(o_added, 16)
                        if h == 5 and prev:
                            pool.wait_ge(o_added, 16 * b)
                            pool.wait_ge(r_loaded, 16 * b)
                            pool.tensor_tensor(o_cat[:], o_cat[:], r_cat[:], ALU.mult).then_inc(o_ready, 1)
                        if h == 7 and prev:
                            pool.wait_ge(var2_ready, b)
                            pool.tensor_tensor(rstd2[:], var_eps2[:], half[:], ALU.pow).then_inc(rstd2_ready, 1)

                batches(pool, body)

            @block.scalar
            def _(act):
                for s in o_stored:
                    act.sem_inc(s, 48)
                act.sem_inc(e_ready, 2)
                act.sem_inc(o_kept, 2)

                def exps(b, par, h, m):
                    pair = 2 * h + m
                    act.wait_ge(s_full, 2 * H * b + pair + 1)
                    act.wait_ge(pv_done, 2 * H * b + pair + 1)
                    act.activation(probs[:, pair % RING], ps_s[m][:].rearrange("p (m n) -> p m n", m=2),
                                   ACT.Exp, scale=HD ** -0.5).then_inc(e_ready, 1)

                def rounded(b, h, m):
                    pair = 2 * h + m
                    act.wait_ge(e_ready, 2 * H * b + pair + 3)
                    act.copy(probs_hi[:, pair % RING], probs[:, pair % RING]).then_inc(hi_ready, 1)

                def keep(b, h, first):
                    g = h // 4
                    stored = o_stored[g % 2]
                    if h % 4 == 0:
                        act.wait_ge(stored, 96 * b + 48 * (g // 2) + 48)
                    act.wait_ge(pv_done, 2 * H * b + 2 * h + 2 + RING)
                    act.copy(o_sb[:, g % 2, h % 4, :], ps_o[h % 2][0:VH, :]).then_inc(o_kept, 1)
                    if h % 4 == 3:
                        if g == 0 and not first:
                            act.wait_ge(o_added, 16 * b)
                            act.wait_ge(sums_loaded, 16 * b)
                        act.wait_ge(o_kept, H * b + h + 3)
                        heads = slice(4 * g, 4 * g + 4)
                        act.dma_start(o_dram[heads].rearrange("h d n -> d h n"), o_sb[0:HD, g % 2]).then_inc(stored, 16)
                        act.dma_start(sum_dram[heads].unsqueeze(0), o_sb[HD:HD + 1, g % 2]).then_inc(stored, 16)
                        act.dma_start(o_lo_dram[heads].rearrange("h d n -> d h n"), o_sb[HD + 1:VH, g % 2]).then_inc(stored, 16)

                def body(b, par, prev, nxt):
                    for h in range(H):
                        if nxt is not None:
                            for m in range(2):
                                exps(b, par, h, m)
                                rounded(b, h, m)
                        if (prev if h < LAG else nxt is not None):
                            before, _, head = head_before(b, par, h)
                            keep(before, head, not prev)

                batches(act, body)

            @block.tensor
            def _(pe):
                uses = Count(pe, w_full)

                def bank():
                    pe.wait_ge(w_free, uses.base + uses.n + 1)
                    return ps_w[uses.n % 2]

                def project_qk(b, j):
                    w = bank()
                    for side, (src, weight) in enumerate(((xn, w_q), (ctx_sb, w_k))):
                        for c in range(TT):
                            last = pe.matmul(w[:, side * T:(side + 1) * T], src[:, c, j * P:(j + 1) * P], weight[:, c, :],
                                             start=(c == 0), stop=(c == TT - 1))
                    uses.inc(last)

                def project_v(b, i):
                    w = bank()
                    for k in range(2):
                        j = 2 * i + k
                        for c in range(TT):
                            last = pe.matmul(w[:, k * T:(k + 1) * T], ctx_sb[:, c, j * P:(j + 1) * P], w_v[:, c, :],
                                             start=(c == 0), stop=(c == TT - 1))
                    uses.inc(last)

                def transpose_qk(b, t):
                    if t == 0:
                        pe.wait_ge(rot_ready, 4 * b + 4)
                    w = bank()
                    half, side = t // 2, t % 2
                    block = 2 * side + half
                    for j in range(NJ):
                        last = pe.transpose(w[:, j * P:(j + 1) * P], qk_rot[:, j, block * P:(block + 1) * P], ident[:])
                    uses.inc(last)

                def maxima(b, par, h, j):
                    if h % (H // 2) == 0 and j == 0:
                        pe.wait_ge(stacks_in[h // (H // 2)], 96 * b + 96)
                    w = bank()
                    uses.inc(pe.matmul(w[:], q_stack[0:ROWS, par, h, j * P:(j + 1) * P], k_stack[0:ROWS, par, h, :],
                                       start=True, stop=True))

                def transpose_max(b, half):
                    pe.wait_ge(max_ready, 2 * b + half + 1)
                    w = bank()
                    uses.inc(pe.transpose(w[:, 0:P], row_max[:, half, :], ident[:]))

                def scores(b, par, h, j):
                    m = j // 2
                    if h % (H // 2) == 0 and j == 0:
                        pe.wait_ge(neg_in[h // (H // 2)], 16 * b + 16)
                    if h == 0 and j == 0:
                        pe.wait_ge(v_ready, 2 * b + 2)
                    if j % 2 == 0:
                        pe.wait_ge(e_ready, 2 * H * b + 2 * h + m + 1)
                    last = pe.matmul(ps_s[m][:, (j % 2) * N:(j % 2 + 1) * N], k_stack[:, par, h, j * P:(j + 1) * P],
                                     q_stack[:, par, h, :], start=True, stop=True)
                    if j % 2:
                        last.then_inc(s_full, 1)

                def probs_v(b, par, h, j):
                    m, k = j // 2, j % 2
                    pair = 2 * h + m
                    if j == 0:
                        pe.wait_ge(o_kept, H * b + h + 1)
                    if k == 0:
                        pe.wait_ge(*remainder_ready(b, pair))
                    v = v_sb[:, par, j, h, :]
                    pe.matmul(ps_o[h % 2][0:VH, :], v, probs_hi[:, pair % RING, k, :], start=(j == 0), stop=False)
                    last = pe.matmul(ps_o[h % 2][0:VH, :], v, probs_lo[:, pair % RING, k, :], start=False, stop=(j == NJ - 1))
                    if k:
                        last.then_inc(pv_done, 1)

                def merge(b, t):
                    if t == 0:
                        pe.wait_ge(o_ready, b + 1)
                    w = bank()
                    for c in range(TT):
                        last = pe.matmul(w[:], w_m[:, c, t * P:(t + 1) * P], o_cat[:, c, :], start=(c == 0), stop=(c == TT - 1))
                    uses.inc(last)

                def transpose_xn2(b, t):
                    if t == 0:
                        pe.wait_ge(xn2_ready, b + 1)
                    w = bank()
                    for c in range(HC):
                        last = pe.transpose(w[:, c * P:(c + 1) * P], xn2_sb[:, t, c * P:(c + 1) * P], ident[:])
                    uses.inc(last)

                def route(b):
                    pe.wait_ge(xn2T_ready, 2 * b + 2)
                    w = bank()
                    for t in range(TT):
                        for c in range(HC):
                            last = pe.matmul(w[:, t * 8:(t + 1) * 8], xn2_T[:, t, c, :], w_router[:, c, :],
                                             start=(c == 0), stop=(c == HC - 1))
                    uses.inc(last)

                def step(name, k, b, par):
                    if name == "qk":
                        if k == 0:
                            pe.wait_ge(xn_loaded, 16 * b + 16)
                            pe.wait_ge(ctx_loaded, 16 * b + 16)
                        project_qk(b, k)
                    elif name == "split":
                        transpose_qk(b, k)
                    elif name == "v":
                        project_v(b, k)
                    elif name == "max":
                        maxima(b, par, k // NJ, k % NJ)
                    elif name == "neg":
                        transpose_max(b, k)
                    elif name == "merge":
                        merge(b, k)
                    elif name == "turn2":
                        transpose_xn2(b, k)
                    elif name == "route":
                        route(b)

                def body(b, par, prev, nxt):
                    for h in range(H):
                        main = []
                        for m in range(2):
                            if (prev if h < LAG else nxt is not None):
                                main += [("probs_v", 2 * m, 0), ("probs_v", 2 * m + 1, 0)]
                            if nxt is not None:
                                main += [("scores", 2 * m, 0), ("scores", 2 * m + 1, 0)]
                        beside = [s for s in steps_beside(h, prev, nxt is not None, nxt) if s[0] != "remainder"]
                        for name, k, off in interleaved(main, beside):
                            if name == "scores":
                                scores(b, par, h, k)
                            elif name == "probs_v":
                                probs_v(*head_before(b, par, h), k)
                            else:
                                step(name, k, b + off, (par + off) % 2)

                pe.wait_ge(consts_in, 16 * 12)
                for h in range(H):
                    for name, k, _ in steps_beside(h, False, False, True):
                        step(name, k, 0, 0)
                pe.wait_ge(ones_ready, 1)
                batches(pe, body, uses, USES)

            @block.vector
            def _(dve):
                chain = Count(dve, s_dve)
                taken = Count(dve, w_free)

                def bank():
                    dve.wait_ge(w_full, taken.base + taken.n + 1)
                    return ps_w[taken.n % 2]

                def pairs_of(ap):
                    return ap.rearrange("p (g k r h) -> p g k r h", g=4, r=2, h=H // 2)

                def rotate(b, j):
                    w = bank()
                    mark = taken.inc(dve.tensor_tensor(qk_b[:], w[:], bias_qk[:], ALU.add))
                    taken.wait(mark + 2)
                    dve.tensor_tensor(rot[:, 0].rearrange("p (g d h) -> p g d h", g=4, d=HD),
                                      qk_b[:].rearrange("p (g d h) -> p g d h", g=4, d=HD),
                                      cos_f[:, j, :].unsqueeze(1).unsqueeze(3).to_broadcast([P, 4, HD, H // 2]), ALU.mult)
                    t, o = pairs_of(qk_b[:]), pairs_of(rot[:, 1])
                    sin = sin_f[:, j, :].rearrange("p (k r) -> p k r", r=2)
                    for r in range(2):
                        last = dve.tensor_tensor(o[:, :, :, r], t[:, :, :, 1 - r],
                                                 sin[:, :, r].unsqueeze(1).unsqueeze(3).to_broadcast([P, 4, HD // 2, H // 2]),
                                                 ALU.mult)
                    chain.link(last)
                    dve.tensor_tensor(qk_rot[:, j, :], rot[:, 0], rot[:, 1], ALU.add).then_inc(rot_ready, 1)

                def split(b, t):
                    w = bank()
                    if t == 0 and (not isinstance(b, int) or b >= 1):
                        for side in range(2):
                            dve.wait_ge(parts_stored[side], 32 * b)
                    p = parts[:, t]
                    chain.link(dve.tensor_copy(p[:, 0, :], w[:]))
                    mark = taken.inc(dve.tensor_tensor(qk_b[:], w[:], p[:, 0, :], ALU.subtract))
                    taken.wait(mark + 2)
                    chain.link(dve.tensor_copy(p[:, 1, :], qk_b[:]))
                    dve.tensor_tensor(p[:, 2, :], qk_b[:], p[:, 1, :], ALU.subtract).then_inc(parts_ready, 1)
                    dve.wait_ge(parts_ready, 4 * b + t + 1)

                def keep_v(b, par, i):
                    w = bank()
                    mark = taken.inc(dve.tensor_tensor(
                        v_full, w[:].rearrange("p (j h d) -> p j h d", j=2, d=HD),
                        bias_v[:].rearrange("p (h d) -> p h d", d=HD).unsqueeze(1).to_broadcast([P, 2, H, HD]), ALU.add))
                    taken.wait(mark + 2)
                    v = v_sb[:, par, 2 * i:2 * i + 2]
                    chain.link(dve.tensor_copy(v[:, :, :, 0:HD], v_full))
                    chain.link(dve.tensor_tensor(v[:, :, :, HD + 1:VH], v_full, v[:, :, :, 0:HD], ALU.subtract))
                    dve.sem_inc(v_ready, 1)
                    if i == 1:
                        dve.sem_inc(inputs_free, 1)

                def reduce_max(b, h, j):
                    w = bank()
                    at = h % (H // 2) * NJ + j
                    mark = taken.inc(dve.tensor_reduce(row_max[:, h // (H // 2), at:at + 1], w[:], AX.X, ALU.max))
                    if h % (H // 2) == H // 2 - 1 and j == NJ - 1:
                        taken.wait(mark + 2)
                        dve.sem_inc(max_ready, 1)

                def negate_max(b, half):
                    w = bank()[0:MH, 0:P]
                    if half or not isinstance(b, int) or b >= 1:
                        dve.wait_ge(neg_stored, 32 * b + 16 * half)
                    chain.link(dve.tensor_scalar(neg_parts[:, 0, :], w, -1.0, None, ALU.mult))
                    mark = taken.inc(dve.scalar_tensor_tensor(neg_rest[:], w, -1.0, neg_parts[:, 0, :], ALU.mult, ALU.subtract))
                    taken.wait(mark + 2)
                    chain.link(dve.tensor_copy(neg_parts[:, 1, :], neg_rest[:]))
                    dve.tensor_tensor(neg_parts[:, 2, :], neg_rest[:], neg_parts[:, 1, :], ALU.subtract).then_inc(neg_ready, 1)

                def reciprocals(b):
                    dve.wait_ge(sums_loaded, 16 * b + 16)
                    dve.reciprocal(rsums[:], sums[:]).then_inc(rsums_ready, 1)

                def residual(b, t):
                    if t == 0:
                        dve.wait_ge(res_loaded, 16 * b + 16)
                        dve.wait_ge(x2_stored, 32 * b + 32)
                    w = bank()
                    mark = taken.inc(dve.scalar_tensor_tensor(x2_sb[:, t, :], w[:], bias_m[:, t:t + 1], x_res[:, t, :],
                                                              ALU.add, ALU.add))
                    if t < TT - 1:
                        return
                    taken.wait(mark + 2)
                    dve.sem_inc(x2_ready, 1)
                    dve.sem_inc(o_used, 1)
                    chain.link(layer_norm_stats(dve, chain, x2_sb, stats2, mean_var2))
                    dve.tensor_scalar(var_eps2[:], mean_var2[:, :, 1], LN_EPS, None, ALU.add).then_inc(var2_ready, 1)

                def norm2_apply(b):
                    dve.wait_ge(rstd2_ready, b + 1)
                    for t in range(TT):
                        last = dve.tensor_scalar(xn2_sb[:, t, :], x2_sb[:, t, :], mean_var2[:, t, 0:1], rstd2[:, t:t + 1],
                                                 ALU.subtract, ALU.mult)
                    last.then_inc(xn2_ready, 1)

                def keep_xn2_T(b, t):
                    w = bank()
                    taken.inc(dve.tensor_copy(xn2_T[:, t], w[:].rearrange("p (c q) -> p c q", c=HC)))
                    taken.wait(taken.base + taken.n + 2)
                    dve.sem_inc(xn2T_ready, 1)

                def remainder(b, h):
                    pair = 2 * h + 1
                    at = pair % RING
                    dve.wait_ge(hi_ready, 2 * H * b + pair + 1)
                    dve.tensor_tensor(probs_lo[:, at], probs[:, at], probs_hi[:, at], ALU.subtract).then_inc(lo2_ready, 1)

                def keep_logits(b):
                    w = bank()
                    taken.inc(dve.tensor_copy(logits[:, bass.ds(b * TT, TT), :],
                                              w[:, 0:TT * 8].rearrange("p (t e) -> p t e", t=TT)))

                TURN = 4 + 4 * 2 + 4 + 2 * 2 + 3

                def step(name, k, b, par):
                    if name == "qk":
                        rotate(b, k)
                    elif name == "split":
                        split(b, k)
                    elif name == "v":
                        keep_v(b, par, k)
                    elif name == "max":
                        reduce_max(b, k // NJ, k % NJ)
                    elif name == "neg":
                        negate_max(b, k)
                    elif name == "merge":
                        residual(b, k)
                    elif name == "norm2":
                        norm2_apply(b)
                    elif name == "turn2":
                        keep_xn2_T(b, k)
                    elif name == "route":
                        keep_logits(b)
                    elif name == "remainder":
                        remainder(b, k)

                def body(b, par, prev, nxt):
                    first = chain.n
                    for h in range(H):
                        if h == 3 and prev:
                            reciprocals(b - 1)
                        for name, k, off in steps_beside(h, prev, nxt is not None, nxt):
                            step(name, k, b + off, (par + off) % 2)
                    return chain.n - first

                chain.link(dve.memset(v_full, 1.0))
                for par in range(2):
                    chain.inc(dve.tensor_copy(v_sb[:, par, :, :, HD], v_full[:, 0, 0:NJ, :].rearrange("p j h -> p j h")))
                chain.link(dve.memset(row_max[:], 0.0))
                for s, n in ((w_free, 2), (pv_done, RING), (o_used, 1), (x2_stored, 32)):
                    dve.sem_inc(s, n)
                dve.wait_ge(consts_in, 16 * 12)
                for j in range(NJ):
                    even = sin_f[:, j, :].rearrange("p (k r) -> p k r", r=2)[:, :, 0]
                    last = chain.inc(dve.tensor_scalar(even, even, -1.0, None, ALU.mult))
                chain.wait(last)
                for h in range(H):
                    for name, k, _ in steps_beside(h, False, False, True):
                        step(name, k, 0, 0)

                body(0, 0, False, True)
                before, used = chain.n, taken.n
                with dve.Fori(0, (B - 2) // 2) as i:
                    for k in range(2):
                        chain.base, taken.base = i * (2 * TURN), i * (2 * USES)
                        assert body(i * 2 + 1 + k, 1 - k, True, True) == TURN
                chain.base, chain.n = 0, before + (B - 2) * TURN
                taken.base, taken.n = 0, used + (B - 2) * USES
                body(B - 1, 1, True, False)
                body(B, 0, True, None)


E = 8
TOP = 2
F = 352
FC = (F + P - 1) // P
TOKENS = B * T
TILES = TOKENS // P
PAIRS = TOP * TILES
BLOCKS = PAIRS + E - 1
NOBODY = 2 * TOKENS


def build_stage_c(nc, xn2, logits, w1_t, w2_t, ident_in, before_in, numbers_in, out):
    with ExitStack() as ctx:
        def sb(name, shape, dt=FP32):
            return ctx.enter_context(nc.sbuf_tensor("c_" + name, shape, dt))

        def pb(name, shape=(P, 512), dt=FP32):
            return ctx.enter_context(nc.psum_tensor("c_" + name, list(shape), dt))

        def sem(name):
            return ctx.enter_context(nc.semaphore("c_" + name))

        W1 = HC * 2 * F
        W2 = FC * HID
        w1_sb = sb("w1", [P, E * W1])
        w2_sb = sb("w2", [P, E * W2])
        w1_hi = sb("w1_hi", [P, HC, 2 * F], FP32R)
        w1_lo = sb("w1_lo", [P, HC, 2 * F], FP32R)
        w2_hi = sb("w2_hi", [P, FC, HID], FP32R)
        w2_lo = sb("w2_lo", [P, FC, HID], FP32R)
        ident = sb("ident", [P, P])
        before = sb("before", [P, 2, P])
        numbers = sb("numbers", [P, P])
        token = sb("token", [P, TILES])
        best_at = sb("best_at", [P, TILES, E], U32)
        choice = sb("choice", [P, TOP, TILES])
        gap = sb("gap", [P, TILES])
        gate = sb("gate", [P, TOP, TILES])
        ones = sb("ones", [P, TILES])
        count_i = sb("count_i", [P, E], I32)
        n_blocks = sb("n_blocks", [P, E])
        block_end = sb("block_end", [P, E])
        start = sb("start", [P, E])
        place = sb("place", [P, TILES, E])
        pos = sb("pos", [P, TOP, TILES])
        pos_i = sb("pos_i", [P, TOP, TILES], I32)
        part_i = sb("part_i", [P, 2, TOP, TILES], I32)
        block_row = sb("block_row", [P, 2, TOP, TILES])
        expert = sb("expert", [1, BLOCKS])
        expert_i = sb("expert_i", [1, BLOCKS], I32)
        ids = sb("ids", [P, BLOCKS], I32)
        gates = sb("gates", [P, BLOCKS])
        id_in = sb("id_in", [P, 2], I32)
        id_out = sb("id_out", [P, 2], I32)
        xb = sb("xb", [P, 2, HID])
        xbT_hi = sb("xbT_hi", [P, 2, HC, P], FP32R)
        xbT_lo = sb("xbT_lo", [P, 2, HC, P], FP32R)
        silu = sb("silu", [P, 2, F])
        hidden = sb("hidden", [P, 2, FC * P])
        hiddenT_hi = sb("hiddenT_hi", [P, FC, P], FP32R)
        hiddenT_lo = sb("hiddenT_lo", [P, FC, P], FP32R)
        yb = sb("yb", [P, 2, HID])

        def over(buffer, first, rows, shape):
            size = 1
            for n in shape:
                size *= n
            flat = buffer[0:rows].rearrange("p k n -> p (k n)")[:, first:first + size]
            names = "abc"[:len(shape)]
            return flat.rearrange(f"p ({' '.join(names)}) -> p {' '.join(names)}", **dict(zip(names, shape)))

        best = over(xb, 0, P, (TILES, E))
        both = over(xb, TILES * E, P, (TILES, E))
        chosen = over(xb, 2 * TILES * E, P, (TOP, TILES, E))
        hot = over(xb, 0, P, (4, BLOCKS))
        in_tile = over(yb, 0, P, (E, TILES))
        ge = over(yb, E * TILES, 1, (BLOCKS, E))
        up_to = over(hidden, 0, P, (E, TILES))
        is_row = over(hidden, E * TILES, P, (4, P))
        in_block = over(silu, 0, P, (4, 2, BLOCKS))

        ps_g = [pb(f"ps_g{i}") for i in range(2)]
        ps_u = [pb(f"ps_u{i}") for i in range(2)]
        ps_y = [pb(f"ps_y{i}") for i in range(2)]
        ps_xT, ps_hT = pb("ps_xT"), pb("ps_hT")

        consts_in, w_in = sem("consts_in"), sem("w_in")
        token_ready = sem("token_ready")
        gap_ready, gate_ready = sem("gap_ready"), sem("gate_ready")
        both_ready, ranks_full = sem("both_ready"), sem("ranks_full")
        onehots, onehots_used = sem("onehots"), sem("onehots_used")
        experts_ready = sem("experts_ready")
        plan_ready = sem("plan_ready")
        gathered = [sem(f"gathered{i}") for i in range(2)]
        scattered = sem("scattered")
        xT_full, xT_ready = sem("xT_full"), sem("xT_ready")
        g_full, silu_ready, hidden_ready = sem("g_full"), sem("silu_ready"), sem("hidden_ready")
        hT_full, hT_ready, y_ready = sem("hT_full"), sem("hT_ready"), sem("y_ready")
        id_ready, id_out_ready = sem("id_ready"), sem("id_out_ready")
        w1_rounded, w1_split, w1_split_last, w1_used = sem("w1_rounded"), sem("w1_split"), sem("w1_split_last"), sem("w1_used")
        w2_rounded, w2_split, w2_split_last, w2_used = sem("w2_rounded"), sem("w2_split"), sem("w2_split_last"), sem("w2_used")
        xT_rounded, hT_rounded = sem("xT_rounded"), sem("hT_rounded")
        s_dve = sem("dve")
        passed = sem("passed")
        assert (BLOCKS - 5) % 2 == 0

        def done(i):
            return i + 3

        def up_done(i):
            return HC * i + 2 * HC

        def down_done(i):
            return FC * i + 2 * FC

        def expert_of(engine, i):
            return engine.value_load(expert_i[0:1, bass.ds(i, 1)], min_val=0, max_val=E - 1)

        def w1_chunk(e, c):
            return w1_sb[:, bass.ds(e * W1 + c * 2 * F, 2 * F)]

        def w2_chunk(e, c):
            return w2_sb[0:rows_of(c), bass.ds(e * W2 + c * HID, HID)]

        def rows_of(c):
            return min(P, F - c * P)

        def blocks(engine, body):
            body(0, 0, False, True, True)
            body(1, 1, True, True, True)
            body(2, 0, True, True, True)
            with engine.Fori(0, (BLOCKS - 5) // 2) as n:
                body(n * 2 + 3, 1, True, True, True)
                body(n * 2 + 4, 0, True, True, True)
            body(BLOCKS - 2, (BLOCKS - 2) % 2, True, True, False)
            body(BLOCKS - 1, (BLOCKS - 1) % 2, True, False, False)
            body(BLOCKS, BLOCKS % 2, True, None, False)

        with nc.Block() as block:
            @block.sync
            def _(sp):
                sp.dma_start(ident[:], ident_in).then_inc(consts_in, 16)
                sp.dma_start(before[:], before_in).then_inc(consts_in, 16)
                sp.dma_start(numbers[:], numbers_in).then_inc(consts_in, 16)
                for e in range(E):
                    sp.dma_start(w1_sb[:, e * W1:(e + 1) * W1].rearrange("p (c n) -> p c n", c=HC),
                                 w1_t[e].rearrange("(c p) n -> p c n", p=P)).then_inc(w_in, 16)
                    for c in range(FC):
                        k = min(P, F - c * P)
                        sp.dma_start(w2_sb[0:k, e * W2 + c * HID:e * W2 + (c + 1) * HID],
                                     w2_t[e, c * P:c * P + k, :]).then_inc(w_in, 16)

            @block.gpsimd
            def _(pool):
                pool.iota(token[:], [[P, TILES]], base=-NOBODY, channel_multiplier=1,
                          allow_small_or_imprecise_dtypes=True).then_inc(token_ready, 1)

                def wait(s, value):
                    pool.wait_ge(s, value)
                    pool.sem_inc(passed, 1)

                def gather(i, par):
                    wait(xT_full, done(i - 2))
                    pool.tensor_copy(id_in[:, par:par + 1], ids[:, bass.ds(i, 1)]).then_inc(id_ready, 1)
                    wait(id_ready, i + 1)
                    pool.indirect_dma_start(xb[:, par, :], None, xn2, bass.IndirectOffsetOnAxis(ap=id_in[:, par:par + 1].bitcast(U32), axis=0),
                                            bounds_check=last_token, oob_is_err=False).then_inc(gathered[par], 16)

                def scatter(i, par):
                    if not isinstance(i, int) or i >= 1:
                        wait(scattered, 16 * i)
                    pool.tensor_copy(id_out[:, par:par + 1], ids[:, bass.ds(i, 1)]).then_inc(id_out_ready, 1)
                    wait(id_out_ready, i + 1)
                    wait(y_ready, done(i))
                    pool.indirect_dma_start(out, bass.IndirectOffsetOnAxis(ap=id_out[:, par:par + 1].bitcast(U32), axis=0), yb[:, par, :], None,
                                            bounds_check=last_token, oob_is_err=False, compute_op=ALU.add).then_inc(scattered, 16)

                def split_w1_last(i):
                    e = expert_of(pool, i)
                    wait(w1_rounded, HC * i + HC)
                    pool.tensor_tensor(w1_lo[:, HC - 1, :], w1_chunk(e, HC - 1), w1_hi[:, HC - 1, :], ALU.subtract) \
                        .then_inc(w1_split_last, 1)

                def split_w2_last(i):
                    c = FC - 1
                    e = expert_of(pool, i)
                    wait(w2_rounded, FC * i + FC)
                    pool.tensor_tensor(w2_lo[0:rows_of(c), c, :], w2_chunk(e, c), w2_hi[0:rows_of(c), c, :], ALU.subtract) \
                        .then_inc(w2_split_last, 1)

                def body(i, par, prev, nxt, nxt2):
                    if prev and (not isinstance(i, int) or i >= 2):
                        scatter(i - 2, par)
                    if prev:
                        split_w2_last(i - 1)
                    if nxt2:
                        gather(i + 2, par)
                    if nxt:
                        split_w1_last(i + 1)

                last_token = pool.to_reg(TOKENS - 1)
                pool.wait_ge(plan_ready, 1)
                gather(0, 0)
                gather(1, 1)
                split_w1_last(0)
                blocks(pool, body)
                scatter(BLOCKS - 1, (BLOCKS - 1) % 2)
                pool.wait_ge(scattered, 16 * BLOCKS)

            @block.tensor
            def _(pe):
                pe.wait_ge(consts_in, 48)
                pe.wait_ge(both_ready, 1)
                o = both.rearrange("p t e -> p (t e)")
                pe.matmul(ps_g[0][:, 0:TILES * E], before[:, 0, :], o, start=True, stop=True)
                pe.matmul(ps_g[1][:, 0:TILES * E], before[:, 1, :], o, start=True, stop=True).then_inc(ranks_full, 1)
                for n in range(PAIRS):
                    if n % 2 == 0:
                        pe.wait_ge(onehots, n // 2 + 1)
                    last = pe.matmul(ps_y[0][:, 0:2 * BLOCKS], is_row[:, n % 4, :], in_block[:, n % 4].rearrange("p k n -> p (k n)"),
                                     start=(n == 0), stop=(n == PAIRS - 1))
                    if n % 2:
                        last.then_inc(onehots_used, 1)

                def transpose_x(i, par):
                    pe.wait_ge(gathered[par], gathers_of(i, par))
                    pe.wait_ge(xT_ready, done(i - 1))
                    for c in range(HC):
                        last = pe.transpose(ps_xT[:, c * P:(c + 1) * P], xb[:, par, c * P:(c + 1) * P], ident[:])
                    last.then_inc(xT_full, 1)

                def gathers_of(i, par):
                    return (i - par) * 8 + 16

                def up(i, par, chunks):
                    if 0 in chunks:
                        pe.wait_ge(xT_ready, done(i))
                        pe.wait_ge(silu_ready, done(i - 2))
                        pe.wait_ge(hidden_ready, done(i - 2))
                    for c in chunks:
                        if c == HC - 1:
                            pe.wait_ge(w1_split_last, i + 1)
                        else:
                            pe.wait_ge(w1_split, (HC - 1) * i + c + 1)
                        for half, ps in enumerate((ps_g, ps_u)):
                            x, w = xbT_hi[:, par, c, :], w1_hi[:, c, half * F:(half + 1) * F]
                            pe.matmul(ps[par][:, 0:F], x, w, start=(c == 0), stop=False)
                            pe.matmul(ps[par][:, 0:F], x, w1_lo[:, c, half * F:(half + 1) * F], start=False, stop=False)
                            last = pe.matmul(ps[par][:, 0:F], xbT_lo[:, par, c, :], w, start=False, stop=(c == HC - 1))
                            if c == HC - 1 and half == 0:
                                last.then_inc(g_full, 1)
                        last.then_inc(w1_used, 1)

                def transpose_hidden(i, par):
                    pe.wait_ge(hidden_ready, done(i))
                    pe.wait_ge(hT_ready, done(i - 1))
                    for c in range(FC):
                        last = pe.transpose(ps_hT[:, c * P:(c + 1) * P], hidden[:, par, c * P:(c + 1) * P], ident[:])
                    last.then_inc(hT_full, 1)

                def down(i, par):
                    pe.wait_ge(hT_ready, done(i))
                    pe.wait_ge(y_ready, done(i - 2))
                    for c in range(FC):
                        if c == FC - 1:
                            pe.wait_ge(w2_split_last, i + 1)
                        else:
                            pe.wait_ge(w2_split, (FC - 1) * i + c + 1)
                        k = rows_of(c)
                        hidden_hi, w = hiddenT_hi[0:k, c, :], w2_hi[0:k, c, :]
                        pe.matmul(ps_y[par][:, :], hidden_hi, w, start=(c == 0), stop=False)
                        pe.matmul(ps_y[par][:, :], hidden_hi, w2_lo[0:k, c, :], start=False, stop=False)
                        pe.matmul(ps_y[par][:, :], hiddenT_lo[0:k, c, :], w, start=False, stop=(c == FC - 1)).then_inc(w2_used, 1)

                def body(i, par, prev, nxt, nxt2):
                    if nxt is not None:
                        up(i, par, (0, 1))
                    if prev:
                        transpose_hidden(i - 1, 1 - par)
                    if nxt:
                        transpose_x(i + 1, 1 - par)
                    if nxt is not None:
                        up(i, par, (2, 3))
                    if prev:
                        down(i - 1, 1 - par)

                pe.wait_ge(plan_ready, 1)
                transpose_x(0, 0)
                blocks(pe, body)

            @block.scalar
            def _(act):
                act.wait_ge(gap_ready, 1)
                act.activation(gate[:, 1, :], gap[:], ACT.Exp).then_inc(gate_ready, 1)

                def keep_xT(i, par):
                    act.wait_ge(xT_full, done(i))
                    if not isinstance(i, int) or i >= 2:
                        act.wait_ge(w1_used, up_done(i - 2))
                    act.copy(xbT_hi[:, par], ps_xT[:].rearrange("p (c q) -> p c q", c=HC)).then_inc(xT_rounded, 1)

                def keep_hT(i):
                    act.wait_ge(hT_full, done(i))
                    act.wait_ge(w2_used, down_done(i - 1))
                    act.copy(hiddenT_hi[:], ps_hT[:, 0:FC * P].rearrange("p (c q) -> p c q", c=FC)).then_inc(hT_rounded, 1)

                def round_w1(i, e, c):
                    act.wait_ge(w1_used, HC * i + c + 1)
                    act.copy(w1_hi[:, c, :], w1_chunk(e, c)).then_inc(w1_rounded, 1)

                def round_w2(i, e, c):
                    act.wait_ge(w2_used, FC * i + c + 1)
                    act.copy(w2_hi[0:rows_of(c), c, :], w2_chunk(e, c)).then_inc(w2_rounded, 1)

                def body(i, par, prev, nxt, nxt2):
                    if nxt:
                        e_next = expert_of(act, i + 1)
                        round_w1(i + 1, e_next, 0)
                        round_w1(i + 1, e_next, 1)
                    if prev:
                        keep_hT(i - 1)
                    if nxt:
                        keep_xT(i + 1, 1 - par)
                        round_w1(i + 1, e_next, 2)
                        round_w1(i + 1, e_next, 3)
                    if nxt is not None:
                        act.wait_ge(g_full, done(i))
                        act.wait_ge(hidden_ready, done(i - 2))
                        act.activation(silu[:, par, :], ps_g[par][:, 0:F], ACT.Silu).then_inc(silu_ready, 1)
                        e = expert_of(act, i)
                        for c in range(FC):
                            round_w2(i, e, c)

                act.wait_ge(experts_ready, 1)
                act.wait_ge(w_in, 16 * (1 + FC) * E)
                first = expert_of(act, 0)
                for c in range(HC):
                    round_w1(0, first, c)
                keep_xT(0, 0)
                blocks(act, body)

            @block.vector
            def _(dve):
                chain = Count(dve, s_dve)
                for s in (xT_full, xT_rounded, xT_ready, g_full, silu_ready, hidden_ready, hT_full, hT_rounded, hT_ready,
                          y_ready):
                    dve.sem_inc(s, 2)
                dve.sem_inc(w1_used, HC)
                dve.sem_inc(w2_used, FC)
                chain.link(dve.memset(ones[:], 1.0))
                for t in range(TILES):
                    last = chain.inc(dve.max(best[:, t, :], logits[:, t, :]))
                chain.wait(last)
                for t in range(TILES):
                    last = chain.inc(dve.max_index(best_at[:, t, :], best[:, t, :], logits[:, t, :]))
                dve.tensor_tensor(gap[:], best[:, :, 1], best[:, :, 0], ALU.subtract).then_inc(gap_ready, 1)
                chain.wait(last)
                for k in range(TOP):
                    last = chain.inc(dve.tensor_copy(choice[:, k, :], best_at[:, :, k]))
                chain.wait(last)
                dve.wait_ge(consts_in, 48)
                each = numbers[:, 0:E].unsqueeze(1).to_broadcast([P, TILES, E])
                for k in range(TOP):
                    last = chain.inc(dve.tensor_tensor(chosen[:, k], choice[:, k, :].unsqueeze(2).to_broadcast([P, TILES, E]), each, ALU.is_equal))
                chain.wait(last)
                dve.tensor_tensor(both, chosen[:, 0], chosen[:, 1], ALU.add).then_inc(both_ready, 1)
                dve.wait_ge(gate_ready, 1)
                chain.link(dve.tensor_scalar(gap[:], gate[:, 1, :], 1.0, None, ALU.add))
                chain.link(dve.reciprocal(gate[:, 0, :], gap[:]))
                chain.link(dve.tensor_tensor(gate[:, 1, :], gate[:, 1, :], gate[:, 0, :], ALU.mult))
                dve.wait_ge(ranks_full, 1)
                chain.link(dve.tensor_copy(in_tile, ps_g[1][:, 0:TILES * E].rearrange("p (t e) -> p e t", e=E)))
                for e in range(E):
                    last = chain.inc(dve.tensor_tensor_scan(up_to[:, e, :], ones[:], in_tile[:, e, :], 0.0, ALU.mult, ALU.add))
                chain.wait(last)
                chain.link(dve.tensor_scalar(count_i[:], up_to[:, :, TILES - 1], float(P - 1), None, ALU.add))
                chain.link(dve.tensor_scalar(count_i[:], count_i[:], P.bit_length() - 1, None, ALU.logical_shift_right))
                chain.link(dve.tensor_copy(n_blocks[:], count_i[:]))
                chain.link(dve.tensor_tensor_scan(block_end[:], ones[:, 0:E], n_blocks[:], 0.0, ALU.mult, ALU.add))
                chain.link(dve.tensor_tensor(start[:], block_end[:], n_blocks[:], ALU.subtract))
                chain.link(dve.tensor_scalar(start[:], start[:], float(P), None, ALU.mult))
                chain.link(dve.tensor_tensor(up_to, up_to, in_tile, ALU.subtract))
                chain.link(dve.tensor_tensor(up_to, up_to, start[:].unsqueeze(2).to_broadcast([P, E, TILES]), ALU.add))
                chain.link(dve.tensor_tensor(place[:], ps_g[0][:, 0:TILES * E].rearrange("p (t e) -> p t e", e=E),
                                             up_to.rearrange("p e t -> p t e"), ALU.add))
                for k in range(TOP):
                    last = chain.inc(dve.tensor_tensor(chosen[:, k], chosen[:, k], place[:], ALU.mult))
                chain.wait(last)
                for k in range(TOP):
                    last = chain.inc(dve.tensor_reduce(pos[:, k, :], chosen[:, k], AX.X, ALU.add))
                chain.wait(last)
                chain.link(dve.tensor_copy(pos_i[:], pos[:]))
                chain.inc(dve.tensor_scalar(part_i[:, 0], pos_i[:], P.bit_length() - 1, None, ALU.logical_shift_right))
                chain.link(dve.tensor_scalar(part_i[:, 1], pos_i[:], P - 1, None, ALU.bitwise_and))
                chain.link(dve.tensor_copy(block_row[:], part_i[:]))
                chain.link(dve.tensor_tensor(ge, numbers[0:1, 0:BLOCKS].unsqueeze(2).to_broadcast([1, BLOCKS, E]),
                                             block_end[0:1, :].unsqueeze(1).to_broadcast([1, BLOCKS, E]), ALU.is_ge))
                chain.link(dve.tensor_reduce(expert[:], ge, AX.X, ALU.add))
                chain.link(dve.tensor_scalar(expert_i[:], expert[:], float(E - 1), None, ALU.min))
                dve.sem_inc(experts_ready, 1)
                dve.wait_ge(token_ready, 1)
                for n in range(PAIRS // 2):
                    k, t, here = 2 * n // TILES, 2 * n % TILES, slice(n % 2 * 2, n % 2 * 2 + 2)
                    if n >= 2:
                        dve.wait_ge(onehots_used, n - 1)
                    mark = chain.inc(dve.tensor_tensor(hot[:, here], numbers[:, 0:BLOCKS].unsqueeze(1).to_broadcast([P, 2, BLOCKS]),
                                                       block_row[:, 0, k, t:t + 2].unsqueeze(2).to_broadcast([P, 2, BLOCKS]), ALU.is_equal))
                    dve.tensor_tensor(is_row[:, here], numbers[:].unsqueeze(1).to_broadcast([P, 2, P]),
                                      block_row[:, 1, k, t:t + 2].unsqueeze(2).to_broadcast([P, 2, P]), ALU.is_equal)
                    chain.wait(mark)
                    dve.tensor_tensor(in_block[:, here, 0, :], hot[:, here],
                                      token[:, t:t + 2].unsqueeze(2).to_broadcast([P, 2, BLOCKS]), ALU.mult)
                    dve.tensor_tensor(in_block[:, here, 1, :], hot[:, here],
                                      gate[:, k, t:t + 2].unsqueeze(2).to_broadcast([P, 2, BLOCKS]), ALU.mult).then_inc(onehots, 1)
                dve.wait_ge(onehots_used, PAIRS // 2)
                chain.inc(dve.tensor_scalar(ids[:], ps_y[0][:, 0:BLOCKS], float(NOBODY), None, ALU.add))
                chain.link(dve.tensor_copy(gates[:], ps_y[0][:, BLOCKS:2 * BLOCKS]))
                chain.link(dve.memset(xb[:], 0.0))
                dve.sem_inc(plan_ready, 1)
                chain.link(dve.memset(hidden[:], 0.0))

                def split_w1(i, e, c):
                    dve.wait_ge(w1_rounded, HC * i + c + 1)
                    dve.tensor_tensor(w1_lo[:, c, :], w1_chunk(e, c), w1_hi[:, c, :], ALU.subtract).then_inc(w1_split, 1)

                def split_w2(i, e, c):
                    dve.wait_ge(w2_rounded, FC * i + c + 1)
                    dve.tensor_tensor(w2_lo[:, c, :], w2_chunk(e, c), w2_hi[:, c, :], ALU.subtract).then_inc(w2_split, 1)

                def split_xT(i, par):
                    dve.wait_ge(xT_rounded, done(i))
                    dve.tensor_tensor(xbT_lo[:, par], ps_xT[:].rearrange("p (c q) -> p c q", c=HC), xbT_hi[:, par], ALU.subtract) \
                       .then_inc(xT_ready, 1)

                def split_hT(i):
                    dve.wait_ge(hT_rounded, done(i))
                    dve.tensor_tensor(hiddenT_lo[:], ps_hT[:, 0:FC * P].rearrange("p (c q) -> p c q", c=FC), hiddenT_hi[:],
                                      ALU.subtract).then_inc(hT_ready, 1)

                def body(i, par, prev, nxt, nxt2):
                    if prev:
                        e_before = expert_of(dve, i - 1)
                        for c in range(FC - 1):
                            split_w2(i - 1, e_before, c)
                    if nxt:
                        e_next = expert_of(dve, i + 1)
                        split_w1(i + 1, e_next, 0)
                    if prev:
                        split_hT(i - 1)
                    if nxt:
                        split_xT(i + 1, 1 - par)
                        split_w1(i + 1, e_next, 1)
                        split_w1(i + 1, e_next, 2)
                    if nxt is not None:
                        dve.wait_ge(silu_ready, done(i))
                        dve.wait_ge(w1_used, up_done(i))
                        dve.wait_ge(hT_full, done(i - 2))
                        dve.tensor_tensor(hidden[:, par, 0:F], silu[:, par, :], ps_u[par][:, 0:F], ALU.mult).then_inc(hidden_ready, 1)
                    if prev:
                        dve.wait_ge(w2_used, down_done(i - 1))
                        if not isinstance(i, int) or i >= 3:
                            dve.wait_ge(scattered, 16 * (i - 2))
                        dve.tensor_scalar(yb[:, 1 - par, :], ps_y[1 - par][:], gates[:, bass.ds(i - 1, 1)], None, ALU.mult) \
                           .then_inc(y_ready, 1)

                dve.wait_ge(plan_ready, 1)
                first = expert_of(dve, 0)
                for c in range(HC - 1):
                    split_w1(0, first, c)
                split_xT(0, 0)
                blocks(dve, body)


def build(nc, x, ctx_in, w_qkv, w_out, decay_rows, enc, wq, bq, wk, bk, wv, bv, wm, bm, router_t, w1_t, w2_t,
          ident, head_sum, head_spread, before, numbers, out):
    x1 = nc.dram_tensor("x1", (B, T, HID), FP32, kind="Internal").ap()
    xn1 = nc.dram_tensor("xn1", (B, T, HID), FP32, kind="Internal").ap()
    xn2 = nc.dram_tensor("xn2", (B, T, HID), FP32, kind="Internal").ap()
    with nc.sbuf_tensor("logits", [P, TILES, E], FP32) as logits:
        build_stage_a(nc, x, w_qkv, w_out, decay_rows, ident, head_sum, head_spread, x1, xn1)
        build_stage_b(nc, x1, xn1, ctx_in, wq, wk, wv, wm, bq, bk, bv, bm, enc, router_t, ident, out, xn2, logits)
        build_stage_c(nc, xn2.rearrange("b t n -> (b t) n"), logits, w1_t, w2_t, ident, before, numbers,
                      out.rearrange("b t n -> (b t) n"))


def kernel(**inputs):
    import numpy as _np
    import concourse.bacc as _bacc
    from concourse import mybir as _mybir
    from concourse.bass_utils import run_bass_kernel_spmd as _run

    a = {k: _np.asarray(v) for k, v in inputs.items()}

    def head_major(w):
        return w.reshape(HD, H, -1).transpose(2, 1, 0).reshape(-1, HD * H)

    def in_halves(w):
        return w.reshape(HD, 2, H // 2, -1).transpose(3, 1, 0, 2).reshape(-1, HD * H)

    head_sum = (_np.arange(HC)[:, None] * 4 + _np.arange(P) // 32)[:, :, None] == _np.arange(H)
    head_sum = head_sum.transpose(1, 0, 2).astype(_np.float32)
    arrays = {
        "x": a["x"], "ctx": a["ctx_2048"], "w_qkv": a["L0_attn_w_qkv"], "w_out": a["L0_attn_w_out"],
        "decay": _np.repeat(a["L0_attn_decay_param"], HID // H).reshape(HC, P).T,
        "enc": a["L0_xattn_encoding"].reshape(2, HID, HD),
        "wq": in_halves(a["L0_xattn_Wq"]), "bq": in_halves(a["L0_xattn_bq"]),
        "wk": in_halves(a["L0_xattn_Wk"]), "bk": in_halves(a["L0_xattn_bk"]),
        "wv": head_major(a["L0_xattn_Wv"]), "bv": head_major(a["L0_xattn_bv"]),
        "wm": a["L0_xattn_Wm"].reshape(-1, HD, H).transpose(2, 1, 0).reshape(HD * H, -1),
        "bm": a["L0_xattn_bm"].reshape(TT, P).T,
        "router": a["L0_ffn_router_w"].T,
        "w1": a["L0_ffn_w1"].transpose(0, 2, 1), "w2": a["L0_ffn_w2"].transpose(0, 2, 1),
        "ident": _np.eye(P, dtype=_np.float32), "head_sum": head_sum, "head_spread": head_sum.transpose(2, 1, 0),
        "before": _np.stack([_np.triu(_np.ones((P, P), _np.float32), 1), _np.ones((P, P), _np.float32)], 1),
        "numbers": _np.tile(_np.arange(P, dtype=_np.float32), (P, 1)),
    }
    arrays = {k: _np.ascontiguousarray(v) for k, v in arrays.items()}
    nc = _bacc.Bacc("TRN2", target_bir_lowering=False, num_devices=1)
    args = [nc.dram_tensor(k, v.shape, _mybir.dt.from_np(v.dtype), kind="ExternalInput").ap() for k, v in arrays.items()]
    out = nc.dram_tensor("out", (B, T, HID), FP32, kind="ExternalOutput").ap()
    build(nc, *args, out)
    r = _run(nc, [arrays], core_ids=[0])
    return r.results[0]["out"]
```
